# Optimizing a Trainium2 kernel written in Bass

```python
import numpy as np
import jax
import jax.numpy as jnp

def _softmax(x, axis=-1):
    return jax.nn.softmax(x, axis=axis)

def _gelu(x):
    return jax.nn.gelu(x, approximate=True)

def _silu(x):
    return jax.nn.silu(x)

def _sigmoid(x):
    return jax.nn.sigmoid(x)

def _layernorm(x, axis=-1, eps=1e-05):
    m = jnp.mean(x, axis=axis, keepdims=True)
    v = jnp.var(x, axis=axis, keepdims=True)
    return (x - m) / jnp.sqrt(v + eps)

def _scatter_add(tgt, idx, src, axis=0):
    return tgt.at[idx].add(src)

def _segment_sum(src, seg, n):
    return jax.ops.segment_sum(src, seg, n)
kernel_name = 'mk_seq_postln_d1_jaxref_r8_41af75'

def setup_inputs(seed: int=0):
    np.random.seed(seed)
    _w = jnp.asarray

    def _L0_attn_setup():
        import jax, jax.numpy as jnp
        import numpy as np
        from jax import lax
        H = 256
        N = 8
        B, L, D_MODEL = (4, 512, 128)
        D_CONV = 4

        def _s4d_kernel(log_dt, log_A_real, A_imag, C_re, C_im, L):
            dt = jnp.exp(log_dt)
            A = -jnp.exp(log_A_real) + 1j * A_imag
            C = C_re + 1j * C_im
            dtA = dt[:, None] * A
            Ct = C * (jnp.exp(dtA) - 1.0) / A
            t = jnp.arange(L, dtype=jnp.float32)
            vand = jnp.exp(dtA[:, :, None] * t)
            return 2.0 * jnp.einsum('hn,hnl->hl', Ct, vand).real
        key = jax.random.key(seed)
        ks = jax.random.split(key, 10)
        hidden_states = jax.random.normal(ks[0], (B, L, D_MODEL), dtype=jnp.float32)
        W_in = jax.random.normal(ks[1], (2 * H, D_MODEL), dtype=jnp.float32) / np.sqrt(D_MODEL)
        conv_w = jax.random.normal(ks[2], (H, D_CONV), dtype=jnp.float32) / np.sqrt(D_CONV)
        conv_b = jax.random.normal(ks[3], (H,), dtype=jnp.float32) * 0.1
        u = jax.random.uniform(ks[4], (H,), dtype=jnp.float32)
        log_dt = jnp.log(0.001) + u * (jnp.log(0.1) - jnp.log(0.001))
        log_A_real = jnp.log(0.5 * jnp.ones((H, N), dtype=jnp.float32))
        A_imag = jnp.pi * jnp.broadcast_to(jnp.arange(N, dtype=jnp.float32), (H, N)).copy()
        C_re = jax.random.normal(ks[5], (H, N), dtype=jnp.float32)
        C_im = jax.random.normal(ks[6], (H, N), dtype=jnp.float32)
        D = jnp.ones((H,), dtype=jnp.float32)
        W_out = jax.random.normal(ks[7], (D_MODEL, H), dtype=jnp.float32) / np.sqrt(H)
        return dict(hidden_states=hidden_states, W_in=W_in, conv_w=conv_w, conv_b=conv_b, log_dt=log_dt, log_A_real=log_A_real, A_imag=A_imag, C_re=C_re, C_im=C_im, D=D, W_out=W_out)
    _L0_attn_in = _L0_attn_setup()

    def _L0_ffn_setup():
        import jax, jax.numpy as jnp
        import numpy as np
        D_MODEL = 128
        D_FF = 512
        NUM_EXPERTS = 8
        key = jax.random.key(seed)
        ks = jax.random.split(key, 8)
        scale_in = 1.0 / np.sqrt(D_MODEL)
        scale_ff = 1.0 / np.sqrt(D_FF)
        x = jax.random.normal(ks[0], (4, 256, D_MODEL), dtype=jnp.float32)
        gate_w = jax.random.uniform(ks[1], (NUM_EXPERTS, D_MODEL), jnp.float32, -scale_in, scale_in)
        gate_b = jax.random.uniform(ks[2], (NUM_EXPERTS,), jnp.float32, -scale_in, scale_in)
        expert_bias = jnp.zeros((NUM_EXPERTS,), dtype=jnp.float32)
        w1 = jax.random.uniform(ks[3], (NUM_EXPERTS, D_MODEL, D_FF), jnp.float32, -scale_in, scale_in)
        b1 = jax.random.uniform(ks[4], (NUM_EXPERTS, D_FF), jnp.float32, -scale_in, scale_in)
        w2 = jax.random.uniform(ks[5], (NUM_EXPERTS, D_FF, D_MODEL), jnp.float32, -scale_ff, scale_ff)
        b2 = jax.random.uniform(ks[6], (NUM_EXPERTS, D_MODEL), jnp.float32, -scale_ff, scale_ff)
        return {'x': x, 'gate_w': gate_w, 'gate_b': gate_b, 'expert_bias': expert_bias, 'w1': w1, 'b1': b1, 'w2': w2, 'b2': b2}
    _L0_ffn_in = _L0_ffn_setup()
    _d = {'L0_attn_hidden_states': _L0_attn_in['hidden_states'], 'L0_attn_W_in': _L0_attn_in['W_in'], 'L0_attn_conv_w': _L0_attn_in['conv_w'], 'L0_attn_conv_b': _L0_attn_in['conv_b'], 'L0_attn_log_dt': _L0_attn_in['log_dt'], 'L0_attn_log_A_real': _L0_attn_in['log_A_real'], 'L0_attn_A_imag': _L0_attn_in['A_imag'], 'L0_attn_C_re': _L0_attn_in['C_re'], 'L0_attn_C_im': _L0_attn_in['C_im'], 'L0_attn_D': _L0_attn_in['D'], 'L0_attn_W_out': _L0_attn_in['W_out'], 'L0_ffn_gate_w': _L0_ffn_in['gate_w'], 'L0_ffn_gate_b': _L0_ffn_in['gate_b'], 'L0_ffn_expert_bias': _L0_ffn_in['expert_bias'], 'L0_ffn_w1': _L0_ffn_in['w1'], 'L0_ffn_b1': _L0_ffn_in['b1'], 'L0_ffn_w2': _L0_ffn_in['w2'], 'L0_ffn_b2': _L0_ffn_in['b2']}
    _x0 = _d['L0_attn_hidden_states']
    _d['L0_attn_hidden_states'] = jax.random.normal(jax.random.fold_in(jax.random.key(seed), 1), (8, 512, 128), dtype=_x0.dtype)
    del _x0
    return _d

def reference(L0_attn_hidden_states, L0_attn_W_in, L0_attn_conv_w, L0_attn_conv_b, L0_attn_log_dt, L0_attn_log_A_real, L0_attn_A_imag, L0_attn_C_re, L0_attn_C_im, L0_attn_D, L0_attn_W_out, L0_ffn_gate_w, L0_ffn_gate_b, L0_ffn_expert_bias, L0_ffn_w1, L0_ffn_b1, L0_ffn_w2, L0_ffn_b2):

    def _L0_attn_ref(hidden_states, W_in, conv_w, conv_b, log_dt, log_A_real, A_imag, C_re, C_im, D, W_out):
        import jax, jax.numpy as jnp
        import numpy as np
        from jax import lax
        H = 256
        N = 8
        B, L, D_MODEL = (4, 512, 128)
        D_CONV = 4

        def _s4d_kernel(log_dt, log_A_real, A_imag, C_re, C_im, L):
            dt = jnp.exp(log_dt)
            A = -jnp.exp(log_A_real) + 1j * A_imag
            C = C_re + 1j * C_im
            dtA = dt[:, None] * A
            Ct = C * (jnp.exp(dtA) - 1.0) / A
            t = jnp.arange(L, dtype=jnp.float32)
            vand = jnp.exp(dtA[:, :, None] * t)
            return 2.0 * jnp.einsum('hn,hnl->hl', Ct, vand).real
        B, L, _ = hidden_states.shape
        xz = jnp.einsum('bld,ed->bel', hidden_states, W_in)
        x, z = jnp.split(xz, 2, axis=1)
        w = conv_w.shape[-1]
        xp = jnp.pad(x, ((0, 0), (0, 0), (w - 1, 0)))
        x = lax.conv_general_dilated(xp, conv_w[:, None, :], (1,), 'VALID', dimension_numbers=('NCH', 'OIH', 'NCH'), feature_group_count=x.shape[1])
        x = jax.nn.silu(x + conv_b[None, :, None])
        k = _s4d_kernel(log_dt, log_A_real, A_imag, C_re, C_im, L)
        n = 2 * L
        y = jnp.fft.irfft(jnp.fft.rfft(x, n=n) * jnp.fft.rfft(k, n=n), n=n)[..., :L]
        y = y + x * D[None, :, None]
        y = y * jax.nn.silu(z)
        return jnp.einsum('bhl,dh->bld', y, W_out)

    def _L0_ffn_ref(x, gate_w, gate_b, expert_bias, w1, b1, w2, b2):
        import jax, jax.numpy as jnp
        import numpy as np
        D_MODEL = 128
        D_FF = 512
        NUM_EXPERTS = 8
        gate_logits = jnp.einsum('bsd,ed->bse', x, gate_w) + gate_b + expert_bias
        top_idx = jnp.argmax(gate_logits, axis=-1)
        out = jnp.zeros_like(x)
        for e in range(NUM_EXPERTS):
            mask = (top_idx == e)[..., None].astype(x.dtype)
            h = jax.nn.relu(jnp.einsum('bsd,df->bsf', x, w1[e]) + b1[e])
            y = jnp.einsum('bsf,fd->bsd', h, w2[e]) + b2[e]
            out = out + mask * y
        return out
    x = L0_attn_hidden_states
    x = _layernorm(x + _L0_attn_ref(x, L0_attn_W_in, L0_attn_conv_w, L0_attn_conv_b, L0_attn_log_dt, L0_attn_log_A_real, L0_attn_A_imag, L0_attn_C_re, L0_attn_C_im, L0_attn_D, L0_attn_W_out), axis=-1)
    x = _layernorm(x + _L0_ffn_ref(x, L0_ffn_gate_w, L0_ffn_gate_b, L0_ffn_expert_bias, L0_ffn_w1, L0_ffn_b1, L0_ffn_w2, L0_ffn_b2), axis=-1)
    return x

_drawn_inputs = setup_inputs


def setup_inputs(seed=0):
    import zlib

    import numpy as np

    out = dict(_drawn_inputs(seed))
    spreads = {'L0_attn_log_A_real': (-0.6931471824645996, 0.2),
     'L0_attn_D': (1.0, 0.2),
     'L0_ffn_expert_bias': (0.0, 0.1)}
    factors = {'L0_ffn_b1': 2.802}
    for name, (base, spread) in spreads.items():
        noise = np.random.default_rng([zlib.crc32(name.encode()), seed]).standard_normal(out[name].shape)
        drawn = base * np.exp(spread * noise) if base else spread * noise
        out[name] = jnp.asarray(drawn.astype(out[name].dtype))
    for name, factor in factors.items():
        out[name] = (out[name] * factor).astype(out[name].dtype)
    return out
```

```python
import math
from contextlib import ExitStack

import numpy as np
import concourse.bass as bass
from concourse import mybir

F32 = mybir.dt.float32
I32 = mybir.dt.int32
U32 = mybir.dt.uint32
ALU = mybir.AluOpType
ACT = mybir.ActivationFunctionType
AX = mybir.AxisListType

P = 128
BATCH, SEQ, DM = 8, 512, 128
CHAN, STATES, TAPS = 256, 8, 4
EXPERTS, DFF = 8, 512
TOKENS = BATCH * SEQ
CHUNK = P
CHUNKS = SEQ // CHUNK
TILES = TOKENS // P
PAIRS = TILES // 2
GH = 8
GROUPS = CHAN // GH
LAGS = CHUNKS - 1
SCOLS = LAGS * BATCH
KLEN = CHUNK + 1
KROW = 2 * CHUNK
BLOCKS = TILES + EXPERTS - 1
ROW = DM + 4
TOKEN_COL = DM
NO_TOKEN = 1 << 17
FCH = DFF // P
EPS = 1e-5
MAGIC = float(1.5 * 2 ** 23)
TWO_PI = 6.2831850
TURN = float(1.0 / (2.0 * math.pi))

T_SLOTS = 8
A_BATCH = 2


def wait_past(engine, semaphore, count):
    if not isinstance(count, int) or count > 0:
        engine.wait_ge(semaphore, count)


def wait_apart(engine, semaphore, count):
    if not isinstance(count, int) or count > 0:
        engine.wait_ge(semaphore, count)
        engine.nop(nofuse=True)


def build(nc, hidden, hidden_t, hidden_r, w_in_t, conv_w, conv_b, log_dt, log_a, a_imag, c_re, c_im, d_skip, w_out_t,
          gate_w_t, gate_b, expert_bias, w1, b1, w2, b2, out):
    kext = nc.dram_tensor("kernel_rows", [CHAN, KROW], F32).ap()
    rows_dram = nc.dram_tensor("decay_and_turns", [2, GH * STATES * GROUPS], F32).ap()
    toeplitz = bass.AP(kext.tensor, 0, [[1, P], [KROW, CHAN], [1, CHUNK]])
    slots_dram = nc.dram_tensor("dispatched_rows", [BLOCKS * P, ROW], F32).ap()
    out_rows = out.rearrange("b l d -> (b l) d")
    hidden_rows = hidden.rearrange("b l d -> (b l) d")

    ctx = ExitStack()
    with ctx:
        def sb(name, shape, dt=F32):
            return ctx.enter_context(nc.sbuf_tensor(name, shape, dt))

        def sem(name):
            return ctx.enter_context(nc.semaphore(name))

        bank = [ctx.enter_context(nc.psum_tensor(f"bank{i}", [P, 512], F32)) for i in range(8)]

        X = sb("X", [P, CHAN, TILES])
        Z = sb("Z", [P, TILES, CHAN])
        BR = sb("BR", [P, 3 * 4096])
        CR = sb("CR", [P, GROUPS * KLEN])
        TR = sb("TR", [P, T_SLOTS * GH * CHUNK])
        RW = sb("RW", [P, 4096])
        EN = sb("EN", [P, 3840])

        Btab = BR[:, :].rearrange("p (m r n g) -> p m r n g", m=3, r=2, g=GROUPS)
        Ctab = CR[:, :].rearrange("p (g j) -> p g j", g=GROUPS)
        turnsC = BR[:, 0:GROUPS * KLEN].rearrange("p (g j) -> p g j", g=GROUPS)
        wholeC = BR[:, GROUPS * KLEN:2 * GROUPS * KLEN].rearrange("p (g j) -> p g j", g=GROUPS)
        Tring = TR[:, :].rearrange("p (s h u) -> p s h u", s=T_SLOTS, h=GH)
        Sel = TR[:, 0:4096].rearrange("p (g c) -> p g c", g=GROUPS)
        X1 = TR[:, 0:TILES * ROW].rearrange("p (j c) -> p j c", j=TILES)
        decay_row = RW[:, 0:2048]
        turns_row = RW[:, 2048:4096]
        E_half = EN[:, 0:1024].rearrange("p (n g) -> p n g", g=GROUPS)
        whole = EN[:, 1024:1536]
        U = EN[:, 1536:2560].rearrange("p (s j c) -> p s j c", s=2, j=2)

        XT = sb("XT", [P, A_BATCH, SEQ])
        XR = EN[:, 2688:2688 + A_BATCH * (SEQ + TAPS - 1)].rearrange("p (k c) -> p k c", k=A_BATCH)
        Win = sb("Win", [P, 2 * CHAN])
        Wx = sb("Wx", [P, TAPS, CHAN])
        cbias = sb("cbias", [P, CHAN])
        BC = Wx[:, :, :].rearrange("p t c -> p (t c)").rearrange("p (k m c) -> p k m c", k=2, m=4)
        V = XT[:, :, 0:GH * SCOLS].rearrange("p k (h c) -> p k h c", h=GH)
        prm = sb("prm", [P, 5, GROUPS])
        sm = sb("sm", [P, 24, GROUPS])
        smt = EN[:, 2560:2560 + 2 * GROUPS].rearrange("p (i g) -> p i g", i=2)
        tau = sb("tau", [P, LAGS])
        jrow = sb("jrow", [P, KLEN])
        phase = sb("phase", [P, 1])
        epscol = sb("epscol", [P, 1])
        mask16 = sb("mask16", [P, 2 * GH])
        mask8 = sb("mask8", [P, GH])
        Kx = TR[:, 4096:4096 + 2 * KROW].rearrange("p (j c) -> p j c", j=2)
        dskip = sb("dskip", [P, 2])
        ident = sb("ident", [P, P])
        LATE = 2048 + 384
        before = CR[:, LATE:LATE + P]
        ones = CR[:, LATE + P:LATE + 2 * P]
        WoT = CR[:, LATE + 256:LATE + 512].rearrange("p (j d) -> p j d", j=2)
        gwT = sb("gwT", [P, EXPERTS])
        gbias = sb("gbias", [P, 2, EXPERTS])
        empty_row = TR[:, 4096 + 2 * KROW:4096 + 2 * KROW + ROW]

        G = RW[:, 0:1024].rearrange("p (k c) -> p k c", k=4)
        GT = RW[:, 1024:2048].rearrange("p (k c) -> p k c", k=4)
        HR = RW[:, 2048:2560].rearrange("p (k c) -> p k c", k=4)
        R = RW[:, 2560:3072].rearrange("p (k c) -> p k c", k=4)
        X1T = RW[:, 3072:3584].rearrange("p (k c) -> p k c", k=4)
        N4 = RW[:, 3584:4096].rearrange("p (k c) -> p k c", k=4)
        st = sb("st", [P, 4, 6])
        mv = sb("mv", [P, 4, 2])
        sd = sb("sd", [P, 4])
        rs = sb("rs", [P, 4])
        LG = sb("LG", [P, 4, EXPERTS])
        top = sb("top", [P, 4, 8])
        IDX = CR[:, LATE + 512:LATE + 544].bitcast(U32).rearrange("p (j c) -> p j c", c=8)

        def late(at, shape, dt=F32):
            view = CR[:, LATE + 768 + at:LATE + 768 + at + shape]
            return view if dt == F32 else view.bitcast(dt)

        idxf = late(0, TILES)
        posf = late(32, TILES)
        pos = late(64, TILES, U32)
        brow = late(96, BLOCKS + 1)
        bexpf = late(136, BLOCKS + 1)
        bexp = late(176, BLOCKS + 1, I32)
        tok = late(216, 6, U32)
        cnt = late(256, 6 * EXPERTS).rearrange("p (i e) -> p i e", e=EXPERTS)
        erow = late(304, EXPERTS)
        OH = EN[:, 0:256].rearrange("p (e j) -> p e j", e=EXPERTS)
        run = EN[:, 256:512].rearrange("p (e j) -> p e j", e=EXPERTS)
        rt = EN[:, 512:768].rearrange("p (e j) -> p e j", e=EXPERTS)
        bcmp = EN[:, 768:768 + (BLOCKS + 1) * EXPERTS].rearrange("p (b e) -> p b e", e=EXPERTS)

        W1 = BR[:, 0:4096].rearrange("p (e f) -> p e f", e=EXPERTS)
        W2 = BR[:, 4096:8192].rearrange("p (e q) -> p e q", e=EXPERTS)
        B1 = BR[:, 8192:12288].rearrange("p (e f) -> p e f", e=EXPERTS)
        B2 = CR[:, 0:1024].rearrange("p (e d) -> p e d", e=EXPERTS)
        XS = CR[:, 1024:1024 + 3 * ROW].rearrange("p (s c) -> p s c", s=3)
        O = CR[:, 2048:2048 + 384].rearrange("p (s c) -> p s c", s=3)
        Hs = EN[:, 0:1536].rearrange("p (s c) -> p s c", s=3)
        HT = EN[:, 1536:3072].rearrange("p (s c) -> p s c", s=3)
        XsT = EN[:, 3072:3456].rearrange("p (s c) -> p s c", s=3)
        F = EN[:, 3456:3840].rearrange("p (s c) -> p s c", s=3)
        est = sb("est", [P, 3, 6])
        emv = sb("emv", [P, 3, 2])
        esd = sb("esd", [P, 3])
        ers = sb("ers", [P, 3])

        s_params = sem("params_loaded")
        s_win = sem("w_in_loaded")
        s_cw = sem("conv_loaded")
        s_late = sem("late_weights_loaded")
        s_xt = [sem(f"batch_loaded{k}") for k in range(A_BATCH)]
        s_pad = sem("padding_zeroed")
        s_wo = sem("output_weights_loaded")
        s_wx = sem("conv_weights_ready")
        s_const = sem("constants_ready")
        s_pstep = sem("pool_step")
        s_vstep = sem("vector_step")
        s_exp1 = sem("rates_ready")
        s_ang = sem("angles_ready")
        s_tanh = sem("tanh_ready")
        s_sin1 = sem("sines_ready")
        s_dec = sem("decay_rates_ready")
        s_rat = sem("ratio_ready")
        s_atan = sem("arctan_ready")
        s_hyp = sem("hypotenuse_ready")
        s_rows = sem("rows_written")
        s_rowl = sem("rows_broadcast")
        s_cexpo = sem("c_exponents_ready")
        s_ce = sem("c_decay_ready")
        s_ct = sem("c_turns_ready")
        s_cs = sem("c_sines_ready")
        s_c = sem("c_table_ready")
        s_sel0 = sem("selectors_zeroed")
        s_sel = sem("selectors_ready")
        s_kp = sem("kernel_rows_summed")
        s_kx = sem("kernel_rows_ready")
        s_kd = sem("kernel_rows_stored")
        s_a = sem("projection_ready")
        s_xb = sem("x_biased")
        s_x = sem("x_ready")
        s_z = sem("z_ready")
        s_bt = sem("state_turns_ready")
        s_bw = sem("state_turns_step")
        s_bs = sem("state_sines_ready")
        s_be = sem("state_decay_ready")
        s_b = sem("state_table_ready")
        s_t = [sem(f"toeplitz_loaded{k}") for k in range(T_SLOTS)]
        s_bc = sem("group_tables_ready")
        s_s = sem("states_summed")
        s_v = sem("states_ready")
        s_y = sem("group_done")
        s_yc = sem("mixer_output_copied")
        s_g = sem("gated_ready")
        s_tp = sem("gated_transposed")
        s_gt = sem("gated_t_copied")
        s_o = sem("mixer_projected")
        s_hr = [sem(f"residual_loaded{k}") for k in range(4)]
        s_r = sem("residual_added")
        s_st = sem("stats_ready")
        s_mv = sem("moments_ready")
        s_sd = sem("deviation_ready")
        s_rs = sem("scale_ready")
        s_x1 = sem("x1_ready")
        s_xp = sem("x1_transposed")
        s_x1t = sem("x1_t_copied")
        s_lp = sem("logits_summed")
        s_lg = sem("logits_ready")
        s_top = sem("maxima_ready")
        s_ix = sem("indices_ready")
        s_idx = sem("choices_ready")
        s_empty = sem("slots_emptied")
        s_oh = sem("one_hot_ready")
        s_cp = sem("counts_ready")
        s_pos = sem("positions_ready")
        s_be2 = sem("block_experts_ready")
        s_sc = sem("rows_dispatched")
        s_rconst = sem("routing_constants_ready")
        s_tk = sem("token_numbers_passed")
        s_tok = sem("token_numbers_ready")
        s_x1c = sem("x1_kept")
        s_xb2 = sem("residual_biased")
        s_rstep = sem("routing_step")
        s_ew = sem("expert_weights_loaded")
        s_xs = [sem(f"slots_loaded{k}") for k in range(3)]
        s_ep = sem("slots_transposed")
        s_ext = sem("slots_t_copied")
        s_up = sem("hidden_summed")
        s_h = sem("hidden_biased")
        s_hp = sem("hidden_transposed")
        s_ht = sem("hidden_ready")
        s_dn = sem("expert_out_summed")
        s_f1 = sem("expert_bias_added")
        s_f2 = sem("expert_residual_added")
        s_f3 = sem("expert_stats_ready")
        s_f4 = sem("expert_moments_ready")
        s_f5 = sem("expert_deviation_ready")
        s_f6 = sem("expert_scale_ready")
        s_f7 = sem("normalized_ready")
        s_out = [sem(f"out_stored{k}") for k in range(3)]

        LOG_DT, LOG_A, A_IM, C_RE, C_IM = range(5)
        (DT, EA, AR, AI, TURNS, TH, EM1, ER, CM1, WR, WI, T1, T2, PP, QQ, AXX, AYY, MX, RAT, PHI, AMP, DEN, T3,
         T4) = range(24)

        def block_of(r, k, behind):
            n = r * 3 + (k - behind)
            if isinstance(n, int) and not 0 <= n < BLOCKS:
                return None
            return n, (k - behind) % 3, r + (k - behind) // 3

        block = ctx.enter_context(nc.Block())

        @block.sync
        def _(sp):
            for n, src in ((LOG_A, log_a), (A_IM, a_imag), (C_RE, c_re), (C_IM, c_im)):
                for half in range(2):
                    sp.dma_start(prm[half * 64:half * 64 + 64, n, :], src).then_inc(s_params, 16)
            sp.dma_start(Wx[:, :, :].rearrange("p t c -> p (t c)"), conv_w.rearrange("t c -> (t c)").unsqueeze(0).to_broadcast([P, TAPS * CHAN]))\
              .then_inc(s_cw, 16)
            sp.dma_start(cbias[:, :], conv_b.to_broadcast([P, CHAN])).then_inc(s_cw, 16)
            sp.dma_start(dskip[:, :], d_skip).then_inc(s_late, 16)
            sp.dma_start(gwT[:, :], gate_w_t).then_inc(s_late, 16)
            sp.dma_start(gbias[:, 0, :], gate_b.to_broadcast([P, EXPERTS])).then_inc(s_late, 16)
            sp.dma_start(gbias[:, 1, :], expert_bias.to_broadcast([P, EXPERTS])).then_inc(s_late, 16)
            sp.wait_ge(s_dec, 2)
            sp.dma_start(rows_dram[0, :].rearrange("(n g) -> n g", g=GROUPS), sm[0:64, AR, :]).then_inc(s_rows, 16)
            sp.dma_start(rows_dram[1, :].rearrange("(n g) -> n g", g=GROUPS), sm[0:64, TURNS, :]).then_inc(s_rows, 16)
            sp.wait_ge(s_rows, 32)
            sp.dma_start(decay_row, rows_dram[0:1, :].to_broadcast([P, 2048])).then_inc(s_rowl, 16)
            sp.dma_start(turns_row, rows_dram[1:2, :].to_broadcast([P, 2048])).then_inc(s_rowl, 16)
            sp.wait_ge(s_const, 1)
            for n in range(BLOCKS):
                sp.dma_start(slots_dram[n * P:(n + 1) * P, :], empty_row[:, :]).then_inc(s_empty, 16)
            sp.wait_ge(s_kx, 3)
            sp.dma_start(kext.rearrange("(j p) c -> p j c", p=P), Kx[:, :, :]).then_inc(s_kd, 16)
            sp.wait_ge(s_kd, 16)
            sp.wait_ge(s_empty, 16 * BLOCKS)

            def load_toeplitz(r, k):
                group = r * T_SLOTS + k
                if not isinstance(r, int):
                    sp.wait_ge(s_y, group - (T_SLOTS - 1))
                sp.dma_start(Tring[:, k, :, :], toeplitz[:, bass.ds(group * GH, GH), :]).then_inc(s_t[k], 16)

            for k in range(T_SLOTS):
                load_toeplitz(0, k)
            with sp.Fori(1, GROUPS // T_SLOTS) as r:
                for k in range(T_SLOTS):
                    load_toeplitz(r, k)

            def load_residual(r, k):
                if not isinstance(r, int):
                    sp.wait_ge(s_r, r)
                row = (r * CHUNKS + k) * P
                sp.dma_start(HR[:, k, :], hidden_rows[bass.ds(row, P), :]).then_inc(s_hr[k], 16)

            sp.wait_ge(s_b, 2 * LAGS)
            for k in range(4):
                load_residual(0, k)
            sp.wait_ge(s_y, GROUPS)
            sp.dma_start(WoT, w_out_t.rearrange("(j p) d -> p j d", p=P)).then_inc(s_wo, 16)
            sp.dma_start(W1, w1.rearrange("e d f -> d e f")).then_inc(s_ew, 16)
            sp.dma_start(W2.rearrange("p e (c d) -> p e c d", c=FCH),
                         w2.rearrange("e (c p) d -> p e c d", p=P)).then_inc(s_ew, 16)
            sp.dma_start(B1, b1.rearrange("e f -> (e f)").unsqueeze(0).to_broadcast([P, EXPERTS * DFF]))\
              .then_inc(s_ew, 16)
            sp.dma_start(B2, b2.rearrange("e d -> (e d)").unsqueeze(0).to_broadcast([P, EXPERTS * DM]))\
              .then_inc(s_ew, 16)
            with sp.Fori(1, TILES // 4) as r:
                for k in range(4):
                    load_residual(r, k)

            def load_slots(r, k):
                n = r * 3 + k
                wait_past(sp, s_ep, n - 2)
                wait_past(sp, s_xb2, n - 2)
                sp.dma_start(XS[:, k, :], slots_dram[bass.ds(n * P, P), :]).then_inc(s_xs[k], 16)

            sp.wait_ge(s_sc, 16 * TILES)
            for k in range(3):
                load_slots(0, k)
            with sp.Fori(1, BLOCKS // 3) as r:
                for k in range(3):
                    load_slots(r, k)
            for k in range(3):
                sp.wait_ge(s_out[k], 16 * (BLOCKS // 3))

        @block.gpsimd
        def _(pool):
            nc.gpsimd.memset(empty_row[:, :], 0.0).then_inc(s_pstep, 1)
            pool.wait_ge(s_pstep, 1)
            nc.gpsimd.memset(empty_row[:, TOKEN_COL:TOKEN_COL + 1].bitcast(I32), NO_TOKEN).then_inc(s_const, 1)
            nc.gpsimd.memset(XR[:, :, SEQ:], 0.0).then_inc(s_pad, 1)
            nc.gpsimd.iota(jrow[:, :], [[1, KLEN]], base=0, channel_multiplier=0, allow_small_or_imprecise_dtypes=True)
            nc.gpsimd.iota(tau[:, :], [[CHUNK, LAGS]], base=0, channel_multiplier=1, allow_small_or_imprecise_dtypes=True)
            nc.gpsimd.memset(mask16[:, :], 1.0).then_inc(s_pstep, 1)
            pool.wait_ge(s_pstep, 2)
            nc.gpsimd.affine_select(out=mask16[:, :], in_=mask16[:, :], compare_op=ALU.is_ge, fill=0.0, base=0,
                                    pattern=[[-GH, 2 * GH]], channel_multiplier=1).then_inc(s_pstep, 1)
            pool.wait_ge(s_pstep, 3)
            nc.gpsimd.affine_select(out=mask16[:, :], in_=mask16[:, :], compare_op=ALU.is_ge, fill=0.0, base=GH - 1,
                                    pattern=[[GH, 2 * GH]], channel_multiplier=-1).then_inc(s_pstep, 1)
            pool.wait_ge(s_pstep, 4)
            nc.gpsimd.tensor_tensor(mask8[:, :], mask16[:, 0:GH], mask16[:, GH:2 * GH], ALU.add).then_inc(s_const, 1)
            nc.gpsimd.memset(TR[:, 0:4096], 0.0).then_inc(s_sel0, 1)
            pool.wait_ge(s_dec, 2)
            nc.gpsimd.tensor_tensor(Ctab, sm[:, AR, :].unsqueeze(2).to_broadcast([P, GROUPS, KLEN]),
                                    jrow[:, :].unsqueeze(1).to_broadcast([P, GROUPS, KLEN]), ALU.mult)\
              .then_inc(s_cexpo, 1)
            nc.gpsimd.memset(Kx[:, :, :], 0.0).then_inc(s_const, 1)
            nc.gpsimd.memset(ident[:, :], 1.0)
            nc.gpsimd.memset(epscol[:, :], EPS).then_inc(s_pstep, 1)
            pool.wait_ge(s_pstep, 5)
            nc.gpsimd.affine_select(out=ident[:, :], in_=ident[:, :], compare_op=ALU.is_equal, fill=0.0, base=0,
                                    pattern=[[-1, P]], channel_multiplier=1).then_inc(s_const, 1)

            with pool.Fori(1, LAGS + 1) as i:
                pool.wait_ge(s_bs, i)
                for half in range(2):
                    pool.wait_ge(s_be, i * 2 + (half - 1))
                    for q in range(2):
                        part = Btab[:, bass.ds(i - 1, 1), q, half * 32:half * 32 + 32, :].rearrange("p m n g -> p (m n) g")
                        last = nc.gpsimd.tensor_tensor(part, part, E_half, ALU.mult)
                    last.then_inc(s_b, 1)

            def group_tables(r, k):
                g = r * 2 + k
                wait_apart(pool, s_y, g - 1)
                nc.gpsimd.tensor_copy(BC[:, k, 0:LAGS, :], BR[:, :].rearrange("p (m c g) -> p m c g", m=LAGS, g=GROUPS)
                                      [:, :, :, bass.ds(g, 1)].rearrange("p m c g -> p m (c g)"))
                nc.gpsimd.tensor_copy(BC[:, k, LAGS, :], Ctab[:, bass.ds(g, 1), 1:KLEN].rearrange("p g j -> p (g j)"))\
                  .then_inc(s_bc, 1)

            pool.wait_ge(s_b, 2 * LAGS)
            pool.wait_ge(s_c, 1)
            pool.wait_ge(s_a, PAIRS)
            for k in range(2):
                group_tables(0, k)
            with pool.Fori(1, GROUPS // 2) as r:
                for k in range(2):
                    group_tables(r, k)

            def gate(r):
                wait_past(pool, s_tp, r * 4)
                for k in range(4):
                    nc.gpsimd.tensor_tensor(G[:, k, :], X[:, :, bass.ds(r + k * BATCH, 1)].rearrange("p c t -> p (c t)"),
                                            Z[:, bass.ds(r + k * BATCH, 1), :].rearrange("p t c -> p (t c)"), ALU.mult)\
                      .then_inc(s_g, 1)

            def keep_x1(r):
                wait_apart(pool, s_x1, (r + 1) * 4)
                nc.gpsimd.tensor_copy(X1[:, bass.ds(r * 4, 4), 0:DM], N4).then_inc(s_x1c, 1)

            pool.wait_ge(s_yc, GROUPS)
            nc.gpsimd.iota(X1[:, :, TOKEN_COL:TOKEN_COL + 1].bitcast(I32), [[P, TILES], [0, 1]], base=0,
                           channel_multiplier=1)
            nc.gpsimd.memset(X1[:, :, TOKEN_COL + 1:ROW], 0.0).then_inc(s_tok, 1)
            gate(0)
            nc.gpsimd.memset(ones, 1.0)
            nc.gpsimd.iota(erow, [[1, EXPERTS]], base=0, channel_multiplier=0, allow_small_or_imprecise_dtypes=True)
            nc.gpsimd.iota(brow, [[1, BLOCKS + 1]], base=0, channel_multiplier=0, allow_small_or_imprecise_dtypes=True)
            nc.gpsimd.memset(before, 1.0).then_inc(s_rconst, 1)
            pool.wait_ge(s_rconst, 1)
            nc.gpsimd.affine_select(out=before, in_=before, compare_op=ALU.is_gt, fill=0.0, base=0, pattern=[[1, P]],
                                    channel_multiplier=-1).then_inc(s_rconst, 1)
            with pool.Fori(1, TILES // 4) as r:
                gate(r)
                keep_x1(r - 1)
            keep_x1(TILES // 4 - 1)

            pool.wait_ge(s_tok, 1)
            pool.wait_ge(s_x1c, TILES // 4)
            pool.wait_ge(s_pos, 1)
            pool.wait_ge(s_empty, 16 * BLOCKS)
            for j in range(TILES):
                pool.indirect_dma_start(slots_dram, bass.IndirectOffsetOnAxis(pos[:, j:j + 1], 0), X1[:, j, :], None)\
                    .then_inc(s_sc, 16)

            pool.wait_ge(s_ew, 64)
            pool.wait_ge(s_be2, 1)

            def residual_and_bias(r, k):
                at = block_of(r, k, 0)
                if at:
                    n, slot, turn = at
                    e = pool.value_load(bexp[0:1, bass.ds(n, 1)], min_val=0, max_val=EXPERTS - 1)
                    pool.wait_ge(s_xs[slot], (turn + 1) * 16)
                    wait_past(pool, s_f1, n - 2)
                    nc.gpsimd.tensor_tensor(O[:, slot, :], XS[:, slot, 0:DM],
                                            B2[:, bass.ds(e, 1), :].rearrange("p e d -> p (e d)"), ALU.add)
                    wait_apart(pool, s_tk, n - 2)
                    nc.gpsimd.tensor_copy(tok[:, slot:slot + 1], XS[:, slot, TOKEN_COL:TOKEN_COL + 1].bitcast(U32))\
                      .then_inc(s_xb2, 1)

            def pass_tokens(r, k):
                at = block_of(r, k, 3)
                if at:
                    n, slot, turn = at
                    if not isinstance(turn, int) or turn > 0:
                        pool.wait_ge(s_out[slot], turn * 16)
                    wait_apart(pool, s_xb2, n + 1)
                    nc.gpsimd.tensor_copy(tok[:, 3 + slot:4 + slot], tok[:, slot:slot + 1]).then_inc(s_tk, 1)

            def store(r, k):
                at = block_of(r, k, 4)
                if at:
                    n, slot, turn = at
                    wait_apart(pool, s_f7, n + 1)
                    wait_apart(pool, s_tk, n + 1)
                    pool.indirect_dma_start(out_rows, bass.IndirectOffsetOnAxis(tok[:, 3 + slot:4 + slot], 0), F[:, slot, :],
                                            None, bounds_check=TOKENS - 1, oob_is_err=False).then_inc(s_out[slot], 16)

            def step(r, k):
                pass_tokens(r, k)
                residual_and_bias(r, k)
                store(r, k)

            for r in range(2):
                for k in range(3):
                    step(r, k)
            with pool.Fori(2, BLOCKS // 3) as r:
                for k in range(3):
                    step(r, k)
            for r in range(BLOCKS // 3, BLOCKS // 3 + 2):
                for k in range(3):
                    step(r, k)

        @block.scalar
        def _(act):
            for half in range(2):
                for h in range(GH):
                    at = half * 64 + h * STATES
                    act.dma_start(prm[at:at + STATES, LOG_DT, :], log_dt[h:h + 1, :].to_broadcast([STATES, GROUPS]))\
                       .then_inc(s_params, 16)
            act.dma_start(Win[:, :], w_in_t).then_inc(s_win, 16)
            for k in range(A_BATCH):
                act.dma_start(XR[:, k, 0:SEQ], hidden_r[:, k, :]).then_inc(s_xt[k], 16)
                act.dma_start(XT[:, k, :], hidden_t[:, k, :]).then_inc(s_xt[k], 16)

            act.wait_ge(s_params, 24 * 16)
            nc.scalar.activation(sm[:, DT, :], prm[:, LOG_DT, :], ACT.Exp)
            nc.scalar.activation(sm[:, EA, :], prm[:, LOG_A, :], ACT.Exp).then_inc(s_exp1, 1)
            act.wait_ge(s_dec, 1)
            nc.scalar.activation(sm[:, TH, :], sm[:, AR, :], ACT.Tanh, scale=0.5).then_inc(s_tanh, 1)
            act.wait_ge(s_cexpo, 1)
            nc.scalar.activation(CR[:, :], CR[:, :], ACT.Exp).then_inc(s_ce, 1)
            act.wait_ge(s_ang, 1)
            nc.scalar.activation(smt[:, :, :], smt[:, :, :], ACT.Sin, scale=TWO_PI).then_inc(s_sin1, 1)
            act.wait_ge(s_rat, 1)
            nc.scalar.activation(sm[:, PHI, :], sm[:, RAT, :], ACT.Arctan).then_inc(s_atan, 1)
            nc.scalar.activation(sm[:, T4, :], sm[:, T3, :], ACT.Sqrt).then_inc(s_hyp, 1)

            x_pairs = X[:, :, :].rearrange("p c (h j b) -> p c h j b", h=2, b=BATCH)
            z_pairs = Z[:, :, :].rearrange("p (h j b) c -> p h j b c", h=2, b=BATCH)

            def silus(i, ks):
                for k in ks:
                    n = i * 4 + k
                    b = bass.ds(i * 2 + k // 2, 1)
                    act.wait_ge(s_a, n + 1)
                    nc.scalar.activation(z_pairs[:, k % 2, :, b, :].rearrange("p j b c -> p j (b c)"),
                                         bank[2 + k % 2][:, :].rearrange("p (j c) -> p j c", j=2), ACT.Silu)\
                      .then_inc(s_z, 1)
                    act.wait_ge(s_xb, n + 1)
                    nc.scalar.activation(x_pairs[:, :, k % 2, :, b].rearrange("p c j b -> p j (c b)"), U[:, k % 2, :, :],
                                         ACT.Silu).then_inc(s_x, 1)

            def next_batch(i, k):
                act.wait_ge(s_a, i * 4 + (k * 2 + 2))
                for dst, src in ((XR, hidden_r), (XT, hidden_t)):
                    act.dma_start(dst[:, k, 0:SEQ], src[:, bass.ds((i + 1) * A_BATCH + k, 1), :]
                                  .rearrange("d b l -> d (b l)")).then_inc(s_xt[k], 16)

            def state_table(i):
                nc_rows = Btab[:, bass.ds(i - 1, 1), :, :, :].rearrange("p m r n g -> p (m r n g)")
                act.wait_ge(s_bt, i * 8)
                nc.scalar.activation(nc_rows, nc_rows, ACT.Sin, scale=TWO_PI).then_inc(s_bs, 1)

            def state_decay(i, half):
                wait_past(act, s_b, i * 2 + (half - 2))
                nc.scalar.activation(EN[:, 0:1024], decay_row[:, half * 1024:half * 1024 + 1024], ACT.Exp,
                                     scale=tau[:, bass.ds(i - 1, 1)]).then_inc(s_be, 1)

            silus(0, range(0, 2))
            next_batch(0, 0)
            act.wait_ge(s_ct, 1)
            nc.scalar.activation(BR[:, 0:GROUPS * KLEN], BR[:, 0:GROUPS * KLEN], ACT.Sin, scale=TWO_PI).then_inc(s_cs, 1)
            silus(0, range(2, 4))
            next_batch(0, 1)

            def projection_and_table(i, last=False):
                silus(i, range(0, 2))
                if not last:
                    next_batch(i, 0)
                state_table(i)
                state_decay(i, 0)
                silus(i, range(2, 4))
                if not last:
                    next_batch(i, 1)
                state_decay(i, 1)

            projection_and_table(1)
            with act.Fori(2, 3) as i:
                projection_and_table(i)
            projection_and_table(3, last=True)

            with act.Fori(0, GROUPS // 2) as r:
                for k in range(2):
                    g = r * 2 + k
                    act.wait_ge(s_y, g + 1)
                    nc.scalar.activation(X[:, bass.ds(g * GH, GH), :].rearrange("p h t -> p (h t)"), bank[4 + k][:, 0:256],
                                         ACT.Copy).then_inc(s_yc, 1)

            def copy_gated(r):
                for k in range(2):
                    act.wait_ge(s_tp, r * 4 + (k * 2 + 2))
                    wait_past(act, s_o, r * 4 + (k * 2 - 2))
                    nc.scalar.activation(GT[:, k * 2:k * 2 + 2, :].rearrange("p k c -> p (k c)"), bank[k][:, :], ACT.Copy)\
                      .then_inc(s_gt, 1)

            def deviation(r):
                act.wait_ge(s_mv, r + 1)
                nc.scalar.activation(sd[:, :], mv[:, :, 1], ACT.Sqrt, bias=epscol[:, :]).then_inc(s_sd, 1)

            def copy_x1(r):
                act.wait_ge(s_xp, r * 4 + 4)
                nc.scalar.activation(X1T.rearrange("p k c -> p (k c)"), bank[3][:, :], ACT.Copy).then_inc(s_x1t, 1)

            copy_gated(0)
            deviation(0)
            with act.Fori(1, TILES // 4) as r:
                copy_gated(r)
                copy_x1(r - 1)
                deviation(r)
            copy_x1(TILES // 4 - 1)

            def copy_slots(r, k):
                at = block_of(r, k, 0)
                if at:
                    n, slot, turn = at
                    act.wait_ge(s_ep, n + 1)
                    wait_past(act, s_up, n - 2)
                    nc.scalar.activation(XsT[:, slot, :], bank[6][:, 0:P], ACT.Copy).then_inc(s_ext, 1)

            def expert_deviation(r, k):
                at = block_of(r, k, 4)
                if at:
                    n, slot, turn = at
                    act.wait_ge(s_f4, n + 1)
                    nc.scalar.activation(esd[:, slot:slot + 1], emv[:, slot, 1:2], ACT.Sqrt, bias=epscol[:, :])\
                      .then_inc(s_f5, 1)

            def relu(r, k):
                at = block_of(r, k, 2)
                if at:
                    n, slot, turn = at
                    act.wait_ge(s_hp, n + 1)
                    wait_past(act, s_dn, n - 2)
                    nc.scalar.activation(HT[:, slot, :], bank[3 + slot][:, :], ACT.Relu).then_inc(s_ht, 1)

            def step(r, k):
                copy_slots(r, k)
                expert_deviation(r, k)
                relu(r, k)

            for r in range(2):
                for k in range(3):
                    step(r, k)
            with act.Fori(2, BLOCKS // 3) as r:
                for k in range(3):
                    step(r, k)
            for r in range(BLOCKS // 3, BLOCKS // 3 + 2):
                for k in range(3):
                    step(r, k)

        @block.vector
        def _(dve):
            steps = [0]

            def done(instruction):
                steps[0] += 1
                instruction.then_inc(s_vstep, 1)
                dve.wait_ge(s_vstep, steps[0])

            tt = nc.vector.tensor_tensor
            ts = nc.vector.tensor_scalar
            stt = nc.vector.scalar_tensor_tensor
            v = lambda i: sm[:, i, :]

            done(nc.vector.memset(phase[0:64, :], 0.25))
            done(nc.vector.memset(phase[64:128, :], 0.5))
            dve.wait_ge(s_win, 16)
            dve.wait_ge(s_cw, 32)
            tt(Wx[:, :, :], Win[:, 0:CHAN].unsqueeze(1).to_broadcast([P, TAPS, CHAN]), Wx[:, :, :], ALU.mult)\
              .then_inc(s_wx, 1)

            dve.wait_ge(s_exp1, 1)
            dve.wait_ge(s_params, 24 * 16)
            done(stt(v(AR), v(DT), -1.0, v(EA), ALU.mult, ALU.mult))
            done(stt(v(AI), v(DT), TURN, prm[:, A_IM, :], ALU.mult, ALU.mult))
            nc.vector.tensor_copy(v(TURNS), v(AI)).then_inc(s_dec, 2)
            done(ts(smt[:, 1, :], v(AI), 0.5, None, ALU.mult))
            done(nc.vector.tensor_copy(smt[:, 0, :], v(AI)))
            done(ts(sm[:, T1:T1 + 2, :], smt[:, :, :], MAGIC, MAGIC, ALU.add, ALU.subtract))
            tt(smt[:, :, :], smt[:, :, :], sm[:, T1:T1 + 2, :], ALU.subtract).then_inc(s_ang, 1)
            dve.wait_ge(s_ang, 1)
            dve.wait_ge(s_tanh, 1)
            done(ts(v(T1), v(TH), -1.0, 1.0, ALU.mult, ALU.add))
            done(nc.vector.reciprocal(v(T2), v(T1)))
            done(stt(v(EM1), v(TH), 2.0, v(T2), ALU.mult, ALU.mult))
            done(ts(v(ER), v(EM1), 1.0, None, ALU.add))
            dve.wait_ge(s_sin1, 1)
            done(stt(v(CM1), smt[:, 1, :], -2.0, smt[:, 1, :], ALU.mult, ALU.mult))
            done(stt(v(T1), v(CM1), 1.0, v(EM1), ALU.add, ALU.mult))
            done(tt(v(WR), v(T1), v(CM1), ALU.add))
            done(tt(v(WI), v(ER), smt[:, 0, :], ALU.mult))
            done(tt(v(T1), prm[:, C_RE, :], v(WR), ALU.mult))
            done(tt(v(T2), prm[:, C_IM, :], v(WI), ALU.mult))
            done(tt(v(T1), v(T1), v(T2), ALU.subtract))
            done(tt(v(T2), prm[:, C_RE, :], v(WI), ALU.mult))
            done(tt(v(T3), prm[:, C_IM, :], v(WR), ALU.mult))
            done(tt(v(T2), v(T2), v(T3), ALU.add))
            done(tt(v(T3), v(T2), prm[:, A_IM, :], ALU.mult))
            done(tt(v(PP), v(T1), v(EA), ALU.mult))
            done(tt(v(PP), v(T3), v(PP), ALU.subtract))
            done(tt(v(T3), v(T2), v(EA), ALU.mult))
            done(tt(v(QQ), v(T1), prm[:, A_IM, :], ALU.mult))
            done(stt(v(QQ), v(T3), -1.0, v(QQ), ALU.mult, ALU.subtract))
            done(stt(v(AXX), v(PP), -1.0, v(PP), ALU.mult, ALU.max))
            done(stt(v(AYY), v(QQ), -1.0, v(QQ), ALU.mult, ALU.max))
            done(tt(v(MX), v(AXX), v(AYY), ALU.max))
            done(tt(v(T1), v(AXX), v(AYY), ALU.min))
            done(ts(v(T2), v(MX), 1e-35, None, ALU.max))
            done(nc.vector.reciprocal(v(T3), v(T2)))
            done(tt(v(RAT), v(T1), v(T3), ALU.mult))
            done(tt(v(T1), v(RAT), v(RAT), ALU.mult))
            ts(v(T3), v(T1), 1.0, None, ALU.add).then_inc(s_rat, 1)
            dve.wait_ge(s_rat, 1)
            done(tt(v(T1), v(EA), v(EA), ALU.mult))
            done(tt(v(T2), prm[:, A_IM, :], prm[:, A_IM, :], ALU.mult))
            done(tt(v(T1), v(T1), v(T2), ALU.add))
            done(nc.vector.reciprocal(v(DEN), v(T1)))
            done(stt(v(DEN), v(DEN), 2.0, v(MX), ALU.mult, ALU.mult))
            dve.wait_ge(s_atan, 1)
            done(ts(v(PHI), v(PHI), TURN, None, ALU.mult))

            def reflect(condition, about):
                done(ts(v(T2), v(PHI), -2.0, about, ALU.mult, ALU.add))
                done(tt(v(T2), v(T2), v(T1), ALU.mult))
                done(tt(v(PHI), v(PHI), v(T2), ALU.add))

            done(tt(v(T1), v(AYY), v(AXX), ALU.is_gt))
            reflect(T1, 0.25)
            done(ts(v(T1), v(PP), 0.0, None, ALU.is_lt))
            reflect(T1, 0.5)
            done(ts(v(T1), v(QQ), 0.0, None, ALU.is_lt))
            reflect(T1, 0.0)
            dve.wait_ge(s_const, 2)
            done(ts(v(PHI), v(PHI), phase[:, :], None, ALU.add))
            dve.wait_ge(s_hyp, 1)
            done(tt(v(AMP), v(T4), v(DEN), ALU.mult))
            dve.wait_ge(s_sel0, 1)
            for j in range(2):
                at = bass.AP(TR[:, :].tensor, j * 16 * P, [[T_SLOTS * GH * CHUNK, P], [P + GH, 16], [1, GH]])
                last = tt(at, v(AMP)[:, j * 16:j * 16 + 16].unsqueeze(2).to_broadcast([P, 16, GH]),
                          mask16[:, 0:GH].unsqueeze(1).to_broadcast([P, 16, GH]), ALU.mult)
            last.then_inc(s_sel, 1)

            def bias(i, k):
                n = i * 4 + k
                dve.wait_ge(s_a, n + 1)
                wait_past(dve, s_x, n - 1)
                tt(U[:, k % 2, :, :], bank[k % 2][:, :].rearrange("p (j c) -> p j c", j=2),
                   cbias[:, :].unsqueeze(1).to_broadcast([P, 2, CHAN]), ALU.add).then_inc(s_xb, 1)

            shape = [P, GROUPS, KLEN]
            bias(0, 0)
            done(tt(turnsC, v(TURNS).unsqueeze(2).to_broadcast(shape), jrow[:, :].unsqueeze(1).to_broadcast(shape), ALU.mult))
            bias(0, 1)
            done(tt(turnsC, turnsC, v(PHI).unsqueeze(2).to_broadcast(shape), ALU.add))
            bias(0, 2)
            done(ts(wholeC, turnsC, MAGIC, MAGIC, ALU.add, ALU.subtract))
            bias(0, 3)
            tt(turnsC, turnsC, wholeC, ALU.subtract).then_inc(s_ct, 1)
            dve.wait_ge(s_ce, 1)
            dve.wait_ge(s_cs, 1)
            tt(Ctab, Ctab, turnsC, ALU.mult).then_inc(s_c, 1)

            dve.wait_ge(s_const, 3)
            dve.wait_ge(s_late, 64)
            dve.wait_ge(s_kp, 1)
            for j in range(2):
                nc.vector.tensor_copy(Kx[:, j, CHUNK - 1:KROW - 1], bank[4 + j][:, 0:CHUNK]).then_inc(s_kx, 1)
            dve.wait_ge(s_kx, 2)
            tt(Kx[:, :, CHUNK - 1], Kx[:, :, CHUNK - 1], dskip[:, :], ALU.add).then_inc(s_kx, 1)

            dve.wait_ge(s_rowl, 32)

            def state_turns(i, q):
                at = slice(q * 8, q * 8 + 8)
                lag = tau[:, bass.ds(i - 1, 1)]
                row = turns_row[:, q * 256:q * 256 + 256]
                part = Btab[:, bass.ds(i - 1, 1), :, at, :].rearrange("p m r n g -> p (m r) (n g)")
                both = whole.rearrange("p (r c) -> p r c", r=2)
                count = (i - 1) * 16 + q * 2
                ts(part[:, 0, :], row, lag, 0.25, ALU.mult, ALU.add)
                ts(part[:, 1, :], row, lag, None, ALU.mult).then_inc(s_bw, 1)
                dve.wait_ge(s_bw, count + 1)
                ts(both, part, MAGIC, MAGIC, ALU.add, ALU.subtract).then_inc(s_bw, 1)
                dve.wait_ge(s_bw, count + 2)
                tt(part, part, both, ALU.subtract).then_inc(s_bt, 1)
                dve.wait_ge(s_bt, (i - 1) * 8 + (q + 1))

            with dve.Fori(1, 4) as i:
                for k in range(4):
                    bias(i, k)
                    state_turns(i, k * 2)
                    state_turns(i, k * 2 + 1)

            def states(r, k):
                g = r * 2 + k
                dve.wait_ge(s_s, g + 1)
                wait_past(dve, s_y, g - 1)
                stt(V[:, k, :, :], bank[6 + k][:, 0:GH * SCOLS].rearrange("p (h c) -> p h c", h=GH),
                    sm[:, AMP, bass.ds(g, 1)], mask8[:, :].unsqueeze(2).to_broadcast([P, GH, SCOLS]), ALU.mult, ALU.mult)\
                    .then_inc(s_v, 1)

            dve.wait_ge(s_a, PAIRS)
            for k in range(2):
                states(0, k)
            with dve.Fori(1, GROUPS // 2) as r:
                for k in range(2):
                    states(r, k)

            def norm(r):
                dve.wait_ge(s_o, r * 4 + 4)
                for k in range(4):
                    dve.wait_ge(s_hr[k], (r + 1) * 16)
                wait_past(dve, s_x1, r * 4)
                tt(R.rearrange("p k c -> p (k c)"), bank[2][:, :], HR.rearrange("p k c -> p (k c)"), ALU.add).then_inc(s_r, 1)
                dve.wait_ge(s_r, r + 1)
                for k in range(4):
                    last = nc.vector.bn_stats(st[:, k, :], R[:, k, :])
                last.then_inc(s_st, 1)
                wait_apart(dve, s_st, r + 1)
                for k in range(4):
                    last = nc.vector.bn_aggr(mv[:, k, :], st[:, k, :])
                last.then_inc(s_mv, 1)
                dve.wait_ge(s_sd, r + 1)
                nc.vector.reciprocal(rs[:, :], sd[:, :]).then_inc(s_rs, 1)
                dve.wait_ge(s_rs, r + 1)
                wait_past(dve, s_xp, r * 4)
                wait_past(dve, s_x1c, r)
                for k in range(4):
                    ts(N4[:, k, :], R[:, k, :], mv[:, k, 0:1], rs[:, k:k + 1], ALU.subtract, ALU.mult).then_inc(s_x1, 1)

            def choose(r):
                dve.wait_ge(s_lp, r + 1)
                wait_past(dve, s_idx, r)
                tt(LG[:, :, :], bank[4][:, 0:32].rearrange("p (k e) -> p k e", k=4),
                   gbias[:, 0, :].unsqueeze(1).to_broadcast([P, 4, EXPERTS]), ALU.add).then_inc(s_lg, 1)
                dve.wait_ge(s_lg, r * 2 + 1)
                tt(LG[:, :, :], LG[:, :, :], gbias[:, 1, :].unsqueeze(1).to_broadcast([P, 4, EXPERTS]), ALU.add)\
                  .then_inc(s_lg, 1)
                wait_apart(dve, s_lg, r * 2 + 2)
                for k in range(4):
                    last = nc.vector.max(top[:, k, :], LG[:, k, :])
                last.then_inc(s_top, 1)
                wait_apart(dve, s_top, r + 1)
                for k in range(4):
                    last = nc.vector.max_index(IDX[:, k, :], top[:, k, :], LG[:, k, :])
                last.then_inc(s_ix, 1)
                dve.wait_ge(s_ix, r + 1)
                nc.vector.tensor_copy(idxf[:, bass.ds(r * 4, 4)], IDX[:, :, 0]).then_inc(s_idx, 1)

            norm(0)
            with dve.Fori(1, TILES // 4) as r:
                norm(r)
                choose(r - 1)
            choose(TILES // 4 - 1)

            dve.wait_ge(s_idx, TILES // 4)
            dve.wait_ge(s_rconst, 2)
            shape = [P, EXPERTS, TILES]
            tt(OH[:, :, :], idxf[:, :].unsqueeze(1).to_broadcast(shape), erow[:, :].unsqueeze(2).to_broadcast(shape),
               ALU.is_equal).then_inc(s_oh, 1)
            dve.wait_ge(s_cp, 1)
            totals = bank[6][:, 0:256]
            flat = lambda a: a[:, :, :].rearrange("p e j -> p (e j)")
            c = lambda i: cnt[:, i, :]
            done(nc.vector.tensor_tensor_scan(flat(run), ones[:, 0:1].to_broadcast([P, EXPERTS * TILES]), totals, 0.0,
                                              ALU.mult, ALU.add))
            done(tt(flat(rt), flat(run), totals, ALU.subtract))
            done(tt(c(0), run[:, :, TILES - 1], rt[:, :, 0], ALU.subtract))
            done(ts(c(1), c(0), 1.0 / P, (P - 1.0) / P - 0.5 + 0.5 / P, ALU.mult, ALU.add))
            done(ts(c(1), c(1), MAGIC, MAGIC, ALU.add, ALU.subtract))
            done(nc.vector.tensor_tensor_scan(c(2), ones[:, 0:1].to_broadcast([P, EXPERTS]), c(1), 0.0, ALU.mult, ALU.add))
            done(tt(c(3), c(2), c(1), ALU.subtract))
            done(stt(c(4), c(3), float(P), rt[:, :, 0], ALU.mult, ALU.subtract))
            done(tt(flat(rt), flat(rt), bank[5][:, 0:256], ALU.add))
            done(tt(rt[:, :, :], rt[:, :, :], c(4).unsqueeze(2).to_broadcast(shape), ALU.add))
            done(tt(flat(rt), flat(rt), flat(OH), ALU.mult))
            done(nc.vector.tensor_reduce(posf[:, :], rt[:, :, :].rearrange("p e j -> p j e"), AX.X, ALU.add))
            nc.vector.tensor_copy(pos[:, :], posf[:, :]).then_inc(s_pos, 1)
            shape = [P, BLOCKS + 1, EXPERTS]
            done(tt(bcmp[:, :, :], c(2).unsqueeze(1).to_broadcast(shape), brow[:, :].unsqueeze(2).to_broadcast(shape),
                    ALU.is_le))
            done(nc.vector.tensor_reduce(bexpf[:, :], bcmp[:, :, :], AX.X, ALU.add))
            done(ts(bexpf[:, :], bexpf[:, :], EXPERTS - 1.0, None, ALU.min))
            nc.vector.tensor_copy(bexp[:, :], bexpf[:, :]).then_inc(s_be2, 1)

            dve.wait_ge(s_ew, 64)
            dve.wait_ge(s_be2, 1)

            def bias_hidden(r, k):
                at = block_of(r, k, 1)
                if at:
                    n, slot, turn = at
                    e = dve.value_load(bexp[0:1, bass.ds(n, 1)], min_val=0, max_val=EXPERTS - 1)
                    dve.wait_ge(s_up, n + 1)
                    wait_past(dve, s_hp, n - 2)
                    tt(Hs[:, slot, :], bank[slot][:, :], B1[:, bass.ds(e, 1), :].rearrange("p e f -> p (e f)"), ALU.add)\
                      .then_inc(s_h, 1)

            def normalize(r, k):
                at = block_of(r, k, 4)
                if at:
                    n, slot, turn = at
                    dve.wait_ge(s_f5, n + 1)
                    nc.vector.reciprocal(ers[:, slot:slot + 1], esd[:, slot:slot + 1]).then_inc(s_f6, 1)
                    dve.wait_ge(s_f6, n + 1)
                    ts(F[:, slot, :], F[:, slot, :], emv[:, slot, 0:1], ers[:, slot:slot + 1], ALU.subtract, ALU.mult)\
                      .then_inc(s_f7, 1)

            def residual(r, k):
                at = block_of(r, k, 3)
                if at:
                    n, slot, turn = at
                    dve.wait_ge(s_dn, n + 1)
                    dve.wait_ge(s_xb2, n + 1)
                    if not isinstance(turn, int) or turn > 0:
                        dve.wait_ge(s_out[slot], turn * 16)
                    tt(F[:, slot, :], bank[7][:, 0:P], O[:, slot, :], ALU.add).then_inc(s_f1, 1)
                    dve.wait_ge(s_f1, n + 1)
                    nc.vector.bn_stats(est[:, slot, :], F[:, slot, :]).then_inc(s_f3, 1)
                    wait_apart(dve, s_f3, n + 1)
                    nc.vector.bn_aggr(emv[:, slot, :], est[:, slot, :]).then_inc(s_f4, 1)

            def step(r, k):
                bias_hidden(r, k)
                normalize(r, k)
                residual(r, k)

            for r in range(2):
                for k in range(3):
                    step(r, k)
            with dve.Fori(2, BLOCKS // 3) as r:
                for k in range(3):
                    step(r, k)
            for r in range(BLOCKS // 3, BLOCKS // 3 + 2):
                for k in range(3):
                    step(r, k)

        @block.tensor
        def _(pe):
            mm = nc.tensor.matmul

            def project(i, k):
                n = i * 4 + k
                slot = k // 2
                if k % 2 == 0:
                    pe.wait_ge(s_xt[slot], (i + 1) * 32)
                wait_past(pe, s_xb, n - 1)
                wait_past(pe, s_z, n - 1)
                for j in range(2):
                    chunk = k % 2 * 2 + j
                    for tap in range(TAPS):
                        at = (CHUNKS - 1 - chunk) * CHUNK + TAPS - 1 - tap
                        mm(bank[k % 2][:, j * CHAN:(j + 1) * CHAN], XR[:, slot, at:at + CHUNK], Wx[:, tap, :],
                           start=(tap == 0), stop=(tap == TAPS - 1))
                    at = chunk * CHUNK
                    last = mm(bank[2 + k % 2][:, j * CHAN:(j + 1) * CHAN], XT[:, slot, at:at + CHUNK], Win[:, CHAN:],
                              start=True, stop=True)
                last.then_inc(s_a, 1)

            pe.wait_ge(s_wx, 1)
            pe.wait_ge(s_pad, 1)
            for k in range(4):
                project(0, k)
            pe.wait_ge(s_sel, 1)
            pe.wait_ge(s_c, 1)
            for g in range(GROUPS):
                last = mm(bank[4 + g // 16][:, 0:CHUNK], Sel[:, g, :], Ctab[:, g, 0:CHUNK], start=(g % 16 == 0),
                          stop=(g % 16 == 15))
            last.then_inc(s_kp, 1)
            with pe.Fori(1, 4) as i:
                for k in range(4):
                    project(i, k)

            def mix(r, k):
                g = r * T_SLOTS + k
                s, y = bank[6 + k % 2], bank[4 + k % 2]
                xg = X[:, bass.ds(g * GH, GH), :]
                out_s = s[:, 0:GH * SCOLS].rearrange("p (h c) -> p h c", h=GH)
                pe.wait_ge(s_bc, g + 1)
                wait_past(pe, s_v, g - 1)
                for lag in range(LAGS):
                    cols = SCOLS - lag * BATCH
                    last = mm(out_s[:, :, lag * BATCH:], BC[:, k % 2, lag, :], xg[:, :, 0:cols], start=(lag == 0),
                              stop=(lag == LAGS - 1))
                last.then_inc(s_s, 1)
                pe.wait_ge(s_t[k], (r + 1) * 16)
                wait_past(pe, s_yc, g - 1)
                for h in range(GH):
                    mm(y[:, h * TILES:(h + 1) * TILES], Tring[:, k, h, :], X[:, bass.ds(g * GH + h, 1), :]
                       .rearrange("p h t -> p (h t)"), start=(h == 0), stop=False)
                pe.wait_ge(s_v, g + 1)
                mm(y[:, 0:GH * TILES].rearrange("p (h t) -> p h t", h=GH)[:, :, BATCH:], BC[:, k % 2, LAGS, :],
                   V[:, k % 2, :, :], start=False, stop=True).then_inc(s_y, 1)

            pe.wait_ge(s_x, PAIRS)
            pe.wait_ge(s_kx, 2)
            for k in range(T_SLOTS):
                mix(0, k)
            with pe.Fori(1, GROUPS // T_SLOTS) as r:
                for k in range(T_SLOTS):
                    mix(r, k)

            pe.wait_ge(s_const, 4)
            pe.wait_ge(s_late, 64)

            def output_projection(r):
                for k in range(4):
                    pe.wait_ge(s_g, r * 4 + (k + 1))
                    wait_past(pe, s_gt, r * 2 + (k // 2 - 1))
                    for j in range(2):
                        at = (k % 2) * 256 + j * P
                        last = nc.tensor.transpose(bank[k // 2][:, at:at + P], G[:, k, j * P:j * P + P], ident[:, :])
                    last.then_inc(s_tp, 1)
                wait_past(pe, s_r, r)
                if isinstance(r, int):
                    pe.wait_ge(s_wo, 16)
                for k in range(4):
                    pe.wait_ge(s_gt, r * 2 + (k // 2 + 1))
                    for j in range(2):
                        last = mm(bank[2][:, k * DM:k * DM + DM], GT[:, k, j * P:j * P + P], WoT[:, j, :],
                                  start=(j == 0), stop=(j == 1))
                    last.then_inc(s_o, 1)

            def logits(r):
                wait_past(pe, s_x1t, r)
                for k in range(4):
                    pe.wait_ge(s_x1, r * 4 + (k + 1))
                    nc.tensor.transpose(bank[3][:, k * P:k * P + P], N4[:, k, :], ident[:, :]).then_inc(s_xp, 1)
                pe.wait_ge(s_x1t, r + 1)
                wait_past(pe, s_lg, r * 2)
                for k in range(4):
                    last = mm(bank[4][:, k * EXPERTS:(k + 1) * EXPERTS], X1T[:, k, :], gwT[:, :], start=True, stop=True)
                last.then_inc(s_lp, 1)

            output_projection(0)
            with pe.Fori(1, TILES // 4) as r:
                output_projection(r)
                logits(r - 1)
            logits(TILES // 4 - 1)

            pe.wait_ge(s_oh, 1)
            pe.wait_ge(s_rconst, 2)
            onehot = OH[:, :, :].rearrange("p e j -> p (e j)")
            mm(bank[5][:, 0:256], before[:, :], onehot, start=True, stop=True)
            mm(bank[6][:, 0:256], ones[:, :], onehot, start=True, stop=True).then_inc(s_cp, 1)

            pe.wait_ge(s_ew, 64)
            pe.wait_ge(s_be2, 1)

            def transpose_slots(r, k):
                at = block_of(r, k, 0)
                if at:
                    n, slot, turn = at
                    pe.wait_ge(s_xs[slot], (turn + 1) * 16)
                    wait_past(pe, s_ext, n)
                    nc.tensor.transpose(bank[6][:, 0:P], XS[:, slot, 0:DM], ident[:, :]).then_inc(s_ep, 1)

            def up(r, k):
                at = block_of(r, k, 1)
                if at:
                    n, slot, turn = at
                    e = pe.value_load(bexp[0:1, bass.ds(n, 1)], min_val=0, max_val=EXPERTS - 1)
                    pe.wait_ge(s_ext, n + 1)
                    wait_past(pe, s_h, n - 2)
                    mm(bank[slot][:, :], XsT[:, slot, :], W1[:, bass.ds(e, 1), :].rearrange("p e f -> p (e f)"),
                       start=True, stop=True).then_inc(s_up, 1)

            def transpose_hidden(r, k):
                at = block_of(r, k, 2)
                if at:
                    n, slot, turn = at
                    pe.wait_ge(s_h, n + 1)
                    wait_past(pe, s_ht, n - 2)
                    for c in range(FCH):
                        last = nc.tensor.transpose(bank[3 + slot][:, c * P:c * P + P], Hs[:, slot, c * P:c * P + P],
                                                   ident[:, :])
                    last.then_inc(s_hp, 1)

            def down(r, k):
                at = block_of(r, k, 3)
                if at:
                    n, slot, turn = at
                    e = pe.value_load(bexp[0:1, bass.ds(n, 1)], min_val=0, max_val=EXPERTS - 1)
                    pe.wait_ge(s_ht, n + 1)
                    wait_past(pe, s_f1, n)
                    for c in range(FCH):
                        last = mm(bank[7][:, 0:P], HT[:, slot, c * P:c * P + P],
                                  W2[:, bass.ds(e, 1), c * DM:(c + 1) * DM].rearrange("p e d -> p (e d)"),
                                  start=(c == 0), stop=(c == FCH - 1))
                    last.then_inc(s_dn, 1)

            def step(r, k):
                transpose_slots(r, k)
                up(r, k)
                transpose_hidden(r, k)
                down(r, k)

            for r in range(2):
                for k in range(3):
                    step(r, k)
            with pe.Fori(2, BLOCKS // 3) as r:
                for k in range(3):
                    step(r, k)
            for k in range(3):
                step(BLOCKS // 3, k)


_ORDER = ("hidden", "hidden_t", "hidden_r", "w_in_t", "conv_w", "conv_b", "log_dt", "log_a", "a_imag", "c_re", "c_im", "d_skip",
          "w_out_t", "gate_w_t", "gate_b", "expert_bias", "w1", "b1", "w2", "b2")


def kernel(**inputs):
    import numpy as _np
    import concourse.bacc as _bacc
    from concourse import mybir as _mybir
    from concourse.bass_utils import run_bass_kernel_spmd as _run

    a = {name: _np.asarray(value) for name, value in inputs.items()}

    def by_group(x):
        return x.reshape((GH, GROUPS) + x.shape[1:]).swapaxes(0, 1).reshape(x.shape)

    def by_state(x):
        return x.reshape(GH, GROUPS, STATES).transpose(0, 2, 1).reshape(GH * STATES, GROUPS)

    hidden = a["L0_attn_hidden_states"]
    w_in = a["L0_attn_W_in"]
    laid = {
        "hidden": hidden,
        "hidden_t": hidden.transpose(2, 0, 1),
        "hidden_r": hidden[:, ::-1].transpose(2, 0, 1),
        "w_in_t": _np.concatenate([by_group(w_in[:CHAN]), by_group(w_in[CHAN:])]).T,
        "conv_w": by_group(a["L0_attn_conv_w"]).T,
        "conv_b": by_group(a["L0_attn_conv_b"])[None],
        "log_dt": a["L0_attn_log_dt"].reshape(GH, GROUPS),
        "log_a": by_state(a["L0_attn_log_A_real"]),
        "a_imag": by_state(a["L0_attn_A_imag"]),
        "c_re": by_state(a["L0_attn_C_re"]),
        "c_im": by_state(a["L0_attn_C_im"]),
        "d_skip": by_group(a["L0_attn_D"]).reshape(2, P).T,
        "w_out_t": by_group(a["L0_attn_W_out"].T),
        "gate_w_t": a["L0_ffn_gate_w"].T,
        "gate_b": a["L0_ffn_gate_b"][None],
        "expert_bias": a["L0_ffn_expert_bias"][None],
        "w1": a["L0_ffn_w1"],
        "b1": a["L0_ffn_b1"],
        "w2": a["L0_ffn_w2"],
        "b2": a["L0_ffn_b2"],
    }
    nc = _bacc.Bacc("TRN2", target_bir_lowering=False, num_devices=1)
    arrays, args = {}, []
    for name in _ORDER:
        x = _np.ascontiguousarray(laid[name])
        arrays[name] = x
        args.append(nc.dram_tensor(name, x.shape, _mybir.dt.from_np(x.dtype), kind="ExternalInput").ap())
    args.append(nc.dram_tensor("out", (BATCH, SEQ, DM), F32, kind="ExternalOutput").ap())
    build(nc, *args)
    result = _run(nc, [arrays], core_ids=[0])
    return result.results[0]["out"]
```

```python
import math
from contextlib import ExitStack

import numpy as np
import concourse.bass as bass
from concourse import mybir

F32 = mybir.dt.float32
I32 = mybir.dt.int32
U32 = mybir.dt.uint32
ALU = mybir.AluOpType
ACT = mybir.ActivationFunctionType
AX = mybir.AxisListType

P = 128
BATCH, SEQ, DM = 8, 512, 128
CHAN, STATES, TAPS = 256, 8, 4
EXPERTS, DFF = 8, 512
TOKENS = BATCH * SEQ
CHUNK = P
CHUNKS = SEQ // CHUNK
TILES = TOKENS // P
PAIRS = TILES // 2
GH = 8
GROUPS = CHAN // GH
LAGS = CHUNKS - 1
SCOLS = LAGS * BATCH
KLEN = CHUNK + 1
KROW = 2 * CHUNK
BLOCKS = TILES + EXPERTS - 1
ROW = DM + 4
TOKEN_COL = DM
NO_TOKEN = 1 << 17
FCH = DFF // P
EPS = 1e-5
MAGIC = float(1.5 * 2 ** 23)
TWO_PI = 6.2831850
QUARTER = float(math.pi / 2)
TURN = float(1.0 / (2.0 * math.pi))

T_SLOTS = 8
X_BANKS, Z_BANKS = (0, 1, 4, 5), (2, 3, 6, 7)
A_BATCH = 2


def wait_past(engine, semaphore, count):
    if not isinstance(count, int) or count > 0:
        engine.wait_ge(semaphore, count)


def wait_apart(engine, semaphore, count):
    if not isinstance(count, int) or count > 0:
        engine.wait_ge(semaphore, count)
        engine.nop(nofuse=True)


def build(nc, hidden, hidden_t, hidden_r, w_in_t, conv_w, conv_b, states, d_skip, w_out_t, gate_w_t,
          gate_b, expert_bias, w1, b1, w2, b2, out):
    kext = nc.dram_tensor("kernel_rows", [CHAN, KROW], F32).ap()
    rows_dram = nc.dram_tensor("decay_and_turns", [2, GH * STATES * GROUPS], F32).ap()
    toeplitz = bass.AP(kext.tensor, 0, [[1, P], [KROW, CHAN], [1, CHUNK]])
    slots_dram = nc.dram_tensor("dispatched_rows", [BLOCKS * P, ROW], F32).ap()
    out_rows = out.rearrange("b l d -> (b l) d")
    hidden_rows = hidden.rearrange("b l d -> (b l) d")

    ctx = ExitStack()
    with ctx:
        def sb(name, shape, dt=F32):
            return ctx.enter_context(nc.sbuf_tensor(name, shape, dt))

        def sem(name):
            return ctx.enter_context(nc.semaphore(name))

        bank = [ctx.enter_context(nc.psum_tensor(f"bank{i}", [P, 512], F32)) for i in range(8)]

        X = sb("X", [P, CHAN, TILES])
        Z = sb("Z", [P, TILES, CHAN])
        BR = sb("BR", [P, 3 * 4096])
        CR = sb("CR", [P, GROUPS * KLEN])
        TR = sb("TR", [P, T_SLOTS * GH * CHUNK])
        RW = sb("RW", [P, 4096])
        EN = sb("EN", [P, 3840])

        Btab = BR[:, :].rearrange("p (m r n g) -> p m r n g", m=3, r=2, g=GROUPS)
        Ctab = CR[:, :].rearrange("p (g j) -> p g j", g=GROUPS)
        turnsC = BR[:, 0:GROUPS * KLEN].rearrange("p (g j) -> p g j", g=GROUPS)
        wholeC = BR[:, GROUPS * KLEN:2 * GROUPS * KLEN].rearrange("p (g j) -> p g j", g=GROUPS)
        Tring = TR[:, :].rearrange("p (s h u) -> p s h u", s=T_SLOTS, h=GH)
        Sel = TR[:, 0:4096].rearrange("p (g c) -> p g c", g=GROUPS)
        X1 = TR[:, 0:TILES * ROW].rearrange("p (j c) -> p j c", j=TILES)
        decay_row = RW[:, 0:2048]
        turns_row = RW[:, 2048:4096]
        decay = EN[:, 0:2048].rearrange("p (s c) -> p s c", s=2)

        XT = sb("XT", [P, A_BATCH, SEQ])
        XR = EN[:, 2688:2688 + A_BATCH * (SEQ + TAPS - 1)].rearrange("p (k c) -> p k c", k=A_BATCH)
        Win = sb("Win", [P, 2 * CHAN])
        Wx = sb("Wx", [P, TAPS, CHAN])
        cbias = sb("cbias", [P, CHAN])
        BC = Wx[:, :, :].rearrange("p t c -> p (t c)").rearrange("p (k m c) -> p k m c", k=2, m=4)
        V = XT[:, :, 0:GH * SCOLS].rearrange("p k (h c) -> p k h c", h=GH)
        prm = sb("prm", [P, 5, GROUPS])
        sm = sb("sm", [P, 24, GROUPS])
        smt = EN[:, 2560:2560 + 2 * GROUPS].rearrange("p (i g) -> p i g", i=2)
        quarter = sb("quarter", [P, 1])
        tau = sb("tau", [P, LAGS])
        jrow = sb("jrow", [P, KLEN])
        phase = sb("phase", [P, 1])
        epscol = sb("epscol", [P, 1])
        mask16 = sb("mask16", [P, 2 * GH])
        mask8 = sb("mask8", [P, GH])
        Kx = TR[:, 4096:4096 + 2 * KROW].rearrange("p (j c) -> p j c", j=2)
        dskip = sb("dskip", [P, 2])
        ident = sb("ident", [P, P])
        LATE = 2048 + 384
        before = CR[:, LATE:LATE + P]
        ones = CR[:, LATE + P:LATE + 2 * P]
        WoT = CR[:, LATE + 256:LATE + 512].rearrange("p (j d) -> p j d", j=2)
        gwT = sb("gwT", [P, EXPERTS])
        gbias = sb("gbias", [P, 2, EXPERTS])
        empty_row = TR[:, 4096 + 2 * KROW:4096 + 2 * KROW + ROW]

        XG = RW[:, 0:512].rearrange("p (k h t) -> p k h t", k=2, h=GH)
        YT = RW[:, 512:1024].rearrange("p (k c) -> p k c", k=2)

        G = RW[:, 0:1024].rearrange("p (k c) -> p k c", k=4)
        GT = RW[:, 1024:2048].rearrange("p (k c) -> p k c", k=4)
        HR = RW[:, 2048:2560].rearrange("p (k c) -> p k c", k=4)
        R = RW[:, 2560:3072].rearrange("p (k c) -> p k c", k=4)
        X1T = RW[:, 3072:3584].rearrange("p (k c) -> p k c", k=4)
        N4 = RW[:, 3584:4096].rearrange("p (k c) -> p k c", k=4)
        st = sb("st", [P, 4, 6])
        mv = sb("mv", [P, 4, 2])
        sd = sb("sd", [P, 4])
        rs = sb("rs", [P, 4])
        LG = sb("LG", [P, 4, EXPERTS])
        top = sb("top", [P, 4, 8])
        IDX = CR[:, LATE + 512:LATE + 544].bitcast(U32).rearrange("p (j c) -> p j c", c=8)

        def late(at, shape, dt=F32):
            view = CR[:, LATE + 768 + at:LATE + 768 + at + shape]
            return view if dt == F32 else view.bitcast(dt)

        idxf = late(0, TILES)
        posf = late(32, TILES)
        pos = late(64, TILES, U32)
        brow = late(96, BLOCKS + 1)
        bexpf = late(136, BLOCKS + 1)
        bexp = late(176, BLOCKS + 1, I32)
        tok = late(216, 6, U32)
        cnt = late(256, 6 * EXPERTS).rearrange("p (i e) -> p i e", e=EXPERTS)
        erow = late(304, EXPERTS)
        OH = EN[:, 0:256].rearrange("p (e j) -> p e j", e=EXPERTS)
        run = EN[:, 256:512].rearrange("p (e j) -> p e j", e=EXPERTS)
        rt = EN[:, 512:768].rearrange("p (e j) -> p e j", e=EXPERTS)
        bcmp = EN[:, 768:768 + (BLOCKS + 1) * EXPERTS].rearrange("p (b e) -> p b e", e=EXPERTS)

        W1 = BR[:, 0:4096].rearrange("p (e f) -> p e f", e=EXPERTS)
        W2 = BR[:, 4096:8192].rearrange("p (e q) -> p e q", e=EXPERTS)
        B1 = BR[:, 8192:12288].rearrange("p (e f) -> p e f", e=EXPERTS)
        B2 = CR[:, 0:1024].rearrange("p (e d) -> p e d", e=EXPERTS)
        XS = CR[:, 1024:1024 + 3 * ROW].rearrange("p (s c) -> p s c", s=3)
        O = CR[:, 2048:2048 + 384].rearrange("p (s c) -> p s c", s=3)
        Hs = EN[:, 0:1536].rearrange("p (s c) -> p s c", s=3)
        HT = EN[:, 1536:3072].rearrange("p (s c) -> p s c", s=3)
        XsT = EN[:, 3072:3456].rearrange("p (s c) -> p s c", s=3)
        F = EN[:, 3456:3840].rearrange("p (s c) -> p s c", s=3)
        est = sb("est", [P, 3, 6])
        emv = sb("emv", [P, 3, 2])
        esd = sb("esd", [P, 3])
        ers = sb("ers", [P, 3])

        x_pairs = X[:, :, :].rearrange("p c (h j b) -> p c h j b", h=2, b=BATCH)
        z_pairs = Z[:, :, :].rearrange("p (h j b) c -> p h j b c", h=2, b=BATCH)

        s_params = sem("params_loaded")
        s_win = sem("w_in_loaded")
        s_cw = sem("conv_loaded")
        s_late = sem("late_weights_loaded")
        s_xt = [sem(f"batch_loaded{k}") for k in range(A_BATCH)]
        s_pad = sem("padding_zeroed")
        s_wo = sem("output_weights_loaded")
        s_wx = sem("conv_weights_ready")
        s_const = sem("constants_ready")
        s_pstep = sem("pool_step")
        s_vstep = sem("vector_step")
        s_exp1 = sem("rates_ready")
        s_ang = sem("angles_ready")
        s_tanh = sem("tanh_ready")
        s_sin1 = sem("sines_ready")
        s_dec = sem("decay_rates_ready")
        s_rat = sem("ratio_ready")
        s_atan = sem("arctan_ready")
        s_hyp = sem("hypotenuse_ready")
        s_rows = sem("rows_written")
        s_rowl = sem("rows_broadcast")
        s_cexpo = sem("c_exponents_ready")
        s_ce = sem("c_decay_ready")
        s_ct = sem("c_turns_ready")
        s_cs = sem("c_sines_ready")
        s_c = sem("c_table_ready")
        s_sel0 = sem("selectors_zeroed")
        s_sel = sem("selectors_ready")
        s_kp = sem("kernel_rows_summed")
        s_kx = sem("kernel_rows_ready")
        s_kd = sem("kernel_rows_stored")
        s_a = sem("projection_ready")
        s_xb = sem("x_biased")
        s_x = sem("x_ready")
        s_yd = sem("product_transposed")
        s_xg = sem("group_input_ready")
        s_tm = sem("toeplitz_multiplied")
        s_yt = sem("product_copied")
        s_cc = sem("output_table_ready")
        s_cg = sem("c_turns_multiplied")
        s_zs = sem("gates_ready")
        s_b3 = sem("last_sines_decayed")
        s_z = sem("z_ready")
        s_bt = sem("state_turns_ready")
        s_bw = sem("state_turns_step")
        s_bs = sem("state_sines_ready")
        s_be = sem("state_decay_ready")
        s_b = sem("state_table_ready")
        s_t = [sem(f"toeplitz_loaded{k}") for k in range(T_SLOTS)]
        s_bc = sem("group_tables_ready")
        s_s = sem("states_summed")
        s_v = sem("states_ready")
        s_y = sem("group_done")
        s_yc = sem("mixer_output_copied")
        s_g = sem("gated_ready")
        s_tp = sem("gated_transposed")
        s_gt = sem("gated_t_copied")
        s_o = sem("mixer_projected")
        s_hr = [sem(f"residual_loaded{k}") for k in range(4)]
        s_r = sem("residual_added")
        s_st = sem("stats_ready")
        s_mv = sem("moments_ready")
        s_sd = sem("deviation_ready")
        s_rs = sem("scale_ready")
        s_x1 = sem("x1_ready")
        s_xp = sem("x1_transposed")
        s_x1t = sem("x1_t_copied")
        s_lp = sem("logits_summed")
        s_lg = sem("logits_ready")
        s_top = sem("maxima_ready")
        s_ix = sem("indices_ready")
        s_idx = sem("choices_ready")
        s_empty = sem("slots_emptied")
        s_oh = sem("one_hot_ready")
        s_cp = sem("counts_ready")
        s_pos = sem("positions_ready")
        s_be2 = sem("block_experts_ready")
        s_sc = sem("rows_dispatched")
        s_rconst = sem("routing_constants_ready")
        s_tk = sem("token_numbers_passed")
        s_tok = sem("token_numbers_ready")
        s_x1c = sem("x1_kept")
        s_xb2 = sem("residual_biased")
        s_rstep = sem("routing_step")
        s_ew = sem("expert_weights_loaded")
        s_xs = [sem(f"slots_loaded{k}") for k in range(3)]
        s_ep = sem("slots_transposed")
        s_ext = sem("slots_t_copied")
        s_up = sem("hidden_summed")
        s_h = sem("hidden_biased")
        s_hp = sem("hidden_transposed")
        s_ht = sem("hidden_ready")
        s_dn = sem("expert_out_summed")
        s_f1 = sem("expert_bias_added")
        s_f2 = sem("expert_residual_added")
        s_f3 = sem("expert_stats_ready")
        s_f4 = sem("expert_moments_ready")
        s_f5 = sem("expert_deviation_ready")
        s_f6 = sem("expert_scale_ready")
        s_f7 = sem("normalized_ready")
        s_out = [sem(f"out_stored{k}") for k in range(3)]

        LOG_DT, LOG_A, A_IM, C_RE, C_IM = range(5)
        (DT, EA, AR, AI, TURNS, TH, EM1, ER, CM1, WR, WI, T1, T2, PP, QQ, AXX, AYY, MX, RAT, PHI, AMP, DEN, T3,
         T4) = range(24)

        def block_of(r, k, behind):
            n = r * 3 + (k - behind)
            if isinstance(n, int) and not 0 <= n < BLOCKS:
                return None
            return n, (k - behind) % 3, r + (k - behind) // 3

        block = ctx.enter_context(nc.Block())

        @block.sync
        def _(sp):
            sp.dma_start(prm[:, :, :], states).then_inc(s_params, 16)
            sp.dma_start(Wx[:, :, :].rearrange("p t c -> p (t c)"), conv_w.rearrange("t c -> (t c)").unsqueeze(0).to_broadcast([P, TAPS * CHAN]))\
              .then_inc(s_cw, 16)
            sp.dma_start(cbias[:, :], conv_b.to_broadcast([P, CHAN])).then_inc(s_cw, 16)
            sp.dma_start(dskip[:, :], d_skip).then_inc(s_late, 16)
            sp.dma_start(gwT[:, :], gate_w_t).then_inc(s_late, 16)
            sp.dma_start(gbias[:, 0, :], gate_b.to_broadcast([P, EXPERTS])).then_inc(s_late, 16)
            sp.dma_start(gbias[:, 1, :], expert_bias.to_broadcast([P, EXPERTS])).then_inc(s_late, 16)
            sp.wait_ge(s_dec, 2)
            sp.dma_start(rows_dram[0, :].rearrange("(n g) -> n g", g=GROUPS), sm[0:64, AR, :]).then_inc(s_rows, 16)
            sp.dma_start(rows_dram[1, :].rearrange("(n g) -> n g", g=GROUPS), sm[0:64, TURNS, :]).then_inc(s_rows, 16)
            sp.wait_ge(s_rows, 32)
            sp.dma_start(decay_row, rows_dram[0:1, :].to_broadcast([P, 2048])).then_inc(s_rowl, 16)
            sp.dma_start(turns_row, rows_dram[1:2, :].to_broadcast([P, 2048])).then_inc(s_rowl, 16)
            sp.wait_ge(s_const, 1)
            for n in range(BLOCKS):
                sp.dma_start(slots_dram[n * P:(n + 1) * P, :], empty_row[:, :]).then_inc(s_empty, 16)
            sp.wait_ge(s_kx, 3)
            sp.dma_start(kext.rearrange("(j p) c -> p j c", p=P), Kx[:, :, :]).then_inc(s_kd, 16)
            sp.wait_ge(s_kd, 16)
            sp.wait_ge(s_empty, 16 * BLOCKS)

            def load_toeplitz(r, k):
                group = r * T_SLOTS + k
                if not isinstance(r, int):
                    sp.wait_ge(s_tm, group - (T_SLOTS - 1))
                sp.dma_start(Tring[:, k, :, :], toeplitz[:, bass.ds(group * GH, GH), :]).then_inc(s_t[k], 16)

            for k in range(T_SLOTS):
                load_toeplitz(0, k)
            with sp.Fori(1, GROUPS // T_SLOTS) as r:
                for k in range(T_SLOTS):
                    load_toeplitz(r, k)

            def load_residual(r, k):
                if not isinstance(r, int):
                    sp.wait_ge(s_r, r)
                row = (r * CHUNKS + k) * P
                sp.dma_start(HR[:, k, :], hidden_rows[bass.ds(row, P), :]).then_inc(s_hr[k], 16)

            sp.wait_ge(s_b, 2 * LAGS)
            for k in range(4):
                load_residual(0, k)
            sp.wait_ge(s_y, GROUPS)
            sp.dma_start(WoT, w_out_t.rearrange("(j p) d -> p j d", p=P)).then_inc(s_wo, 16)
            sp.dma_start(W1, w1.rearrange("e d f -> d e f")).then_inc(s_ew, 16)
            sp.dma_start(W2.rearrange("p e (c d) -> p e c d", c=FCH),
                         w2.rearrange("e (c p) d -> p e c d", p=P)).then_inc(s_ew, 16)
            sp.dma_start(B1, b1.rearrange("e f -> (e f)").unsqueeze(0).to_broadcast([P, EXPERTS * DFF]))\
              .then_inc(s_ew, 16)
            sp.dma_start(B2, b2.rearrange("e d -> (e d)").unsqueeze(0).to_broadcast([P, EXPERTS * DM]))\
              .then_inc(s_ew, 16)
            with sp.Fori(1, TILES // 4) as r:
                for k in range(4):
                    load_residual(r, k)

            def load_slots(r, k):
                n = r * 3 + k
                wait_past(sp, s_ep, n - 2)
                wait_past(sp, s_xb2, n - 2)
                sp.dma_start(XS[:, k, :], slots_dram[bass.ds(n * P, P), :]).then_inc(s_xs[k], 16)

            sp.wait_ge(s_sc, 16 * TILES)
            for k in range(3):
                load_slots(0, k)
            with sp.Fori(1, BLOCKS // 3) as r:
                for k in range(3):
                    load_slots(r, k)
            for k in range(3):
                sp.wait_ge(s_out[k], 16 * (BLOCKS // 3))

        @block.gpsimd
        def _(pool):
            nc.gpsimd.memset(empty_row[:, :], 0.0).then_inc(s_pstep, 1)
            pool.wait_ge(s_pstep, 1)
            nc.gpsimd.memset(empty_row[:, TOKEN_COL:TOKEN_COL + 1].bitcast(I32), NO_TOKEN).then_inc(s_const, 1)
            nc.gpsimd.memset(XR[:, :, SEQ:], 0.0).then_inc(s_pad, 1)
            nc.gpsimd.iota(jrow[:, :], [[1, KLEN]], base=0, channel_multiplier=0, allow_small_or_imprecise_dtypes=True)
            nc.gpsimd.iota(tau[:, :], [[CHUNK, LAGS]], base=0, channel_multiplier=1, allow_small_or_imprecise_dtypes=True)
            nc.gpsimd.memset(mask16[:, :], 1.0).then_inc(s_pstep, 1)
            pool.wait_ge(s_pstep, 2)
            nc.gpsimd.affine_select(out=mask16[:, :], in_=mask16[:, :], compare_op=ALU.is_ge, fill=0.0, base=0,
                                    pattern=[[-GH, 2 * GH]], channel_multiplier=1).then_inc(s_pstep, 1)
            pool.wait_ge(s_pstep, 3)
            nc.gpsimd.affine_select(out=mask16[:, :], in_=mask16[:, :], compare_op=ALU.is_ge, fill=0.0, base=GH - 1,
                                    pattern=[[GH, 2 * GH]], channel_multiplier=-1).then_inc(s_pstep, 1)
            pool.wait_ge(s_pstep, 4)
            nc.gpsimd.tensor_tensor(mask8[:, :], mask16[:, 0:GH], mask16[:, GH:2 * GH], ALU.add).then_inc(s_const, 1)
            nc.gpsimd.memset(TR[:, 0:4096], 0.0).then_inc(s_sel0, 1)
            pool.wait_ge(s_dec, 2)
            nc.gpsimd.tensor_tensor(Ctab, sm[:, AR, :].unsqueeze(2).to_broadcast([P, GROUPS, KLEN]),
                                    jrow[:, :].unsqueeze(1).to_broadcast([P, GROUPS, KLEN]), ALU.mult)\
              .then_inc(s_cexpo, 1)
            nc.gpsimd.tensor_tensor(turnsC, sm[:, TURNS, :].unsqueeze(2).to_broadcast([P, GROUPS, KLEN]),
                                    jrow[:, :].unsqueeze(1).to_broadcast([P, GROUPS, KLEN]), ALU.mult).then_inc(s_cg, 1)
            nc.gpsimd.memset(Kx[:, :, :], 0.0).then_inc(s_const, 1)
            nc.gpsimd.memset(ident[:, :], 1.0)
            nc.gpsimd.memset(epscol[:, :], EPS)
            nc.gpsimd.memset(quarter[:, :], QUARTER).then_inc(s_pstep, 1)
            pool.wait_ge(s_pstep, 5)
            nc.gpsimd.affine_select(out=ident[:, :], in_=ident[:, :], compare_op=ALU.is_equal, fill=0.0, base=0,
                                    pattern=[[-1, P]], channel_multiplier=1).then_inc(s_const, 1)

            def state_product(i, parts):
                pool.wait_ge(s_bs, i * 2)
                for half in range(2):
                    pool.wait_ge(s_be, i * 2 + (half - 1))
                    for q in parts:
                        part = Btab[:, bass.ds(i - 1, 1), q, half * 32:half * 32 + 32, :].rearrange("p m n g -> p (m n g)")
                        last = nc.gpsimd.tensor_tensor(part, part, decay[:, half, :], ALU.mult)
                    last.then_inc(s_b, 1)

            with pool.Fori(1, LAGS) as i:
                state_product(i, (0, 1))
            state_product(LAGS, (0,))

            def group_tables(r, k):
                g = r * 2 + k
                wait_apart(pool, s_s, g - 1)
                nc.gpsimd.tensor_copy(BC[:, k, 0:LAGS, :], BR[:, :].rearrange("p (m c g) -> p m c g", m=LAGS, g=GROUPS)
                                      [:, :, :, bass.ds(g, 1)].rearrange("p m c g -> p m (c g)")).then_inc(s_bc, 1)
                wait_apart(pool, s_y, g - 1)
                nc.gpsimd.tensor_copy(BC[:, k, LAGS, :], Ctab[:, bass.ds(g, 1), 1:KLEN].rearrange("p g j -> p (g j)"))\
                  .then_inc(s_cc, 1)

            pool.wait_ge(s_b, 2 * LAGS)
            pool.wait_ge(s_b3, 2)
            pool.wait_ge(s_c, 1)
            pool.wait_ge(s_a, PAIRS)
            for k in range(2):
                group_tables(0, k)
            with pool.Fori(1, GROUPS // 2) as r:
                for k in range(2):
                    group_tables(r, k)

            def gate(r):
                wait_past(pool, s_tp, r * 4)
                for k in range(4):
                    nc.gpsimd.tensor_tensor(G[:, k, :], X[:, :, bass.ds(r + k * BATCH, 1)].rearrange("p c t -> p (c t)"),
                                            Z[:, bass.ds(r + k * BATCH, 1), :].rearrange("p t c -> p (t c)"), ALU.mult)\
                      .then_inc(s_g, 1)

            def keep_x1(r):
                wait_apart(pool, s_x1, (r + 1) * 4)
                nc.gpsimd.tensor_copy(X1[:, bass.ds(r * 4, 4), 0:DM], N4).then_inc(s_x1c, 1)

            pool.wait_ge(s_yc, GROUPS)
            pool.wait_ge(s_zs, GROUPS // 2)
            nc.gpsimd.iota(X1[:, :, TOKEN_COL:TOKEN_COL + 1].bitcast(I32), [[P, TILES], [0, 1]], base=0,
                           channel_multiplier=1)
            nc.gpsimd.memset(X1[:, :, TOKEN_COL + 1:ROW], 0.0).then_inc(s_tok, 1)
            gate(0)
            nc.gpsimd.memset(ones, 1.0)
            nc.gpsimd.iota(erow, [[1, EXPERTS]], base=0, channel_multiplier=0, allow_small_or_imprecise_dtypes=True)
            nc.gpsimd.iota(brow, [[1, BLOCKS + 1]], base=0, channel_multiplier=0, allow_small_or_imprecise_dtypes=True)
            nc.gpsimd.memset(before, 1.0).then_inc(s_rconst, 1)
            pool.wait_ge(s_rconst, 1)
            nc.gpsimd.affine_select(out=before, in_=before, compare_op=ALU.is_gt, fill=0.0, base=0, pattern=[[1, P]],
                                    channel_multiplier=-1).then_inc(s_rconst, 1)
            with pool.Fori(1, TILES // 4) as r:
                gate(r)
                keep_x1(r - 1)
            keep_x1(TILES // 4 - 1)

            pool.wait_ge(s_tok, 1)
            pool.wait_ge(s_x1c, TILES // 4)
            pool.wait_ge(s_pos, 1)
            pool.wait_ge(s_empty, 16 * BLOCKS)
            for j in range(TILES):
                pool.indirect_dma_start(slots_dram, bass.IndirectOffsetOnAxis(pos[:, j:j + 1], 0), X1[:, j, :], None)\
                    .then_inc(s_sc, 16)

            pool.wait_ge(s_ew, 64)
            pool.wait_ge(s_be2, 1)

            def residual_and_bias(r, k):
                at = block_of(r, k, 0)
                if at:
                    n, slot, turn = at
                    e = pool.value_load(bexp[0:1, bass.ds(n, 1)], min_val=0, max_val=EXPERTS - 1)
                    pool.wait_ge(s_xs[slot], (turn + 1) * 16)
                    wait_past(pool, s_f1, n - 2)
                    nc.gpsimd.tensor_tensor(O[:, slot, :], XS[:, slot, 0:DM],
                                            B2[:, bass.ds(e, 1), :].rearrange("p e d -> p (e d)"), ALU.add)
                    wait_apart(pool, s_tk, n - 2)
                    nc.gpsimd.tensor_copy(tok[:, slot:slot + 1], XS[:, slot, TOKEN_COL:TOKEN_COL + 1].bitcast(U32))\
                      .then_inc(s_xb2, 1)

            def pass_tokens(r, k):
                at = block_of(r, k, 3)
                if at:
                    n, slot, turn = at
                    if not isinstance(turn, int) or turn > 0:
                        pool.wait_ge(s_out[slot], turn * 16)
                    wait_apart(pool, s_xb2, n + 1)
                    nc.gpsimd.tensor_copy(tok[:, 3 + slot:4 + slot], tok[:, slot:slot + 1]).then_inc(s_tk, 1)

            def store(r, k):
                at = block_of(r, k, 4)
                if at:
                    n, slot, turn = at
                    wait_apart(pool, s_f7, n + 1)
                    wait_apart(pool, s_tk, n + 1)
                    pool.indirect_dma_start(out_rows, bass.IndirectOffsetOnAxis(tok[:, 3 + slot:4 + slot], 0), F[:, slot, :],
                                            None, bounds_check=TOKENS - 1, oob_is_err=False).then_inc(s_out[slot], 16)

            def step(r, k):
                pass_tokens(r, k)
                residual_and_bias(r, k)
                store(r, k)

            for r in range(2):
                for k in range(3):
                    step(r, k)
            with pool.Fori(2, BLOCKS // 3) as r:
                for k in range(3):
                    step(r, k)
            for r in range(BLOCKS // 3, BLOCKS // 3 + 2):
                for k in range(3):
                    step(r, k)

        @block.scalar
        def _(act):
            act.dma_start(Win[:, :], w_in_t).then_inc(s_win, 16)
            for k in range(A_BATCH):
                act.dma_start(XR[:, k, 0:SEQ], hidden_r[:, k, :]).then_inc(s_xt[k], 16)
                act.dma_start(XT[:, k, :], hidden_t[:, k, :]).then_inc(s_xt[k], 16)

            act.wait_ge(s_params, 16)
            nc.scalar.activation(sm[:, DT, :], prm[:, LOG_DT, :], ACT.Exp)
            nc.scalar.activation(sm[:, EA, :], prm[:, LOG_A, :], ACT.Exp).then_inc(s_exp1, 1)
            act.wait_ge(s_dec, 1)
            nc.scalar.activation(sm[:, TH, :], sm[:, AR, :], ACT.Tanh, scale=0.5).then_inc(s_tanh, 1)
            act.wait_ge(s_ang, 1)
            nc.scalar.activation(smt[:, :, :], smt[:, :, :], ACT.Sin, scale=TWO_PI).then_inc(s_sin1, 1)
            act.wait_ge(s_cexpo, 1)
            nc.scalar.activation(CR[:, :], CR[:, :], ACT.Exp).then_inc(s_ce, 1)
            act.wait_ge(s_rat, 1)
            nc.scalar.activation(sm[:, PHI, :], sm[:, RAT, :], ACT.Arctan).then_inc(s_atan, 1)
            nc.scalar.activation(sm[:, T4, :], sm[:, T3, :], ACT.Sqrt).then_inc(s_hyp, 1)

            def keep_z(i, k):
                n = i * 4 + k
                act.wait_ge(s_a, n + 1)
                nc.scalar.activation(z_pairs[:, k % 2, :, bass.ds(i * 2 + k // 2, 1), :].rearrange("p j b c -> p j (b c)"),
                                     bank[Z_BANKS[k]][:, :].rearrange("p (j c) -> p j c", j=2), ACT.Copy).then_inc(s_z, 1)

            def next_batch(i, k):
                act.wait_ge(s_a, i * 4 + (k * 2 + 2))
                for dst, src in ((XR, hidden_r), (XT, hidden_t)):
                    act.dma_start(dst[:, k, 0:SEQ], src[:, bass.ds((i + 1) * A_BATCH + k, 1), :]
                                  .rearrange("d b l -> d (b l)")).then_inc(s_xt[k], 16)

            def state_sines(i):
                for q, scale, bias, count in ((1, TWO_PI, 0.0, 1), (0, -TWO_PI, quarter[:, :], 2)):
                    rows = Btab[:, bass.ds(i - 1, 1), q, :, :].rearrange("p m n g -> p (m n g)")
                    act.wait_ge(s_bt, i * 2)
                    nc.scalar.activation(rows, rows, ACT.Sin, scale=scale, bias=bias).then_inc(s_bs, 1)

            def state_decay(i, half):
                wait_past(act, s_b, i * 2 + (half - 3))
                nc.scalar.activation(decay[:, half, :], decay_row[:, half * 1024:half * 1024 + 1024], ACT.Exp,
                                     scale=tau[:, bass.ds(i - 1, 1)]).then_inc(s_be, 1)

            def keep_batch(i, half):
                for k in range(half * 2, half * 2 + 2):
                    keep_z(i, k)
                if i < 3:
                    next_batch(i, half)

            def state_table(i):
                state_sines(i)
                state_decay(i, 0)
                state_decay(i, 1)

            keep_batch(0, 0)
            keep_batch(0, 1)
            act.wait_ge(s_ct, 1)
            nc.scalar.activation(BR[:, 0:GROUPS * KLEN], BR[:, 0:GROUPS * KLEN], ACT.Sin, scale=TWO_PI).then_inc(s_cs, 1)
            keep_batch(1, 0)
            keep_batch(1, 1)
            act.wait_ge(s_rowl, 32)
            act.wait_ge(s_const, 4)
            state_table(1)
            keep_batch(2, 0)
            state_table(2)
            keep_batch(2, 1)
            state_table(3)
            keep_batch(3, 0)
            keep_batch(3, 1)
            act.wait_ge(s_xb, PAIRS)
            def silu_x(r):
                part = X[:, r * T_SLOTS * GH:(r + 1) * T_SLOTS * GH, :].rearrange("p c t -> p (c t)")
                nc.scalar.activation(part, part, ACT.Silu).then_inc(s_x, 1)

            silu_x(0)

            def group_input(r, k):
                g = r * 2 + k
                wait_past(act, s_tm, g - 1)
                nc.scalar.activation(XG[:, k, :, :], X[:, bass.ds(g * GH, GH), :], ACT.Copy).then_inc(s_xg, 1)

            def group_product(r, k):
                g = r * 2 + k
                act.wait_ge(s_tm, g + 1)
                wait_past(act, s_y, g - 1)
                nc.scalar.activation(YT[:, k, :], bank[k][:, 0:2 * P], ACT.Copy).then_inc(s_yt, 1)

            act.wait_ge(s_x, 1)
            act.wait_ge(s_be, LAGS * 2)
            for k in range(2):
                group_input(0, k)
            for r in range(1, GROUPS // T_SLOTS):
                silu_x(r)
            act.wait_ge(s_x, GROUPS // T_SLOTS)
            act.wait_ge(s_z, PAIRS)

            def gate_silu(r):
                part = Z[:, bass.ds(r * 2, 2), :].rearrange("p t c -> p (t c)")
                nc.scalar.activation(part, part, ACT.Silu).then_inc(s_zs, 1)

            def groups_and_gate(r):
                for k in range(2):
                    group_product(r, k)
                    group_input(r + 1, k)
                gate_silu(r)

            groups_and_gate(0)
            with act.Fori(1, GROUPS // 2 - 1) as r:
                groups_and_gate(r)
            for k in range(2):
                group_product(GROUPS // 2 - 1, k)
            gate_silu(GROUPS // 2 - 1)

            def copy_gated(r):
                for k in range(2):
                    act.wait_ge(s_tp, r * 4 + (k * 2 + 2))
                    wait_past(act, s_o, r * 4 + (k * 2 - 2))
                    nc.scalar.activation(GT[:, k * 2:k * 2 + 2, :].rearrange("p k c -> p (k c)"), bank[k][:, :], ACT.Copy)\
                      .then_inc(s_gt, 1)

            def deviation(r):
                act.wait_ge(s_mv, r + 1)
                nc.scalar.activation(sd[:, :], mv[:, :, 1], ACT.Sqrt, bias=epscol[:, :]).then_inc(s_sd, 1)

            def copy_x1(r):
                act.wait_ge(s_xp, r * 4 + 4)
                nc.scalar.activation(X1T.rearrange("p k c -> p (k c)"), bank[3][:, :], ACT.Copy).then_inc(s_x1t, 1)

            copy_gated(0)
            deviation(0)
            with act.Fori(1, TILES // 4) as r:
                copy_gated(r)
                copy_x1(r - 1)
                deviation(r)
            copy_x1(TILES // 4 - 1)

            def copy_slots(r, k):
                at = block_of(r, k, 0)
                if at:
                    n, slot, turn = at
                    act.wait_ge(s_ep, n + 1)
                    wait_past(act, s_up, n - 2)
                    nc.scalar.activation(XsT[:, slot, :], bank[6][:, 0:P], ACT.Copy).then_inc(s_ext, 1)

            def expert_deviation(r, k):
                at = block_of(r, k, 4)
                if at:
                    n, slot, turn = at
                    act.wait_ge(s_f4, n + 1)
                    nc.scalar.activation(esd[:, slot:slot + 1], emv[:, slot, 1:2], ACT.Sqrt, bias=epscol[:, :])\
                      .then_inc(s_f5, 1)

            def relu(r, k):
                at = block_of(r, k, 2)
                if at:
                    n, slot, turn = at
                    act.wait_ge(s_hp, n + 1)
                    wait_past(act, s_dn, n - 2)
                    nc.scalar.activation(HT[:, slot, :], bank[3 + slot][:, :], ACT.Relu).then_inc(s_ht, 1)

            def step(r, k):
                copy_slots(r, k)
                expert_deviation(r, k)
                relu(r, k)

            for r in range(2):
                for k in range(3):
                    step(r, k)
            with act.Fori(2, BLOCKS // 3) as r:
                for k in range(3):
                    step(r, k)
            for r in range(BLOCKS // 3, BLOCKS // 3 + 2):
                for k in range(3):
                    step(r, k)

        @block.vector
        def _(dve):
            steps = [0]

            def done(instruction):
                steps[0] += 1
                instruction.then_inc(s_vstep, 1)
                dve.wait_ge(s_vstep, steps[0])

            tt = nc.vector.tensor_tensor
            ts = nc.vector.tensor_scalar
            stt = nc.vector.scalar_tensor_tensor
            v = lambda i: sm[:, i, :]

            done(nc.vector.memset(phase[0:64, :], 0.25))
            done(nc.vector.memset(phase[64:128, :], 0.5))
            dve.wait_ge(s_win, 16)
            dve.wait_ge(s_cw, 32)
            tt(Wx[:, :, :], Win[:, 0:CHAN].unsqueeze(1).to_broadcast([P, TAPS, CHAN]), Wx[:, :, :], ALU.mult)\
              .then_inc(s_wx, 1)

            def bias(i, k):
                n = i * 4 + k
                dve.wait_ge(s_a, n + 1)
                b = bass.ds(i * 2 + k // 2, 1)
                tt(x_pairs[:, :, k % 2, :, b].rearrange("p c j b -> p j (c b)"),
                   bank[X_BANKS[k]][:, :].rearrange("p (j c) -> p j c", j=2),
                   cbias[:, :].unsqueeze(1).to_broadcast([P, 2, CHAN]), ALU.add).then_inc(s_xb, 1)

            def state_turns(i, step):
                lag = tau[:, bass.ds(i - 1, 1)]
                for half in range(2):
                    row = turns_row[:, half * 1024:half * 1024 + 1024]
                    part = Btab[:, bass.ds(i - 1, 1), :, half * 32:half * 32 + 32, :].rearrange("p m r n g -> p (m r) (n g)")
                    cosine, sine = part[:, 0, :], part[:, 1, :]
                    if step:
                        dve.wait_ge(s_bw, (i - 1) * 6 + ((step - 1) * 2 + half + 1))
                    if step == 0:
                        ts(cosine, row, lag, MAGIC, ALU.mult, ALU.add).then_inc(s_bw, 1)
                    elif step == 1:
                        ts(cosine, cosine, MAGIC, None, ALU.subtract).then_inc(s_bw, 1)
                    elif step == 2:
                        stt(sine, row, lag, cosine, ALU.mult, ALU.subtract).then_inc(s_bw, 1)
                    else:
                        stt(cosine, sine, -1.0, sine, ALU.mult, ALU.max).then_inc(s_bt, 1)

            dve.wait_ge(s_exp1, 1)
            dve.wait_ge(s_params, 16)
            done(stt(v(AR), v(DT), -1.0, v(EA), ALU.mult, ALU.mult))
            done(stt(v(AI), v(DT), TURN, prm[:, A_IM, :], ALU.mult, ALU.mult))
            nc.vector.tensor_copy(v(TURNS), v(AI)).then_inc(s_dec, 2)
            done(ts(smt[:, 1, :], v(AI), 0.5, None, ALU.mult))
            done(nc.vector.tensor_copy(smt[:, 0, :], v(AI)))
            done(ts(sm[:, T1:T1 + 2, :], smt[:, :, :], MAGIC, MAGIC, ALU.add, ALU.subtract))
            tt(smt[:, :, :], smt[:, :, :], sm[:, T1:T1 + 2, :], ALU.subtract).then_inc(s_ang, 1)
            dve.wait_ge(s_ang, 1)
            dve.wait_ge(s_tanh, 1)
            done(ts(v(T1), v(TH), -1.0, 1.0, ALU.mult, ALU.add))
            done(nc.vector.reciprocal(v(T2), v(T1)))
            done(stt(v(EM1), v(TH), 2.0, v(T2), ALU.mult, ALU.mult))
            done(ts(v(ER), v(EM1), 1.0, None, ALU.add))
            dve.wait_ge(s_sin1, 1)
            done(stt(v(CM1), smt[:, 1, :], -2.0, smt[:, 1, :], ALU.mult, ALU.mult))
            done(stt(v(T1), v(CM1), 1.0, v(EM1), ALU.add, ALU.mult))
            done(tt(v(WR), v(T1), v(CM1), ALU.add))
            done(tt(v(WI), v(ER), smt[:, 0, :], ALU.mult))
            done(tt(v(T1), prm[:, C_RE, :], v(WR), ALU.mult))
            done(tt(v(T2), prm[:, C_IM, :], v(WI), ALU.mult))
            done(tt(v(T1), v(T1), v(T2), ALU.subtract))
            done(tt(v(T2), prm[:, C_RE, :], v(WI), ALU.mult))
            done(tt(v(T3), prm[:, C_IM, :], v(WR), ALU.mult))
            done(tt(v(T2), v(T2), v(T3), ALU.add))
            done(tt(v(T3), v(T2), prm[:, A_IM, :], ALU.mult))
            done(tt(v(PP), v(T1), v(EA), ALU.mult))
            done(tt(v(PP), v(T3), v(PP), ALU.subtract))
            done(tt(v(T3), v(T2), v(EA), ALU.mult))
            done(tt(v(QQ), v(T1), prm[:, A_IM, :], ALU.mult))
            done(stt(v(QQ), v(T3), -1.0, v(QQ), ALU.mult, ALU.subtract))
            done(stt(v(AXX), v(PP), -1.0, v(PP), ALU.mult, ALU.max))
            done(stt(v(AYY), v(QQ), -1.0, v(QQ), ALU.mult, ALU.max))
            done(tt(v(MX), v(AXX), v(AYY), ALU.max))
            done(tt(v(T1), v(AXX), v(AYY), ALU.min))
            done(ts(v(T2), v(MX), 1e-35, None, ALU.max))
            done(nc.vector.reciprocal(v(T3), v(T2)))
            done(tt(v(RAT), v(T1), v(T3), ALU.mult))
            done(tt(v(T1), v(RAT), v(RAT), ALU.mult))
            ts(v(T3), v(T1), 1.0, None, ALU.add).then_inc(s_rat, 1)
            dve.wait_ge(s_rat, 1)
            bias(0, 0)
            done(tt(v(T1), v(EA), v(EA), ALU.mult))
            done(tt(v(T2), prm[:, A_IM, :], prm[:, A_IM, :], ALU.mult))
            done(tt(v(T1), v(T1), v(T2), ALU.add))
            done(nc.vector.reciprocal(v(DEN), v(T1)))
            done(stt(v(DEN), v(DEN), 2.0, v(MX), ALU.mult, ALU.mult))
            bias(0, 1)
            dve.wait_ge(s_atan, 1)
            done(ts(v(PHI), v(PHI), TURN, None, ALU.mult))

            def reflect(condition, about):
                done(ts(v(T2), v(PHI), -2.0, about, ALU.mult, ALU.add))
                done(tt(v(T2), v(T2), v(T1), ALU.mult))
                done(tt(v(PHI), v(PHI), v(T2), ALU.add))

            done(tt(v(T1), v(AYY), v(AXX), ALU.is_gt))
            reflect(T1, 0.25)
            done(ts(v(T1), v(PP), 0.0, None, ALU.is_lt))
            reflect(T1, 0.5)
            done(ts(v(T1), v(QQ), 0.0, None, ALU.is_lt))
            reflect(T1, 0.0)
            dve.wait_ge(s_const, 2)
            done(ts(v(PHI), v(PHI), phase[:, :], None, ALU.add))
            dve.wait_ge(s_hyp, 1)
            done(tt(v(AMP), v(T4), v(DEN), ALU.mult))
            dve.wait_ge(s_sel0, 1)
            for j in range(2):
                at = bass.AP(TR[:, :].tensor, j * 16 * P, [[T_SLOTS * GH * CHUNK, P], [P + GH, 16], [1, GH]])
                last = tt(at, v(AMP)[:, j * 16:j * 16 + 16].unsqueeze(2).to_broadcast([P, 16, GH]),
                          mask16[:, 0:GH].unsqueeze(1).to_broadcast([P, 16, GH]), ALU.mult)
            last.then_inc(s_sel, 1)

            bias(0, 2)
            dve.wait_ge(s_cg, 1)
            done(tt(turnsC, turnsC, v(PHI).unsqueeze(2).to_broadcast([P, GROUPS, KLEN]), ALU.add))
            done(ts(wholeC, turnsC, MAGIC, MAGIC, ALU.add, ALU.subtract))
            bias(0, 3)
            tt(turnsC, turnsC, wholeC, ALU.subtract).then_inc(s_ct, 1)
            bias(1, 0)
            dve.wait_ge(s_rowl, 32)
            dve.wait_ge(s_ce, 1)
            dve.wait_ge(s_cs, 1)
            tt(Ctab, Ctab, turnsC, ALU.mult).then_inc(s_c, 1)
            dve.wait_ge(s_c, 1)
            state_turns(1, 0)
            for k in range(1, 4):
                bias(1, k)
                state_turns(1, k)

            dve.wait_ge(s_const, 3)
            dve.wait_ge(s_late, 64)
            dve.wait_ge(s_kp, 1)
            for j in range(2):
                nc.vector.tensor_copy(Kx[:, j, CHUNK - 1:KROW - 1], bank[4 + j][:, 0:CHUNK]).then_inc(s_kx, 1)
            dve.wait_ge(s_kx, 2)
            tt(Kx[:, :, CHUNK - 1], Kx[:, :, CHUNK - 1], dskip[:, :], ALU.add).then_inc(s_kx, 1)

            for k in range(4):
                bias(2, k)
                for j in range(2):
                    state_turns(2 + k // 2, k % 2 * 2 + j)
            for k in range(4):
                bias(3, k)
            for half in range(2):
                dve.wait_ge(s_bs, LAGS * 2)
                dve.wait_ge(s_be, LAGS * 2 - 1 + half)
                part = Btab[:, LAGS - 1, 1, half * 32:half * 32 + 32, :].rearrange("p n g -> p (n g)")
                tt(part, part, decay[:, half, :], ALU.mult).then_inc(s_b3, 1)

            def states(r, k):
                g = r * 2 + k
                dve.wait_ge(s_s, g + 1)
                wait_past(dve, s_y, g - 1)
                stt(V[:, k, :, :], bank[6 + k][:, 0:GH * SCOLS].rearrange("p (h c) -> p h c", h=GH),
                    sm[:, AMP, bass.ds(g, 1)], mask8[:, :].unsqueeze(2).to_broadcast([P, GH, SCOLS]), ALU.mult, ALU.mult)\
                    .then_inc(s_v, 1)

            def output(r, k):
                g = r * 2 + k
                group = X[:, bass.ds(g * GH, GH), :]
                product = bank[4 + k][:, 0:GH * TILES].rearrange("p (h t) -> p h t", h=GH)
                from_states = bank[4 + k][:, GH * TILES:GH * (TILES + SCOLS)].rearrange("p (h c) -> p h c", h=GH)
                dve.wait_ge(s_y, g + 1)
                nc.vector.tensor_copy(group, product).then_inc(s_yd, 1)
                dve.wait_ge(s_yd, g + 1)
                tt(group[:, :, BATCH:], group[:, :, BATCH:], from_states, ALU.add).then_inc(s_yc, 1)

            dve.wait_ge(s_a, PAIRS)
            states(0, 0)
            states(0, 1)
            output(0, 0)
            with dve.Fori(1, GROUPS // 2) as r:
                states(r, 0)
                output(r - 1, 1)
                states(r, 1)
                output(r, 0)
            output(GROUPS // 2 - 1, 1)

            def norm(r):
                dve.wait_ge(s_o, r * 4 + 4)
                for k in range(4):
                    dve.wait_ge(s_hr[k], (r + 1) * 16)
                wait_past(dve, s_x1, r * 4)
                tt(R.rearrange("p k c -> p (k c)"), bank[2][:, :], HR.rearrange("p k c -> p (k c)"), ALU.add).then_inc(s_r, 1)
                dve.wait_ge(s_r, r + 1)
                for k in range(4):
                    last = nc.vector.bn_stats(st[:, k, :], R[:, k, :])
                last.then_inc(s_st, 1)
                wait_apart(dve, s_st, r + 1)
                for k in range(4):
                    last = nc.vector.bn_aggr(mv[:, k, :], st[:, k, :])
                last.then_inc(s_mv, 1)
                dve.wait_ge(s_sd, r + 1)
                nc.vector.reciprocal(rs[:, :], sd[:, :]).then_inc(s_rs, 1)
                dve.wait_ge(s_rs, r + 1)
                wait_past(dve, s_xp, r * 4)
                wait_past(dve, s_x1c, r)
                for k in range(4):
                    ts(N4[:, k, :], R[:, k, :], mv[:, k, 0:1], rs[:, k:k + 1], ALU.subtract, ALU.mult).then_inc(s_x1, 1)

            def choose(r):
                dve.wait_ge(s_lp, r + 1)
                wait_past(dve, s_idx, r)
                tt(LG[:, :, :], bank[4][:, 0:32].rearrange("p (k e) -> p k e", k=4),
                   gbias[:, 0, :].unsqueeze(1).to_broadcast([P, 4, EXPERTS]), ALU.add).then_inc(s_lg, 1)
                dve.wait_ge(s_lg, r * 2 + 1)
                tt(LG[:, :, :], LG[:, :, :], gbias[:, 1, :].unsqueeze(1).to_broadcast([P, 4, EXPERTS]), ALU.add)\
                  .then_inc(s_lg, 1)
                wait_apart(dve, s_lg, r * 2 + 2)
                for k in range(4):
                    last = nc.vector.max(top[:, k, :], LG[:, k, :])
                last.then_inc(s_top, 1)
                wait_apart(dve, s_top, r + 1)
                for k in range(4):
                    last = nc.vector.max_index(IDX[:, k, :], top[:, k, :], LG[:, k, :])
                last.then_inc(s_ix, 1)
                dve.wait_ge(s_ix, r + 1)
                nc.vector.tensor_copy(idxf[:, bass.ds(r * 4, 4)], IDX[:, :, 0]).then_inc(s_idx, 1)

            norm(0)
            with dve.Fori(1, TILES // 4) as r:
                norm(r)
                choose(r - 1)
            choose(TILES // 4 - 1)

            dve.wait_ge(s_idx, TILES // 4)
            dve.wait_ge(s_rconst, 2)
            shape = [P, EXPERTS, TILES]
            tt(OH[:, :, :], idxf[:, :].unsqueeze(1).to_broadcast(shape), erow[:, :].unsqueeze(2).to_broadcast(shape),
               ALU.is_equal).then_inc(s_oh, 1)
            dve.wait_ge(s_cp, 1)
            totals = bank[6][:, 0:256]
            flat = lambda a: a[:, :, :].rearrange("p e j -> p (e j)")
            c = lambda i: cnt[:, i, :]
            done(nc.vector.tensor_tensor_scan(flat(run), ones[:, 0:1].to_broadcast([P, EXPERTS * TILES]), totals, 0.0,
                                              ALU.mult, ALU.add))
            done(tt(flat(rt), flat(run), totals, ALU.subtract))
            done(tt(c(0), run[:, :, TILES - 1], rt[:, :, 0], ALU.subtract))
            done(ts(c(1), c(0), 1.0 / P, (P - 1.0) / P - 0.5 + 0.5 / P, ALU.mult, ALU.add))
            done(ts(c(1), c(1), MAGIC, MAGIC, ALU.add, ALU.subtract))
            done(nc.vector.tensor_tensor_scan(c(2), ones[:, 0:1].to_broadcast([P, EXPERTS]), c(1), 0.0, ALU.mult, ALU.add))
            done(tt(c(3), c(2), c(1), ALU.subtract))
            done(stt(c(4), c(3), float(P), rt[:, :, 0], ALU.mult, ALU.subtract))
            done(tt(flat(rt), flat(rt), bank[5][:, 0:256], ALU.add))
            done(tt(rt[:, :, :], rt[:, :, :], c(4).unsqueeze(2).to_broadcast(shape), ALU.add))
            done(tt(flat(rt), flat(rt), flat(OH), ALU.mult))
            done(nc.vector.tensor_reduce(posf[:, :], rt[:, :, :].rearrange("p e j -> p j e"), AX.X, ALU.add))
            nc.vector.tensor_copy(pos[:, :], posf[:, :]).then_inc(s_pos, 1)
            shape = [P, BLOCKS + 1, EXPERTS]
            done(tt(bcmp[:, :, :], c(2).unsqueeze(1).to_broadcast(shape), brow[:, :].unsqueeze(2).to_broadcast(shape),
                    ALU.is_le))
            done(nc.vector.tensor_reduce(bexpf[:, :], bcmp[:, :, :], AX.X, ALU.add))
            done(ts(bexpf[:, :], bexpf[:, :], EXPERTS - 1.0, None, ALU.min))
            nc.vector.tensor_copy(bexp[:, :], bexpf[:, :]).then_inc(s_be2, 1)

            dve.wait_ge(s_ew, 64)
            dve.wait_ge(s_be2, 1)

            def bias_hidden(r, k):
                at = block_of(r, k, 1)
                if at:
                    n, slot, turn = at
                    e = dve.value_load(bexp[0:1, bass.ds(n, 1)], min_val=0, max_val=EXPERTS - 1)
                    dve.wait_ge(s_up, n + 1)
                    wait_past(dve, s_hp, n - 2)
                    tt(Hs[:, slot, :], bank[slot][:, :], B1[:, bass.ds(e, 1), :].rearrange("p e f -> p (e f)"), ALU.add)\
                      .then_inc(s_h, 1)

            def normalize(r, k):
                at = block_of(r, k, 4)
                if at:
                    n, slot, turn = at
                    dve.wait_ge(s_f5, n + 1)
                    nc.vector.reciprocal(ers[:, slot:slot + 1], esd[:, slot:slot + 1]).then_inc(s_f6, 1)
                    dve.wait_ge(s_f6, n + 1)
                    ts(F[:, slot, :], F[:, slot, :], emv[:, slot, 0:1], ers[:, slot:slot + 1], ALU.subtract, ALU.mult)\
                      .then_inc(s_f7, 1)

            def residual(r, k):
                at = block_of(r, k, 3)
                if at:
                    n, slot, turn = at
                    dve.wait_ge(s_dn, n + 1)
                    dve.wait_ge(s_xb2, n + 1)
                    if not isinstance(turn, int) or turn > 0:
                        dve.wait_ge(s_out[slot], turn * 16)
                    tt(F[:, slot, :], bank[7][:, 0:P], O[:, slot, :], ALU.add).then_inc(s_f1, 1)
                    dve.wait_ge(s_f1, n + 1)
                    nc.vector.bn_stats(est[:, slot, :], F[:, slot, :]).then_inc(s_f3, 1)
                    wait_apart(dve, s_f3, n + 1)
                    nc.vector.bn_aggr(emv[:, slot, :], est[:, slot, :]).then_inc(s_f4, 1)

            def step(r, k):
                bias_hidden(r, k)
                normalize(r, k)
                residual(r, k)

            for r in range(2):
                for k in range(3):
                    step(r, k)
            with dve.Fori(2, BLOCKS // 3) as r:
                for k in range(3):
                    step(r, k)
            for r in range(BLOCKS // 3, BLOCKS // 3 + 2):
                for k in range(3):
                    step(r, k)

        @block.tensor
        def _(pe):
            mm = nc.tensor.matmul

            def project(i, k):
                n = i * 4 + k
                slot = k // 2
                if k % 2 == 0:
                    pe.wait_ge(s_xt[slot], (i + 1) * 32)
                wait_past(pe, s_xb, n - 3)
                wait_past(pe, s_z, n - 3)
                if k >= 2 and not isinstance(i, int):
                    pe.wait_ge(s_kx, 2)
                for j in range(2):
                    chunk = k % 2 * 2 + j
                    for tap in range(TAPS):
                        at = (CHUNKS - 1 - chunk) * CHUNK + TAPS - 1 - tap
                        mm(bank[X_BANKS[k]][:, j * CHAN:(j + 1) * CHAN], XR[:, slot, at:at + CHUNK], Wx[:, tap, :],
                           start=(tap == 0), stop=(tap == TAPS - 1))
                    at = chunk * CHUNK
                    last = mm(bank[Z_BANKS[k]][:, j * CHAN:(j + 1) * CHAN], XT[:, slot, at:at + CHUNK], Win[:, CHAN:],
                              start=True, stop=True)
                last.then_inc(s_a, 1)

            pe.wait_ge(s_wx, 1)
            pe.wait_ge(s_pad, 1)
            for i in range(2):
                for k in range(4):
                    project(i, k)
            pe.wait_ge(s_xb, 8)
            pe.wait_ge(s_sel, 1)
            pe.wait_ge(s_c, 1)
            for g in range(GROUPS):
                last = mm(bank[4 + g // 16][:, 0:CHUNK], Sel[:, g, :], Ctab[:, g, 0:CHUNK], start=(g % 16 == 0),
                          stop=(g % 16 == 15))
            last.then_inc(s_kp, 1)
            with pe.Fori(2, 4) as i:
                for k in range(4):
                    project(i, k)

            def mix(r, k):
                g = r * T_SLOTS + k
                s, yt = bank[6 + k % 2], bank[k % 2]
                xg = XG[:, k % 2, :, :]
                out_s = s[:, 0:GH * SCOLS].rearrange("p (h c) -> p h c", h=GH)
                pe.wait_ge(s_xg, g + 1)
                pe.wait_ge(s_bc, g + 1)
                wait_past(pe, s_v, g - 1)
                for lag in range(LAGS):
                    cols = SCOLS - lag * BATCH
                    last = mm(out_s[:, :, lag * BATCH:], BC[:, k % 2, lag, :], xg[:, :, 0:cols], start=(lag == 0),
                              stop=(lag == LAGS - 1))
                last.then_inc(s_s, 1)
                pe.wait_ge(s_t[k], (r + 1) * 16)
                wait_past(pe, s_yt, g - 1)
                for h in range(GH):
                    at, part = h // 4 * P, h % 4 * TILES
                    last = mm(yt[part:part + TILES, at:at + P], xg[:, h, :], Tring[:, k, h, :], start=True, stop=True)
                last.then_inc(s_tm, 1)

            def finish(r, k):
                g, slot = r * T_SLOTS + k, k % 2
                y = bank[4 + slot]
                pe.wait_ge(s_yt, g + 1)
                wait_past(pe, s_yc, g - 1)
                for j in range(2):
                    nc.tensor.transpose(y[:, j * P:(j + 1) * P], YT[:, slot, j * P:(j + 1) * P], ident[:, :])
                pe.wait_ge(s_v, g + 1)
                pe.wait_ge(s_cc, g + 1)
                mm(y[:, GH * TILES:GH * (TILES + SCOLS)], BC[:, slot, LAGS, :],
                   V[:, slot, :, :].rearrange("p h c -> p (h c)"), start=True, stop=True).then_inc(s_y, 1)

            pe.wait_ge(s_z, PAIRS)
            pe.wait_ge(s_kx, 2)
            pe.wait_ge(s_const, 4)
            mix(0, 0)
            for k in range(1, T_SLOTS):
                mix(0, k)
                finish(0, k - 1)
            with pe.Fori(1, GROUPS // T_SLOTS) as r:
                for k in range(T_SLOTS):
                    mix(r, k)
                    finish(r, k - 1)
            finish(GROUPS // T_SLOTS - 1, T_SLOTS - 1)

            pe.wait_ge(s_const, 4)
            pe.wait_ge(s_late, 64)

            def output_projection(r):
                for k in range(4):
                    pe.wait_ge(s_g, r * 4 + (k + 1))
                    wait_past(pe, s_gt, r * 2 + (k // 2 - 1))
                    for j in range(2):
                        at = (k % 2) * 256 + j * P
                        last = nc.tensor.transpose(bank[k // 2][:, at:at + P], G[:, k, j * P:j * P + P], ident[:, :])
                    last.then_inc(s_tp, 1)
                wait_past(pe, s_r, r)
                if isinstance(r, int):
                    pe.wait_ge(s_wo, 16)
                for k in range(4):
                    pe.wait_ge(s_gt, r * 2 + (k // 2 + 1))
                    for j in range(2):
                        last = mm(bank[2][:, k * DM:k * DM + DM], GT[:, k, j * P:j * P + P], WoT[:, j, :],
                                  start=(j == 0), stop=(j == 1))
                    last.then_inc(s_o, 1)

            def logits(r):
                wait_past(pe, s_x1t, r)
                for k in range(4):
                    pe.wait_ge(s_x1, r * 4 + (k + 1))
                    nc.tensor.transpose(bank[3][:, k * P:k * P + P], N4[:, k, :], ident[:, :]).then_inc(s_xp, 1)
                pe.wait_ge(s_x1t, r + 1)
                wait_past(pe, s_lg, r * 2)
                for k in range(4):
                    last = mm(bank[4][:, k * EXPERTS:(k + 1) * EXPERTS], X1T[:, k, :], gwT[:, :], start=True, stop=True)
                last.then_inc(s_lp, 1)

            output_projection(0)
            with pe.Fori(1, TILES // 4) as r:
                output_projection(r)
                logits(r - 1)
            logits(TILES // 4 - 1)

            pe.wait_ge(s_oh, 1)
            pe.wait_ge(s_rconst, 2)
            onehot = OH[:, :, :].rearrange("p e j -> p (e j)")
            mm(bank[5][:, 0:256], before[:, :], onehot, start=True, stop=True)
            mm(bank[6][:, 0:256], ones[:, :], onehot, start=True, stop=True).then_inc(s_cp, 1)

            pe.wait_ge(s_ew, 64)
            pe.wait_ge(s_be2, 1)

            def transpose_slots(r, k):
                at = block_of(r, k, 0)
                if at:
                    n, slot, turn = at
                    pe.wait_ge(s_xs[slot], (turn + 1) * 16)
                    wait_past(pe, s_ext, n)
                    nc.tensor.transpose(bank[6][:, 0:P], XS[:, slot, 0:DM], ident[:, :]).then_inc(s_ep, 1)

            def up(r, k):
                at = block_of(r, k, 1)
                if at:
                    n, slot, turn = at
                    e = pe.value_load(bexp[0:1, bass.ds(n, 1)], min_val=0, max_val=EXPERTS - 1)
                    pe.wait_ge(s_ext, n + 1)
                    wait_past(pe, s_h, n - 2)
                    mm(bank[slot][:, :], XsT[:, slot, :], W1[:, bass.ds(e, 1), :].rearrange("p e f -> p (e f)"),
                       start=True, stop=True).then_inc(s_up, 1)

            def transpose_hidden(r, k):
                at = block_of(r, k, 2)
                if at:
                    n, slot, turn = at
                    pe.wait_ge(s_h, n + 1)
                    wait_past(pe, s_ht, n - 2)
                    for c in range(FCH):
                        last = nc.tensor.transpose(bank[3 + slot][:, c * P:c * P + P], Hs[:, slot, c * P:c * P + P],
                                                   ident[:, :])
                    last.then_inc(s_hp, 1)

            def down(r, k):
                at = block_of(r, k, 3)
                if at:
                    n, slot, turn = at
                    e = pe.value_load(bexp[0:1, bass.ds(n, 1)], min_val=0, max_val=EXPERTS - 1)
                    pe.wait_ge(s_ht, n + 1)
                    wait_past(pe, s_f1, n)
                    for c in range(FCH):
                        last = mm(bank[7][:, 0:P], HT[:, slot, c * P:c * P + P],
                                  W2[:, bass.ds(e, 1), c * DM:(c + 1) * DM].rearrange("p e d -> p (e d)"),
                                  start=(c == 0), stop=(c == FCH - 1))
                    last.then_inc(s_dn, 1)

            def step(r, k):
                transpose_slots(r, k)
                up(r, k)
                transpose_hidden(r, k)
                down(r, k)

            for r in range(2):
                for k in range(3):
                    step(r, k)
            with pe.Fori(2, BLOCKS // 3) as r:
                for k in range(3):
                    step(r, k)
            for k in range(3):
                step(BLOCKS // 3, k)


_ORDER = ("hidden", "hidden_t", "hidden_r", "w_in_t", "conv_w", "conv_b", "states", "d_skip",
          "w_out_t", "gate_w_t", "gate_b", "expert_bias", "w1", "b1", "w2", "b2")


def kernel(**inputs):
    import numpy as _np
    import concourse.bacc as _bacc
    from concourse import mybir as _mybir
    from concourse.bass_utils import run_bass_kernel_spmd as _run

    a = {name: _np.asarray(value) for name, value in inputs.items()}

    def by_group(x):
        return x.reshape((GH, GROUPS) + x.shape[1:]).swapaxes(0, 1).reshape(x.shape)

    def by_state(x):
        x = x.reshape(GH, GROUPS, STATES).transpose(0, 2, 1).reshape(GH * STATES, GROUPS)
        return _np.concatenate([x, x])

    hidden = a["L0_attn_hidden_states"]
    w_in = a["L0_attn_W_in"]
    laid = {
        "hidden": hidden,
        "hidden_t": hidden.transpose(2, 0, 1),
        "hidden_r": hidden[:, ::-1].transpose(2, 0, 1),
        "w_in_t": _np.concatenate([by_group(w_in[:CHAN]), by_group(w_in[CHAN:])]).T,
        "conv_w": by_group(a["L0_attn_conv_w"]).T,
        "conv_b": by_group(a["L0_attn_conv_b"])[None],
        "states": _np.stack([by_state(x) for x in (
            _np.broadcast_to(a["L0_attn_log_dt"][:, None], (CHAN, STATES)), a["L0_attn_log_A_real"],
            a["L0_attn_A_imag"], a["L0_attn_C_re"], a["L0_attn_C_im"])], axis=1),
        "d_skip": by_group(a["L0_attn_D"]).reshape(2, P).T,
        "w_out_t": by_group(a["L0_attn_W_out"].T),
        "gate_w_t": a["L0_ffn_gate_w"].T,
        "gate_b": a["L0_ffn_gate_b"][None],
        "expert_bias": a["L0_ffn_expert_bias"][None],
        "w1": a["L0_ffn_w1"],
        "b1": a["L0_ffn_b1"],
        "w2": a["L0_ffn_w2"],
        "b2": a["L0_ffn_b2"],
    }
    nc = _bacc.Bacc("TRN2", target_bir_lowering=False, num_devices=1)
    arrays, args = {}, []
    for name in _ORDER:
        x = _np.ascontiguousarray(laid[name])
        arrays[name] = x
        args.append(nc.dram_tensor(name, x.shape, _mybir.dt.from_np(x.dtype), kind="ExternalInput").ap())
    args.append(nc.dram_tensor("out", (BATCH, SEQ, DM), F32, kind="ExternalOutput").ap())
    build(nc, *args)
    result = _run(nc, [arrays], core_ids=[0])
    return result.results[0]["out"]
```

```python
import math
from contextlib import ExitStack

import numpy as np
import concourse.bass as bass
from concourse import mybir

F32 = mybir.dt.float32
I32 = mybir.dt.int32
U32 = mybir.dt.uint32
ALU = mybir.AluOpType
ACT = mybir.ActivationFunctionType
AX = mybir.AxisListType

P = 128
BATCH, SEQ, DM = 8, 512, 128
CHAN, STATES, TAPS = 256, 8, 4
EXPERTS, DFF = 8, 512
TOKENS = BATCH * SEQ
CHUNK = P
CHUNKS = SEQ // CHUNK
TILES = TOKENS // P
PAIRS = TILES // 2
GH = 8
GROUPS = CHAN // GH
LAGS = CHUNKS - 1
SCOLS = LAGS * BATCH
KLEN = CHUNK + 1
KROW = 2 * CHUNK
BLOCKS = TILES + EXPERTS - 1
REGION = TOKENS + P
QUADS = TILES // 4
ROW = DM + 4
TOKEN_COL = DM
NO_TOKEN = float(1 << 17)
FCH = DFF // P
EPS = 1e-5
MAGIC = float(1.5 * 2 ** 23)
TWO_PI = 6.2831850
QUARTER = float(math.pi / 2)
TURN = float(1.0 / (2.0 * math.pi))

T_SLOTS = 8
LAG_ORDER = (3, 1, 2)
X_BANKS, Z_BANKS = (0, 1, 4, 5), (2, 3, 6, 7)
A_BATCH = 2


def wait_past(engine, semaphore, count):
    if not isinstance(count, int) or count > 0:
        engine.wait_ge(semaphore, count)


def wait_apart(engine, semaphore, count):
    if not isinstance(count, int) or count > 0:
        engine.wait_ge(semaphore, count)
        engine.nop(nofuse=True)


def build(nc, hidden, hidden_t, hidden_r, w_in_t, conv_w, conv_b, states, d_skip, w_out_t, gate_w_t,
          gate_b, expert_bias, w1, b1, w2, b2, out):
    kext = nc.dram_tensor("kernel_rows", [CHAN, KROW], F32).ap()
    rows_dram = nc.dram_tensor("decay_and_turns", [2, GH * STATES * GROUPS], F32).ap()
    toeplitz = bass.AP(kext.tensor, 0, [[1, P], [KROW, CHAN], [1, CHUNK]])
    spare = BLOCKS - TILES
    slots_dram = nc.dram_tensor("dispatched_rows", [EXPERTS * REGION + spare * P, ROW], F32).ap()
    out_rows = out.rearrange("b l d -> (b l) d")
    hidden_rows = hidden.rearrange("b l d -> (b l) d")

    ctx = ExitStack()
    with ctx:
        def sb(name, shape, dt=F32):
            return ctx.enter_context(nc.sbuf_tensor(name, shape, dt))

        def sem(name):
            return ctx.enter_context(nc.semaphore(name))

        bank = [ctx.enter_context(nc.psum_tensor(f"bank{i}", [P, 512], F32)) for i in range(8)]

        X = sb("X", [P, CHAN, TILES])
        Z = sb("Z", [P, TILES, CHAN])
        BR = sb("BR", [P, 3 * 4096])
        CR = sb("CR", [P, GROUPS * KLEN])
        TR = sb("TR", [P, T_SLOTS * GH * CHUNK])
        RW = sb("RW", [P, 4096])
        EN = sb("EN", [P, 3840])

        Btab = BR[:, :].rearrange("p (m r n g) -> p m r n g", m=3, r=2, g=GROUPS)
        Ctab = CR[:, :].rearrange("p (g j) -> p g j", g=GROUPS)
        turnsC = BR[:, 0:GROUPS * KLEN].rearrange("p (g j) -> p g j", g=GROUPS)
        wholeC = BR[:, GROUPS * KLEN:2 * GROUPS * KLEN].rearrange("p (g j) -> p g j", g=GROUPS)
        Tring = TR[:, :].rearrange("p (s h u) -> p s h u", s=T_SLOTS, h=GH)
        Sel = TR[:, 0:4096].rearrange("p (g c) -> p g c", g=GROUPS)
        decay_row = RW[:, 0:2048]
        turns_row = RW[:, 2048:4096]
        decay = EN[:, 0:2048].rearrange("p (s c) -> p s c", s=2)

        XT = sb("XT", [P, A_BATCH, SEQ])
        XR = EN[:, 2688:2688 + A_BATCH * (SEQ + TAPS - 1)].rearrange("p (k c) -> p k c", k=A_BATCH)
        Win = sb("Win", [P, 2 * CHAN])
        Wx = sb("Wx", [P, TAPS, CHAN])
        cbias = sb("cbias", [P, CHAN])
        BC = Wx[:, :, :].rearrange("p t c -> p (t c)").rearrange("p (k m c) -> p k m c", k=2, m=4)
        V = XT[:, :, 0:GH * SCOLS].rearrange("p k (h c) -> p k h c", h=GH)
        prm = sb("prm", [P, 5, GROUPS])
        sm = sb("sm", [P, 24, GROUPS])
        smt = EN[:, 2560:2560 + 2 * GROUPS].rearrange("p (i g) -> p i g", i=2)
        quarter = sb("quarter", [P, 1])
        tau = sb("tau", [P, LAGS])
        jrow = sb("jrow", [P, KLEN])
        phase = sb("phase", [P, 1])
        epscol = sb("epscol", [P, 1])
        mask16 = sb("mask16", [P, 2 * GH])
        mask8 = sb("mask8", [P, GH])
        Kx = TR[:, 4096:4096 + 2 * KROW].rearrange("p (j c) -> p j c", j=2)
        dskip = sb("dskip", [P, 2])
        ident = sb("ident", [P, P])
        LATE = 2048 + 384
        before = CR[:, LATE:LATE + P]
        ones = CR[:, LATE + P:LATE + 2 * P]
        WoT = CR[:, LATE + 256:LATE + 512].rearrange("p (j d) -> p j d", j=2)
        gwT = sb("gwT", [P, EXPERTS])
        gbias = sb("gbias", [P, 2, EXPERTS])

        XG = RW[:, 0:512].rearrange("p (k h t) -> p k h t", k=2, h=GH)
        YT = RW[:, 512:1024].rearrange("p (k c) -> p k c", k=2)

        G = RW[:, 0:1024].rearrange("p (k c) -> p k c", k=4)
        GT = RW[:, 1024:2048].rearrange("p (k c) -> p k c", k=4)
        HR = RW[:, 2048:2560].rearrange("p (k c) -> p k c", k=4)
        X1T = RW[:, 2560:3072].rearrange("p (k c) -> p k c", k=4)
        R = RW[:, 3072:4096].rearrange("p (s k c) -> p s k c", s=2, k=4)
        X1 = TR[:, 0:16 * ROW].rearrange("p (s k c) -> p s k c", s=4, k=4)
        empty_row = TR[:, 16 * ROW:17 * ROW]
        st = sb("st", [P, 4, 6])
        mv = sb("mv", [P, 4, 2])
        sd = sb("sd", [P, 4])
        rs = sb("rs", [P, 2, 2, 4])
        LG = sb("LG", [P, 4, EXPERTS])
        top = sb("top", [P, 4, 8])
        IDX = CR[:, LATE + 512:LATE + 544].bitcast(U32).rearrange("p (j c) -> p j c", c=8)

        def late(at, shape, dt=F32):
            view = CR[:, LATE + 768 + at:LATE + 768 + at + shape]
            return view if dt == F32 else view.bitcast(dt)

        tokf = late(0, TILES)
        pos = late(80, 16, U32).rearrange("p (s k) -> p s k", s=4)
        posf = late(44, 4)
        tail = late(48, EXPERTS, I32)
        ebase = late(56, EXPERTS)
        free_row = late(64, EXPERTS)
        total = late(72, EXPERTS)
        brow = late(96, BLOCKS + 1)
        bexpf = late(136, BLOCKS + 1)
        bexp = late(176, BLOCKS + 1, I32)
        tok = late(216, 6, U32)
        cnt = late(224, 4 * EXPERTS).rearrange("p (i e) -> p i e", e=EXPERTS)
        erow = late(256, EXPERTS)
        bstart = late(264, BLOCKS + 1)
        first_row = late(304, BLOCKS + 1, I32)
        OH = EN[:, 0:32].rearrange("p (k e) -> p k e", e=EXPERTS)
        place = EN[:, 32:64].rearrange("p (k e) -> p k e", e=EXPERTS)
        bcmp = EN[:, 768:768 + (BLOCKS + 1) * EXPERTS].rearrange("p (b e) -> p b e", e=EXPERTS)

        W1 = BR[:, 0:4096].rearrange("p (e f) -> p e f", e=EXPERTS)
        W2 = BR[:, 4096:8192].rearrange("p (e q) -> p e q", e=EXPERTS)
        B1 = BR[:, 8192:8192 + EXPERTS * FCH]
        B2 = CR[:, 0:1024].rearrange("p (e d) -> p e d", e=EXPERTS)
        XS = CR[:, 1024:1024 + 3 * ROW].rearrange("p (s c) -> p s c", s=3)
        O = CR[:, 2048:2048 + 384].rearrange("p (s c) -> p s c", s=3)
        WS = EN[:, 0:1536].rearrange("p (s c) -> p s c", s=3)
        HT = EN[:, 1536:3072].rearrange("p (s c) -> p s c", s=3)
        XsT = EN[:, 3072:3456].rearrange("p (s c) -> p s c", s=3)
        F = EN[:, 3456:3840].rearrange("p (s c) -> p s c", s=3)
        est = sb("est", [P, 3, 6])
        emv = sb("emv", [P, 3, 2])
        esd = sb("esd", [P, 3])
        ers = sb("ers", [P, 3])

        x_pairs = X[:, :, :].rearrange("p c (h j b) -> p c h j b", h=2, b=BATCH)
        z_pairs = Z[:, :, :].rearrange("p (h j b) c -> p h j b c", h=2, b=BATCH)

        s_params = sem("params_loaded")
        s_win = sem("w_in_loaded")
        s_cw = sem("conv_loaded")
        s_late = sem("late_weights_loaded")
        s_xt = [sem(f"batch_loaded{k}") for k in range(A_BATCH)]
        s_pad = sem("padding_zeroed")
        s_wo = sem("output_weights_loaded")
        s_wx = sem("conv_weights_ready")
        s_const = sem("constants_ready")
        s_pstep = sem("pool_step")
        s_vstep = sem("vector_step")
        s_exp1 = sem("rates_ready")
        s_ang = sem("angles_ready")
        s_tanh = sem("tanh_ready")
        s_sin1 = sem("sines_ready")
        s_dec = sem("decay_rates_ready")
        s_rat = sem("ratio_ready")
        s_atan = sem("arctan_ready")
        s_hyp = sem("hypotenuse_ready")
        s_rows = sem("rows_written")
        s_rowl = sem("rows_broadcast")
        s_cexpo = sem("c_exponents_ready")
        s_ce = sem("c_decay_ready")
        s_ct = sem("c_turns_ready")
        s_cs = sem("c_sines_ready")
        s_c = sem("c_table_ready")
        s_sel0 = sem("selectors_zeroed")
        s_sel = sem("selectors_ready")
        s_kp = sem("kernel_rows_summed")
        s_kx = sem("kernel_rows_ready")
        s_kd = sem("kernel_rows_stored")
        s_a = sem("projection_ready")
        s_xb = sem("x_biased")
        s_x = sem("x_ready")
        s_yd = sem("product_transposed")
        s_xg = sem("group_input_ready")
        s_tm = sem("toeplitz_multiplied")
        s_yt = sem("product_copied")
        s_cc = sem("output_table_ready")
        s_cg = sem("c_turns_multiplied")
        s_zs = sem("gates_ready")
        s_b3 = sem("last_sines_decayed")
        s_z = sem("z_ready")
        s_bt = sem("state_turns_ready")
        s_bw = sem("state_turns_step")
        s_bs = sem("state_sines_ready")
        s_be = sem("state_decay_ready")
        s_b = sem("state_table_ready")
        s_t = [sem(f"toeplitz_loaded{k}") for k in range(T_SLOTS)]
        s_bc = sem("group_tables_ready")
        s_s = sem("states_summed")
        s_v = sem("states_ready")
        s_y = sem("group_done")
        s_yc = sem("mixer_output_copied")
        s_g = sem("gated_ready")
        s_g2 = sem("gated_by_pool_ready")
        s_tp = sem("gated_transposed")
        s_gt = sem("gated_t_copied")
        s_o = sem("mixer_projected")
        s_hr = [sem(f"residual_loaded{k}") for k in range(4)]
        s_r = sem("residual_added")
        s_st = sem("stats_ready")
        s_mv = sem("moments_ready")
        s_sd = sem("deviation_ready")
        s_rs = sem("scale_ready")
        s_rc = sem("reciprocal_ready")
        s_x1 = sem("x1_ready")
        s_xp = sem("x1_transposed")
        s_x1t = sem("x1_t_copied")
        s_lp = sem("logits_summed")
        s_lg = sem("logits_ready")
        s_top = sem("maxima_ready")
        s_ix = sem("indices_ready")
        s_empty = sem("spare_blocks_emptied")
        s_tail = sem("tail_rows_ready")
        s_tails = sem("tails_emptied")
        s_pl = sem("places_step")
        s_oh = sem("one_hot_ready")
        s_cp = sem("counts_ready")
        s_pos = sem("positions_ready")
        s_be2 = sem("block_experts_ready")
        s_sc = [sem(f"rows_dispatched{k}") for k in range(4)]
        s_rconst = sem("routing_constants_ready")
        s_tk = sem("token_numbers_passed")
        s_xb2 = sem("residual_biased")
        s_ew = sem("expert_weights_loaded")
        s_xs = [sem(f"slots_loaded{k}") for k in range(3)]
        s_ep = sem("slots_transposed")
        s_ext = sem("slots_t_copied")
        s_up = sem("hidden_summed")
        s_ws = sem("first_weights_staged")
        s_b1 = sem("first_biases_loaded")
        s_ht = sem("hidden_ready")
        s_dn = sem("expert_out_summed")
        s_f1 = sem("expert_bias_added")
        s_f3 = sem("expert_stats_ready")
        s_f4 = sem("expert_moments_ready")
        s_f5 = sem("expert_deviation_ready")
        s_f6 = sem("expert_scale_ready")
        s_f7 = sem("normalized_ready")
        s_out = [sem(f"out_stored{k}") for k in range(3)]

        LOG_DT, LOG_A, A_IM, C_RE, C_IM = range(5)
        (DT, EA, AR, AI, TURNS, TH, EM1, ER, CM1, WR, WI, T1, T2, PP, QQ, AXX, AYY, MX, RAT, PHI, AMP, DEN, T3,
         T4) = range(24)

        def block_of(r, k, behind):
            n = r * 3 + (k - behind)
            if isinstance(n, int) and not 0 <= n < BLOCKS:
                return None
            return n, (k - behind) % 3, r + (k - behind) // 3

        def quad_of(step, behind):
            n = step - behind
            if not 0 <= n < QUADS:
                return None
            return n, n % 2, n % 4, n // 4

        block = ctx.enter_context(nc.Block())

        @block.sync
        def _(sp):
            sp.dma_start(prm[:, :, :], states).then_inc(s_params, 16)
            sp.dma_start(Wx[:, :, :].rearrange("p t c -> p (t c)"),
                         conv_w.rearrange("t c -> (t c)").unsqueeze(0).to_broadcast([P, TAPS * CHAN]))\
              .then_inc(s_cw, 16)
            sp.dma_start(cbias[:, :], conv_b.to_broadcast([P, CHAN])).then_inc(s_cw, 16)
            sp.dma_start(dskip[:, :], d_skip).then_inc(s_late, 16)
            sp.dma_start(gwT[:, :], gate_w_t).then_inc(s_late, 16)
            sp.dma_start(gbias[:, 0, :], gate_b.to_broadcast([P, EXPERTS])).then_inc(s_late, 16)
            sp.dma_start(gbias[:, 1, :], expert_bias.to_broadcast([P, EXPERTS])).then_inc(s_late, 16)
            sp.wait_ge(s_dec, 2)
            sp.dma_start(rows_dram[0, :].rearrange("(n g) -> n g", g=GROUPS), sm[0:64, AR, :]).then_inc(s_rows, 16)
            sp.dma_start(rows_dram[1, :].rearrange("(n g) -> n g", g=GROUPS), sm[0:64, TURNS, :]).then_inc(s_rows, 16)
            sp.wait_ge(s_rows, 32)
            sp.dma_start(decay_row, rows_dram[0:1, :].to_broadcast([P, 2048])).then_inc(s_rowl, 16)
            sp.dma_start(turns_row, rows_dram[1:2, :].to_broadcast([P, 2048])).then_inc(s_rowl, 16)
            sp.wait_ge(s_kx, 3)
            sp.dma_start(kext.rearrange("(j p) c -> p j c", p=P), Kx[:, :, :]).then_inc(s_kd, 16)
            sp.wait_ge(s_kd, 16)

            def load_toeplitz(r, k):
                group = r * T_SLOTS + k
                if not isinstance(r, int):
                    sp.wait_ge(s_tm, group - (T_SLOTS - 1))
                sp.dma_start(Tring[:, k, :, :], toeplitz[:, bass.ds(group * GH, GH), :]).then_inc(s_t[k], 16)

            for k in range(T_SLOTS):
                load_toeplitz(0, k)
            with sp.Fori(1, GROUPS // T_SLOTS) as r:
                for k in range(T_SLOTS):
                    load_toeplitz(r, k)

            def load_residual(r, k):
                if not isinstance(r, int):
                    sp.wait_ge(s_r, r)
                row = (r * CHUNKS + k) * P
                sp.dma_start(HR[:, k, :], hidden_rows[bass.ds(row, P), :]).then_inc(s_hr[k], 16)

            sp.wait_ge(s_b, 2 * LAGS)
            for k in range(4):
                load_residual(0, k)
            sp.wait_ge(s_y, GROUPS)
            sp.dma_start(WoT, w_out_t.rearrange("(j p) d -> p j d", p=P)).then_inc(s_wo, 16)

            def load_weights(e):
                one = bass.ds(e, 1)
                sp.dma_start(W1[:, one, :].rearrange("p e f -> p (e f)"), w1[one, :, :].rearrange("e d f -> (e d) f"))\
                  .then_inc(s_ew, 16)
                sp.dma_start(W2[:, one, :].rearrange("p e (c d) -> p (e c) d", c=FCH),
                             w2[one, :, :].rearrange("e (c p) d -> p (e c) d", p=P)).then_inc(s_ew, 16)
                sp.dma_start(B2[:, one, :].rearrange("p e f -> p (e f)"), b2[one, :].to_broadcast([P, DM]))\
                  .then_inc(s_ew, 16)

            sp.wait_ge(s_rconst, 1)
            sp.dma_start(slots_dram[EXPERTS * REGION:, :].rearrange("(n p) c -> p n c", p=P),
                         empty_row.unsqueeze(1).to_broadcast([P, spare, ROW])).then_inc(s_empty, 16)
            sp.dma_start(B1, b1).then_inc(s_b1, 16)
            load_weights(0)
            with sp.Fori(1, QUADS) as r:
                for k in range(4):
                    load_residual(r, k)
                load_weights(r)
            sp.wait_ge(s_tail, 1)
            for e in range(0, EXPERTS, 2):
                row = sp.value_load(tail[0:1, e:e + 1], min_val=0, max_val=EXPERTS * REGION - P)
                sp.dma_start(slots_dram[bass.ds(row, P), :], empty_row).then_inc(s_tails, 16)

            def row_of(n):
                return sp.value_load(first_row[0:1, bass.ds(n, 1)], min_val=0, max_val=EXPERTS * REGION + (spare - 1) * P)

            def load_slots(row, k):
                sp.dma_start(XS[:, k, :], slots_dram[bass.ds(row, P), :]).then_inc(s_xs[k], 16)

            sp.wait_ge(s_be2, 1)
            rows = [row_of(k) for k in range(3)]
            sp.wait_ge(s_empty, 16)
            sp.wait_ge(s_tails, 16 * EXPERTS)
            for k in range(4):
                sp.wait_ge(s_sc[k], 4 * TILES)
            for k in range(3):
                load_slots(rows[k], k)
            with sp.Fori(1, BLOCKS // 3) as r:
                for k in range(3):
                    sp.wait_ge(s_ep, r * 3 + (k - 2))
                    sp.wait_ge(s_xb2, r * 3 + (k - 2))
                    load_slots(row_of(r * 3 + k), k)
            for k in range(3):
                sp.wait_ge(s_out[k], 16 * (BLOCKS // 3))

        @block.gpsimd
        def _(pool):
            nc.gpsimd.memset(XR[:, :, SEQ:], 0.0).then_inc(s_pad, 1)
            nc.gpsimd.iota(jrow[:, :], [[1, KLEN]], base=0, channel_multiplier=0, allow_small_or_imprecise_dtypes=True)
            nc.gpsimd.iota(tau[:, :], [[CHUNK, LAGS]], base=0, channel_multiplier=1, allow_small_or_imprecise_dtypes=True)
            nc.gpsimd.memset(mask16[:, :], 1.0).then_inc(s_pstep, 1)
            pool.wait_ge(s_pstep, 1)
            nc.gpsimd.affine_select(out=mask16[:, :], in_=mask16[:, :], compare_op=ALU.is_ge, fill=0.0, base=0,
                                    pattern=[[-GH, 2 * GH]], channel_multiplier=1).then_inc(s_pstep, 1)
            pool.wait_ge(s_pstep, 2)
            nc.gpsimd.affine_select(out=mask16[:, :], in_=mask16[:, :], compare_op=ALU.is_ge, fill=0.0, base=GH - 1,
                                    pattern=[[GH, 2 * GH]], channel_multiplier=-1).then_inc(s_pstep, 1)
            pool.wait_ge(s_pstep, 3)
            nc.gpsimd.tensor_tensor(mask8[:, :], mask16[:, 0:GH], mask16[:, GH:2 * GH], ALU.add).then_inc(s_const, 1)
            nc.gpsimd.memset(TR[:, 0:4096], 0.0).then_inc(s_sel0, 1)
            pool.wait_ge(s_dec, 2)
            nc.gpsimd.tensor_tensor(Ctab, sm[:, AR, :].unsqueeze(2).to_broadcast([P, GROUPS, KLEN]),
                                    jrow[:, :].unsqueeze(1).to_broadcast([P, GROUPS, KLEN]), ALU.mult)\
              .then_inc(s_cexpo, 1)
            nc.gpsimd.tensor_tensor(turnsC, sm[:, TURNS, :].unsqueeze(2).to_broadcast([P, GROUPS, KLEN]),
                                    jrow[:, :].unsqueeze(1).to_broadcast([P, GROUPS, KLEN]), ALU.mult).then_inc(s_cg, 1)
            nc.gpsimd.memset(Kx[:, :, :], 0.0).then_inc(s_const, 1)
            nc.gpsimd.memset(ident[:, :], 1.0)
            nc.gpsimd.memset(epscol[:, :], EPS)
            nc.gpsimd.memset(quarter[:, :], QUARTER).then_inc(s_pstep, 1)
            pool.wait_ge(s_pstep, 4)
            nc.gpsimd.affine_select(out=ident[:, :], in_=ident[:, :], compare_op=ALU.is_equal, fill=0.0, base=0,
                                    pattern=[[-1, P]], channel_multiplier=1).then_inc(s_const, 1)

            def state_product(i, parts):
                pool.wait_ge(s_bs, i * 2 + 2)
                for half in range(2):
                    pool.wait_ge(s_be, i * 2 + (half + 1))
                    for q in parts:
                        part = Btab[:, LAG_ORDER[i] - 1, q, half * 32:half * 32 + 32, :].rearrange("p n g -> p (n g)")
                        last = nc.gpsimd.tensor_tensor(part, part, decay[:, half, :], ALU.mult)
                    last.then_inc(s_b, 1)

            for i in range(LAGS - 1):
                state_product(i, (0, 1))
            state_product(LAGS - 1, (0,))

            def group_tables(r, k):
                g = r * 2 + k
                wait_apart(pool, s_s, g - 1)
                nc.gpsimd.tensor_copy(BC[:, k, 0:LAGS, :], BR[:, :].rearrange("p (m c g) -> p m c g", m=LAGS, g=GROUPS)
                                      [:, :, :, bass.ds(g, 1)].rearrange("p m c g -> p m (c g)")).then_inc(s_bc, 1)

            pool.wait_ge(s_b, 2 * LAGS)
            pool.wait_ge(s_b3, 2)
            pool.wait_ge(s_c, 1)
            pool.wait_ge(s_a, PAIRS)
            for k in range(2):
                group_tables(0, k)
            with pool.Fori(1, GROUPS // 2) as r:
                for k in range(2):
                    group_tables(r, k)

            def gate(s):
                at = quad_of(s, -1)
                if at:
                    n, slot, ring, turn = at
                    wait_past(pool, s_tp, n * 4)
                    for k in range(2, 4):
                        tile = bass.ds(n + k * BATCH, 1)
                        nc.gpsimd.tensor_tensor(G[:, k, :], X[:, :, tile].rearrange("p c t -> p (c t)"),
                                                Z[:, tile, :].rearrange("p t c -> p (t c)"), ALU.mult).then_inc(s_g2, 1)

            def dispatch(s):
                at = quad_of(s, 3)
                if at:
                    n, slot, ring, turn = at
                    wait_apart(pool, s_pos, n + 1)
                    wait_apart(pool, s_x1, n + 1)
                    for k in range(4):
                        pool.indirect_dma_start(slots_dram, bass.IndirectOffsetOnAxis(pos[:, ring, k:k + 1], 0),
                                                X1[:, ring, k, :], None).then_inc(s_sc[ring], 16)

            pool.wait_ge(s_yc, GROUPS)
            pool.wait_ge(s_zs, GROUPS // 2)
            nc.gpsimd.memset(empty_row, 0.0).then_inc(s_pstep, 1)
            pool.wait_ge(s_pstep, 5)
            nc.gpsimd.memset(empty_row[:, TOKEN_COL:TOKEN_COL + 1], NO_TOKEN).then_inc(s_rconst, 1)
            nc.gpsimd.iota(tokf, [[P, TILES]], base=0, channel_multiplier=1, allow_small_or_imprecise_dtypes=True)
            nc.gpsimd.memset(X1[:, :, :, TOKEN_COL:], 0.0).then_inc(s_rconst, 1)
            nc.gpsimd.memset(ones, 1.0)
            nc.gpsimd.iota(erow, [[1, EXPERTS]], base=0, channel_multiplier=0, allow_small_or_imprecise_dtypes=True)
            nc.gpsimd.iota(ebase, [[REGION, EXPERTS]], base=0, channel_multiplier=0, allow_small_or_imprecise_dtypes=True)
            nc.gpsimd.iota(free_row, [[REGION, EXPERTS]], base=0, channel_multiplier=0, allow_small_or_imprecise_dtypes=True)
            nc.gpsimd.iota(brow, [[1, BLOCKS + 1]], base=0, channel_multiplier=0, allow_small_or_imprecise_dtypes=True)
            nc.gpsimd.memset(before, 1.0).then_inc(s_rconst, 1)
            pool.wait_ge(s_rconst, 3)
            nc.gpsimd.affine_select(out=before, in_=before, compare_op=ALU.is_gt, fill=0.0, base=0, pattern=[[1, P]],
                                    channel_multiplier=-1).then_inc(s_rconst, 1)
            for s in range(-1, QUADS + 3):
                gate(s)
                dispatch(s)

            pool.wait_ge(s_ew, 48 * EXPERTS)
            pool.wait_ge(s_be2, 1)

            def residual_and_bias(r, k):
                at = block_of(r, k, 0)
                if at:
                    n, slot, turn = at
                    e = pool.value_load(bexp[0:1, bass.ds(n, 1)], min_val=0, max_val=EXPERTS - 1)
                    pool.wait_ge(s_xs[slot], (turn + 1) * 16)
                    wait_past(pool, s_f1, n - 2)
                    nc.gpsimd.tensor_tensor(O[:, slot, :], XS[:, slot, 0:DM],
                                            B2[:, bass.ds(e, 1), :].rearrange("p e d -> p (e d)"), ALU.add)
                    wait_apart(pool, s_tk, n - 2)
                    nc.gpsimd.tensor_copy(tok[:, slot:slot + 1], XS[:, slot, TOKEN_COL:TOKEN_COL + 1])\
                      .then_inc(s_xb2, 1)

            def pass_tokens(r, k):
                at = block_of(r, k, 2)
                if at:
                    n, slot, turn = at
                    if not isinstance(turn, int) or turn > 0:
                        pool.wait_ge(s_out[slot], turn * 16)
                    wait_apart(pool, s_xb2, n + 1)
                    nc.gpsimd.tensor_copy(tok[:, 3 + slot:4 + slot], tok[:, slot:slot + 1]).then_inc(s_tk, 1)

            def store(r, k):
                at = block_of(r, k, 3)
                if at:
                    n, slot, turn = at
                    wait_apart(pool, s_f7, n + 1)
                    wait_apart(pool, s_tk, n + 1)
                    pool.indirect_dma_start(out_rows, bass.IndirectOffsetOnAxis(tok[:, 3 + slot:4 + slot], 0), F[:, slot, :],
                                            None, bounds_check=TOKENS - 1, oob_is_err=False).then_inc(s_out[slot], 16)

            def step(r, k):
                pass_tokens(r, k)
                residual_and_bias(r, k)
                store(r, k)

            for r in range(2):
                for k in range(3):
                    step(r, k)
            with pool.Fori(2, BLOCKS // 3) as r:
                for k in range(3):
                    step(r, k)
            for k in range(3):
                step(BLOCKS // 3, k)

        @block.scalar
        def _(act):
            act.dma_start(Win[:, :], w_in_t).then_inc(s_win, 16)
            for k in range(A_BATCH):
                act.dma_start(XR[:, k, 0:SEQ], hidden_r[:, k, :]).then_inc(s_xt[k], 16)
                act.dma_start(XT[:, k, :], hidden_t[:, k, :]).then_inc(s_xt[k], 16)

            act.wait_ge(s_params, 16)
            nc.scalar.activation(sm[:, DT, :], prm[:, LOG_DT, :], ACT.Exp)
            nc.scalar.activation(sm[:, EA, :], prm[:, LOG_A, :], ACT.Exp).then_inc(s_exp1, 1)
            act.wait_ge(s_dec, 1)
            nc.scalar.activation(sm[:, TH, :], sm[:, AR, :], ACT.Tanh, scale=0.5).then_inc(s_tanh, 1)
            act.wait_ge(s_ang, 1)
            nc.scalar.activation(smt[:, :, :], smt[:, :, :], ACT.Sin, scale=TWO_PI).then_inc(s_sin1, 1)
            act.wait_ge(s_cexpo, 1)
            nc.scalar.activation(CR[:, :], CR[:, :], ACT.Exp).then_inc(s_ce, 1)
            act.wait_ge(s_rat, 1)
            nc.scalar.activation(sm[:, PHI, :], sm[:, RAT, :], ACT.Arctan).then_inc(s_atan, 1)
            nc.scalar.activation(sm[:, T4, :], sm[:, T3, :], ACT.Sqrt).then_inc(s_hyp, 1)

            def keep_z(i, k):
                n = i * 4 + k
                act.wait_ge(s_a, n + 1)
                nc.scalar.activation(z_pairs[:, k % 2, :, bass.ds(i * 2 + k // 2, 1), :].rearrange("p j b c -> p j (b c)"),
                                     bank[Z_BANKS[k]][:, :].rearrange("p (j c) -> p j c", j=2), ACT.Copy).then_inc(s_z, 1)

            def next_batch(i, k):
                act.wait_ge(s_a, i * 4 + (k * 2 + 2))
                for dst, src in ((XR, hidden_r), (XT, hidden_t)):
                    act.dma_start(dst[:, k, 0:SEQ], src[:, bass.ds((i + 1) * A_BATCH + k, 1), :]
                                  .rearrange("d b l -> d (b l)")).then_inc(s_xt[k], 16)

            def state_sines(i):
                for q, scale, bias, count in ((1, TWO_PI, 0.0, 1), (0, -TWO_PI, quarter[:, :], 2)):
                    rows = Btab[:, LAG_ORDER[i] - 1, q, :, :].rearrange("p n g -> p (n g)")
                    act.wait_ge(s_bt, i * 2 + 2)
                    nc.scalar.activation(rows, rows, ACT.Sin, scale=scale, bias=bias).then_inc(s_bs, 1)

            def state_decay(i, half):
                wait_past(act, s_b, i * 2 + (half - 1) if i else 0)
                nc.scalar.activation(decay[:, half, :], decay_row[:, half * 1024:half * 1024 + 1024], ACT.Exp,
                                     scale=tau[:, LAG_ORDER[i] - 1:LAG_ORDER[i]]).then_inc(s_be, 1)

            def keep_batch(i, half):
                for k in range(half * 2, half * 2 + 2):
                    keep_z(i, k)
                if i < 3:
                    next_batch(i, half)

            def state_table(i):
                state_sines(i)
                state_decay(i, 0)
                state_decay(i, 1)

            keep_batch(0, 0)
            keep_batch(0, 1)
            act.wait_ge(s_ct, 1)
            nc.scalar.activation(BR[:, 0:GROUPS * KLEN], BR[:, 0:GROUPS * KLEN], ACT.Sin, scale=TWO_PI).then_inc(s_cs, 1)
            keep_batch(1, 0)
            keep_batch(1, 1)
            act.wait_ge(s_rowl, 32)
            act.wait_ge(s_const, 3)
            state_table(0)
            keep_batch(2, 0)
            state_table(1)
            keep_batch(2, 1)
            state_table(2)

            def silu_x(r, rows):
                part = X[:, r * T_SLOTS * GH:(r + 1) * T_SLOTS * GH, :].rearrange("p c (q b) -> p (c q) b", b=BATCH)[:, :, rows]
                nc.scalar.activation(part, part, ACT.Silu).then_inc(s_x, 1)

            act.wait_ge(s_xb, PAIRS - 4)
            for r in range(GROUPS // T_SLOTS):
                silu_x(r, slice(0, BATCH - A_BATCH))
            keep_batch(3, 0)
            keep_batch(3, 1)
            act.wait_ge(s_xb, PAIRS)
            silu_x(0, slice(BATCH - A_BATCH, BATCH))

            def group_input(r, k):
                g = r * 2 + k
                wait_past(act, s_tm, g - 1)
                nc.scalar.activation(XG[:, k, :, :], X[:, bass.ds(g * GH, GH), :], ACT.Copy).then_inc(s_xg, 1)

            def group_product(r, k):
                g = r * 2 + k
                wait_past(act, s_y, g - 1)
                nc.scalar.activation(BC[:, k, LAGS, :], Ctab[:, bass.ds(g, 1), 1:KLEN].rearrange("p g j -> p (g j)"),
                                     ACT.Copy).then_inc(s_cc, 1)
                act.wait_ge(s_tm, g + 1)
                nc.scalar.activation(YT[:, k, :], bank[k][:, 0:2 * P], ACT.Copy).then_inc(s_yt, 1)

            act.wait_ge(s_x, GROUPS // T_SLOTS + 1)
            act.wait_ge(s_be, LAGS * 2)
            for k in range(2):
                group_input(0, k)
            for r in range(1, GROUPS // T_SLOTS):
                silu_x(r, slice(BATCH - A_BATCH, BATCH))
            act.wait_ge(s_x, 2 * (GROUPS // T_SLOTS))
            act.wait_ge(s_z, PAIRS)

            def gate_silu(r):
                part = Z[:, bass.ds(r * 2, 2), :].rearrange("p t c -> p (t c)")
                nc.scalar.activation(part, part, ACT.Silu).then_inc(s_zs, 1)

            def groups_and_gate(r):
                for k in range(2):
                    group_product(r, k)
                    group_input(r + 1, k)
                gate_silu(r)

            groups_and_gate(0)
            with act.Fori(1, GROUPS // 2 - 1) as r:
                groups_and_gate(r)
            for k in range(2):
                group_product(GROUPS // 2 - 1, k)
            gate_silu(GROUPS // 2 - 1)

            def copy_gated(s):
                at = quad_of(s, 0)
                if at:
                    n, slot, ring, turn = at
                    for j in range(2):
                        act.wait_ge(s_tp, n * 4 + (j * 2 + 2))
                        wait_past(act, s_o, n * 4 + (j * 2 - 2))
                        nc.scalar.activation(GT[:, j * 2:j * 2 + 2, :].rearrange("p k c -> p (k c)"), bank[j][:, :],
                                             ACT.Copy).then_inc(s_gt, 1)

            def deviation(s):
                at = quad_of(s, 1)
                if at:
                    n, slot, ring, turn = at
                    act.wait_ge(s_mv, n + 1)
                    nc.scalar.activation(sd[:, :], mv[:, :, 1], ACT.Sqrt, bias=epscol[:, :]).then_inc(s_sd, 1)

            def normalize(s):
                at = quad_of(s, 1)
                if at:
                    n, slot, ring, turn = at
                    act.wait_ge(s_rs, n + 1)
                    wait_past(act, s_xp, n - 3)
                    wait_past(act, s_sc[ring], turn * 64)
                    for k in range(4):
                        nc.scalar.activation(X1[:, ring, k, 0:DM], R[:, slot, k, :], ACT.Identity,
                                             scale=rs[:, slot, 0, k:k + 1], bias=rs[:, slot, 1, k:k + 1])
                    if isinstance(n, int) and n == 0:
                        act.wait_ge(s_rconst, 2)
                    nc.scalar.activation(X1[:, ring, :, TOKEN_COL], tokf[:, bass.ds(n * 4, 4)], ACT.Copy).then_inc(s_x1, 1)

            def copy_x1(s):
                at = quad_of(s, 2)
                if at:
                    n, slot, ring, turn = at
                    act.wait_ge(s_xp, n + 1)
                    nc.scalar.activation(X1T.rearrange("p k c -> p (k c)"), bank[3][:, :], ACT.Copy).then_inc(s_x1t, 1)

            act.wait_ge(s_yc, GROUPS)
            for s in range(-1, QUADS + 3):
                copy_gated(s)
                copy_x1(s)
                deviation(s)
                normalize(s)

            act.wait_ge(s_rconst, 1)
            act.wait_ge(s_tail, 1)
            for e in range(1, EXPERTS, 2):
                row = act.value_load(tail[0:1, e:e + 1], min_val=0, max_val=EXPERTS * REGION - P)
                act.dma_start(slots_dram[bass.ds(row, P), :], empty_row).then_inc(s_tails, 16)

            def copy_slots(r, k):
                at = block_of(r, k, 0)
                if at:
                    n, slot, turn = at
                    act.wait_ge(s_ep, n + 1)
                    wait_past(act, s_up, n - 2)
                    nc.scalar.activation(XsT[:, slot, :], bank[6][:, 0:P], ACT.Copy).then_inc(s_ext, 1)

            def expert_deviation(r, k):
                at = block_of(r, k, 3)
                if at:
                    n, slot, turn = at
                    act.wait_ge(s_f4, n + 1)
                    nc.scalar.activation(esd[:, slot:slot + 1], emv[:, slot, 1:2], ACT.Sqrt, bias=epscol[:, :])\
                      .then_inc(s_f5, 1)

            def bias_and_relu(r, k, e):
                at = block_of(r, k, 1)
                if at:
                    n, slot, turn = at
                    act.wait_ge(s_up, n + 1)
                    wait_past(act, s_dn, n - 2)
                    for c in range(FCH):
                        last = nc.scalar.activation(HT[:, slot, c * P:c * P + P], bank[slot][:, c * P:c * P + P], ACT.Relu,
                                                    bias=B1[:, bass.ds(e * FCH + c, 1)])
                    last.then_inc(s_ht, 1)

            def step(r, k):
                at = block_of(r, k, 1)
                e = at and act.value_load(bexp[0:1, bass.ds(at[0], 1)], min_val=0, max_val=EXPERTS - 1)
                copy_slots(r, k)
                expert_deviation(r, k)
                bias_and_relu(r, k, e)

            act.wait_ge(s_b1, 16)
            act.wait_ge(s_be2, 1)
            for r in range(2):
                for k in range(3):
                    step(r, k)
            with act.Fori(2, BLOCKS // 3) as r:
                for k in range(3):
                    step(r, k)
            for k in range(3):
                step(BLOCKS // 3, k)

        @block.vector
        def _(dve):
            steps = [0]

            def done(instruction):
                steps[0] += 1
                instruction.then_inc(s_vstep, 1)
                dve.wait_ge(s_vstep, steps[0])

            tt = nc.vector.tensor_tensor
            ts = nc.vector.tensor_scalar
            stt = nc.vector.scalar_tensor_tensor
            v = lambda i: sm[:, i, :]

            done(nc.vector.memset(phase[0:64, :], 0.25))
            done(nc.vector.memset(phase[64:128, :], 0.5))
            dve.wait_ge(s_win, 16)
            dve.wait_ge(s_cw, 32)
            tt(Wx[:, :, :], Win[:, 0:CHAN].unsqueeze(1).to_broadcast([P, TAPS, CHAN]), Wx[:, :, :], ALU.mult)\
              .then_inc(s_wx, 1)

            def bias(i, k):
                n = i * 4 + k
                dve.wait_ge(s_a, n + 1)
                b = bass.ds(i * 2 + k // 2, 1)
                tt(x_pairs[:, :, k % 2, :, b].rearrange("p c j b -> p j (c b)"),
                   bank[X_BANKS[k]][:, :].rearrange("p (j c) -> p j c", j=2),
                   cbias[:, :].unsqueeze(1).to_broadcast([P, 2, CHAN]), ALU.add).then_inc(s_xb, 1)

            def state_turns(i, step):
                lag = tau[:, LAG_ORDER[i] - 1:LAG_ORDER[i]]
                for half in range(2):
                    row = turns_row[:, half * 1024:half * 1024 + 1024]
                    part = Btab[:, LAG_ORDER[i] - 1, :, half * 32:half * 32 + 32, :].rearrange("p r n g -> p r (n g)")
                    cosine, sine = part[:, 0, :], part[:, 1, :]
                    if step:
                        dve.wait_ge(s_bw, i * 6 + ((step - 1) * 2 + half + 1))
                    if step == 0:
                        ts(cosine, row, lag, MAGIC, ALU.mult, ALU.add).then_inc(s_bw, 1)
                    elif step == 1:
                        ts(cosine, cosine, MAGIC, None, ALU.subtract).then_inc(s_bw, 1)
                    elif step == 2:
                        stt(sine, row, lag, cosine, ALU.mult, ALU.subtract).then_inc(s_bw, 1)
                    else:
                        stt(cosine, sine, -1.0, sine, ALU.mult, ALU.max).then_inc(s_bt, 1)

            dve.wait_ge(s_exp1, 1)
            dve.wait_ge(s_params, 16)
            done(stt(v(AR), v(DT), -1.0, v(EA), ALU.mult, ALU.mult))
            done(stt(v(AI), v(DT), TURN, prm[:, A_IM, :], ALU.mult, ALU.mult))
            nc.vector.tensor_copy(v(TURNS), v(AI)).then_inc(s_dec, 2)
            done(ts(smt[:, 1, :], v(AI), 0.5, None, ALU.mult))
            done(nc.vector.tensor_copy(smt[:, 0, :], v(AI)))
            done(ts(sm[:, T1:T1 + 2, :], smt[:, :, :], MAGIC, MAGIC, ALU.add, ALU.subtract))
            tt(smt[:, :, :], smt[:, :, :], sm[:, T1:T1 + 2, :], ALU.subtract).then_inc(s_ang, 1)
            dve.wait_ge(s_ang, 1)
            dve.wait_ge(s_tanh, 1)
            done(ts(v(T1), v(TH), -1.0, 1.0, ALU.mult, ALU.add))
            done(nc.vector.reciprocal(v(T2), v(T1)))
            done(stt(v(EM1), v(TH), 2.0, v(T2), ALU.mult, ALU.mult))
            done(ts(v(ER), v(EM1), 1.0, None, ALU.add))
            dve.wait_ge(s_sin1, 1)
            done(stt(v(CM1), smt[:, 1, :], -2.0, smt[:, 1, :], ALU.mult, ALU.mult))
            done(stt(v(T1), v(CM1), 1.0, v(EM1), ALU.add, ALU.mult))
            done(tt(v(WR), v(T1), v(CM1), ALU.add))
            done(tt(v(WI), v(ER), smt[:, 0, :], ALU.mult))
            done(tt(v(T1), prm[:, C_RE, :], v(WR), ALU.mult))
            done(tt(v(T2), prm[:, C_IM, :], v(WI), ALU.mult))
            done(tt(v(T1), v(T1), v(T2), ALU.subtract))
            done(tt(v(T2), prm[:, C_RE, :], v(WI), ALU.mult))
            done(tt(v(T3), prm[:, C_IM, :], v(WR), ALU.mult))
            done(tt(v(T2), v(T2), v(T3), ALU.add))
            done(tt(v(T3), v(T2), prm[:, A_IM, :], ALU.mult))
            done(tt(v(PP), v(T1), v(EA), ALU.mult))
            done(tt(v(PP), v(T3), v(PP), ALU.subtract))
            done(tt(v(T3), v(T2), v(EA), ALU.mult))
            done(tt(v(QQ), v(T1), prm[:, A_IM, :], ALU.mult))
            done(stt(v(QQ), v(T3), -1.0, v(QQ), ALU.mult, ALU.subtract))
            done(stt(v(AXX), v(PP), -1.0, v(PP), ALU.mult, ALU.max))
            done(stt(v(AYY), v(QQ), -1.0, v(QQ), ALU.mult, ALU.max))
            done(tt(v(MX), v(AXX), v(AYY), ALU.max))
            done(tt(v(T1), v(AXX), v(AYY), ALU.min))
            done(ts(v(T2), v(MX), 1e-35, None, ALU.max))
            done(nc.vector.reciprocal(v(T3), v(T2)))
            done(tt(v(RAT), v(T1), v(T3), ALU.mult))
            done(tt(v(T1), v(RAT), v(RAT), ALU.mult))
            ts(v(T3), v(T1), 1.0, None, ALU.add).then_inc(s_rat, 1)
            dve.wait_ge(s_rat, 1)
            bias(0, 0)
            done(tt(v(T1), v(EA), v(EA), ALU.mult))
            done(tt(v(T2), prm[:, A_IM, :], prm[:, A_IM, :], ALU.mult))
            done(tt(v(T1), v(T1), v(T2), ALU.add))
            done(nc.vector.reciprocal(v(DEN), v(T1)))
            done(stt(v(DEN), v(DEN), 2.0, v(MX), ALU.mult, ALU.mult))
            bias(0, 1)
            dve.wait_ge(s_atan, 1)
            done(ts(v(PHI), v(PHI), TURN, None, ALU.mult))

            def reflect(condition, about):
                done(ts(v(T2), v(PHI), -2.0, about, ALU.mult, ALU.add))
                done(tt(v(T2), v(T2), v(T1), ALU.mult))
                done(tt(v(PHI), v(PHI), v(T2), ALU.add))

            done(tt(v(T1), v(AYY), v(AXX), ALU.is_gt))
            reflect(T1, 0.25)
            done(ts(v(T1), v(PP), 0.0, None, ALU.is_lt))
            reflect(T1, 0.5)
            done(ts(v(T1), v(QQ), 0.0, None, ALU.is_lt))
            reflect(T1, 0.0)
            dve.wait_ge(s_const, 1)
            done(ts(v(PHI), v(PHI), phase[:, :], None, ALU.add))
            dve.wait_ge(s_hyp, 1)
            done(tt(v(AMP), v(T4), v(DEN), ALU.mult))
            dve.wait_ge(s_sel0, 1)
            for j in range(2):
                at = bass.AP(TR[:, :].tensor, j * 16 * P, [[T_SLOTS * GH * CHUNK, P], [P + GH, 16], [1, GH]])
                last = tt(at, v(AMP)[:, j * 16:j * 16 + 16].unsqueeze(2).to_broadcast([P, 16, GH]),
                          mask16[:, 0:GH].unsqueeze(1).to_broadcast([P, 16, GH]), ALU.mult)
            last.then_inc(s_sel, 1)

            bias(0, 2)
            dve.wait_ge(s_cg, 1)
            done(tt(turnsC, turnsC, v(PHI).unsqueeze(2).to_broadcast([P, GROUPS, KLEN]), ALU.add))
            done(ts(wholeC, turnsC, MAGIC, MAGIC, ALU.add, ALU.subtract))
            bias(0, 3)
            tt(turnsC, turnsC, wholeC, ALU.subtract).then_inc(s_ct, 1)
            bias(1, 0)
            dve.wait_ge(s_rowl, 32)
            dve.wait_ge(s_ct, 1)
            state_turns(0, 0)
            state_turns(0, 1)
            dve.wait_ge(s_ce, 1)
            dve.wait_ge(s_cs, 1)
            tt(Ctab, Ctab, turnsC, ALU.mult).then_inc(s_c, 1)
            bias(1, 1)
            state_turns(0, 2)
            bias(1, 2)
            state_turns(0, 3)
            bias(1, 3)
            dve.wait_ge(s_c, 1)
            for k in range(4):
                for step in ((0, 1), (2,), (3,), ())[k]:
                    state_turns(1, step)
                for step in ((), (), (0,), (1,))[k]:
                    state_turns(2, step)
                bias(2, k)
            state_turns(2, 2)
            state_turns(2, 3)

            dve.wait_ge(s_const, 2)
            dve.wait_ge(s_late, 64)
            dve.wait_ge(s_kp, 1)
            for j in range(2):
                nc.vector.tensor_copy(Kx[:, j, CHUNK - 1:KROW - 1], bank[4 + j][:, 0:CHUNK]).then_inc(s_kx, 1)
            dve.wait_ge(s_kx, 2)
            tt(Kx[:, :, CHUNK - 1], Kx[:, :, CHUNK - 1], dskip[:, :], ALU.add).then_inc(s_kx, 1)

            bias(3, 0)
            for half in range(2):
                dve.wait_ge(s_bs, LAGS * 2)
                dve.wait_ge(s_be, LAGS * 2 - 1 + half)
                part = Btab[:, LAG_ORDER[-1] - 1, 1, half * 32:half * 32 + 32, :].rearrange("p n g -> p (n g)")
                tt(part, part, decay[:, half, :], ALU.mult).then_inc(s_b3, 1)
            for k in range(1, 4):
                bias(3, k)

            def states(r, k):
                g = r * 2 + k
                dve.wait_ge(s_s, g + 1)
                wait_past(dve, s_y, g - 1)
                stt(V[:, k, :, :], bank[6 + k][:, 0:GH * SCOLS].rearrange("p (h c) -> p h c", h=GH),
                    sm[:, AMP, bass.ds(g, 1)], mask8[:, :].unsqueeze(2).to_broadcast([P, GH, SCOLS]), ALU.mult, ALU.mult)\
                    .then_inc(s_v, 1)

            def output(r, k):
                g = r * 2 + k
                group = X[:, bass.ds(g * GH, GH), :]
                product = bank[4 + k][:, 0:GH * TILES].rearrange("p (h t) -> p h t", h=GH)
                from_states = bank[4 + k][:, GH * TILES:GH * (TILES + SCOLS)].rearrange("p (h c) -> p h c", h=GH)
                dve.wait_ge(s_y, g + 1)
                nc.vector.tensor_copy(group, product).then_inc(s_yd, 1)
                dve.wait_ge(s_yd, g + 1)
                tt(group[:, :, BATCH:], group[:, :, BATCH:], from_states, ALU.add).then_inc(s_yc, 1)

            dve.wait_ge(s_a, PAIRS)
            states(0, 0)
            states(0, 1)
            output(0, 0)
            with dve.Fori(1, GROUPS // 2) as r:
                states(r, 0)
                output(r - 1, 1)
                states(r, 1)
                output(r, 0)
            output(GROUPS // 2 - 1, 1)

            def gate(s):
                at = quad_of(s, -1)
                if at:
                    n, slot, ring, turn = at
                    wait_past(dve, s_tp, n * 4)
                    for k in range(2):
                        tile = bass.ds(n + k * BATCH, 1)
                        tt(G[:, k, :], X[:, :, tile].rearrange("p c t -> p (c t)"), Z[:, tile, :].rearrange("p t c -> p (t c)"),
                           ALU.mult).then_inc(s_g, 1)

            def norm(s):
                at = quad_of(s, 1)
                if at:
                    n, slot, ring, turn = at
                    dve.wait_ge(s_o, n * 4 + 4)
                    for k in range(4):
                        dve.wait_ge(s_hr[k], (n + 1) * 16)
                    wait_past(dve, s_x1, n - 1)
                    tt(R[:, slot, :, :].rearrange("p k c -> p (k c)"), bank[2][:, :], HR.rearrange("p k c -> p (k c)"),
                       ALU.add).then_inc(s_r, 1)
                    dve.wait_ge(s_r, n + 1)
                    for k in range(4):
                        last = nc.vector.bn_stats(st[:, k, :], R[:, slot, k, :])
                    last.then_inc(s_st, 1)
                    wait_apart(dve, s_st, n + 1)
                    for k in range(4):
                        last = nc.vector.bn_aggr(mv[:, k, :], st[:, k, :])
                    last.then_inc(s_mv, 1)

            def scale(s):
                at = quad_of(s, 1)
                if at:
                    n, slot, ring, turn = at
                    dve.wait_ge(s_sd, n + 1)
                    nc.vector.reciprocal(rs[:, slot, 0, :], sd[:, :]).then_inc(s_rc, 1)
                    dve.wait_ge(s_rc, n + 1)
                    stt(rs[:, slot, 1, :], mv[:, :, 0], -1.0, rs[:, slot, 0, :], ALU.mult, ALU.mult).then_inc(s_rs, 1)

            def choose(s):
                at = quad_of(s, 2)
                if at:
                    n, slot, ring, turn = at
                    dve.wait_ge(s_lp, n + 1)
                    tt(LG[:, :, :], bank[4][:, 0:32].rearrange("p (k e) -> p k e", k=4),
                       gbias[:, 0, :].unsqueeze(1).to_broadcast([P, 4, EXPERTS]), ALU.add).then_inc(s_lg, 1)
                    dve.wait_ge(s_lg, n * 2 + 1)
                    tt(LG[:, :, :], LG[:, :, :], gbias[:, 1, :].unsqueeze(1).to_broadcast([P, 4, EXPERTS]), ALU.add)\
                      .then_inc(s_lg, 1)
                    wait_apart(dve, s_lg, n * 2 + 2)
                    for k in range(4):
                        last = nc.vector.max(top[:, k, :], LG[:, k, :])
                    last.then_inc(s_top, 1)
                    wait_apart(dve, s_top, n + 1)
                    for k in range(4):
                        last = nc.vector.max_index(IDX[:, k, :], top[:, k, :], LG[:, k, :])
                    last.then_inc(s_ix, 1)
                    dve.wait_ge(s_ix, n + 1)
                    tt(OH, IDX[:, :, 0].unsqueeze(2).to_broadcast([P, 4, EXPERTS]),
                       erow.unsqueeze(1).to_broadcast([P, 4, EXPERTS]), ALU.is_equal).then_inc(s_oh, 1)

            def places(s):
                at = quad_of(s, 3)
                if at:
                    n, slot, ring, turn = at
                    dve.wait_ge(s_cp, n + 1)
                    counted = bank[5][:, 0:32].rearrange("p (k e) -> p k e", k=4)
                    tt(place, counted, free_row.unsqueeze(1).to_broadcast([P, 4, EXPERTS]), ALU.add).then_inc(s_pl, 1)
                    nc.vector.tensor_reduce(total, bank[6][:, 0:32].rearrange("p (k e) -> p e k", k=4), AX.X, ALU.add)\
                      .then_inc(s_pl, 1)
                    dve.wait_ge(s_pl, n * 5 + 2)
                    tt(place, place, OH, ALU.mult).then_inc(s_pl, 1)
                    tt(free_row, free_row, total, ALU.add).then_inc(s_pl, 1)
                    dve.wait_ge(s_pl, n * 5 + 4)
                    nc.vector.tensor_reduce(posf, place, AX.X, ALU.add).then_inc(s_pl, 1)
                    dve.wait_ge(s_pl, n * 5 + 5)
                    wait_past(dve, s_sc[ring], turn * 64)
                    nc.vector.tensor_copy(pos[:, ring, :], posf).then_inc(s_pos, 1)

            dve.wait_ge(s_yc, GROUPS)
            dve.wait_ge(s_zs, GROUPS // 2)
            for s in range(-1, QUADS + 3):
                norm(s)
                gate(s)
                places(s)
                scale(s)
                if s == 2:
                    dve.wait_ge(s_rconst, 4)
                choose(s)

            dve.wait_ge(s_pl, QUADS * 5)
            c = lambda i: cnt[:, i, :]
            nc.vector.tensor_copy(tail, free_row).then_inc(s_tail, 1)
            done(tt(c(0), free_row, ebase, ALU.subtract))
            done(ts(c(1), c(0), 1.0 / P, (P - 1.0) / P - 0.5 + 0.5 / P, ALU.mult, ALU.add))
            done(ts(c(1), c(1), MAGIC, MAGIC, ALU.add, ALU.subtract))
            done(nc.vector.tensor_tensor_scan(c(2), ones[:, 0:1].to_broadcast([P, EXPERTS]), c(1), 0.0, ALU.mult, ALU.add))
            shape = [P, BLOCKS + 1, EXPERTS]
            done(tt(bcmp[:, :, :], c(2).unsqueeze(1).to_broadcast(shape), brow[:, :].unsqueeze(2).to_broadcast(shape),
                    ALU.is_le))
            done(nc.vector.tensor_reduce(bexpf[:, :], bcmp[:, :, :], AX.X, ALU.add))
            done(tt(bcmp[:, :, :], bcmp[:, :, :], c(1).unsqueeze(1).to_broadcast(shape), ALU.mult))
            done(nc.vector.tensor_reduce(bstart[:, :], bcmp[:, :, :], AX.X, ALU.add))
            done(tt(bstart, brow, bstart, ALU.subtract))
            done(ts(bstart, bstart, float(P), None, ALU.mult))
            done(stt(bstart, bexpf, float(REGION), bstart, ALU.mult, ALU.add))
            done(nc.vector.tensor_copy(first_row, bstart))
            done(ts(bexpf[:, :], bexpf[:, :], EXPERTS - 1.0, None, ALU.min))
            nc.vector.tensor_copy(bexp[:, :], bexpf[:, :]).then_inc(s_be2, 1)

            dve.wait_ge(s_ew, 48 * EXPERTS)
            dve.wait_ge(s_be2, 1)

            def stage_weights(r, k, e):
                at = block_of(r, k, 0)
                if at:
                    n, slot, turn = at
                    wait_past(dve, s_up, n - 2)
                    nc.vector.tensor_copy(WS[:, slot, :], W1[:, bass.ds(e, 1), :].rearrange("p e f -> p (e f)"))\
                      .then_inc(s_ws, 1)

            def normalize(r, k):
                at = block_of(r, k, 3)
                if at:
                    n, slot, turn = at
                    dve.wait_ge(s_f5, n + 1)
                    nc.vector.reciprocal(ers[:, slot:slot + 1], esd[:, slot:slot + 1]).then_inc(s_f6, 1)
                    dve.wait_ge(s_f6, n + 1)
                    ts(F[:, slot, :], F[:, slot, :], emv[:, slot, 0:1], ers[:, slot:slot + 1], ALU.subtract, ALU.mult)\
                      .then_inc(s_f7, 1)

            def residual(r, k):
                at = block_of(r, k, 2)
                if at:
                    n, slot, turn = at
                    dve.wait_ge(s_dn, n + 1)
                    dve.wait_ge(s_xb2, n + 1)
                    if not isinstance(turn, int) or turn > 0:
                        dve.wait_ge(s_out[slot], turn * 16)
                    tt(F[:, slot, :], bank[7][:, 0:P], O[:, slot, :], ALU.add).then_inc(s_f1, 1)
                    dve.wait_ge(s_f1, n + 1)
                    nc.vector.bn_stats(est[:, slot, :], F[:, slot, :]).then_inc(s_f3, 1)
                    wait_apart(dve, s_f3, n + 1)
                    nc.vector.bn_aggr(emv[:, slot, :], est[:, slot, :]).then_inc(s_f4, 1)

            def step(r, k):
                at = block_of(r, k, 0)
                e = at and dve.value_load(bexp[0:1, bass.ds(at[0], 1)], min_val=0, max_val=EXPERTS - 1)
                stage_weights(r, k, e)
                residual(r, k)
                normalize(r, k)

            for r in range(2):
                for k in range(3):
                    step(r, k)
            with dve.Fori(2, BLOCKS // 3) as r:
                for k in range(3):
                    step(r, k)
            for k in range(3):
                step(BLOCKS // 3, k)

        @block.tensor
        def _(pe):
            mm = nc.tensor.matmul

            def project(i, k):
                n = i * 4 + k
                slot = k // 2
                if k % 2 == 0:
                    pe.wait_ge(s_xt[slot], (i + 1) * 32)
                wait_past(pe, s_xb, n - 3)
                wait_past(pe, s_z, n - 3)
                if k >= 2 and i == 3:
                    pe.wait_ge(s_kx, 2)
                for j in range(2):
                    chunk = k % 2 * 2 + j
                    for tap in range(TAPS):
                        at = (CHUNKS - 1 - chunk) * CHUNK + TAPS - 1 - tap
                        mm(bank[X_BANKS[k]][:, j * CHAN:(j + 1) * CHAN], XR[:, slot, at:at + CHUNK], Wx[:, tap, :],
                           start=(tap == 0), stop=(tap == TAPS - 1))
                    at = chunk * CHUNK
                    last = mm(bank[Z_BANKS[k]][:, j * CHAN:(j + 1) * CHAN], XT[:, slot, at:at + CHUNK], Win[:, CHAN:],
                              start=True, stop=True)
                last.then_inc(s_a, 1)

            pe.wait_ge(s_wx, 1)
            pe.wait_ge(s_pad, 1)
            for i in range(3):
                for k in range(4):
                    project(i, k)
            pe.wait_ge(s_xb, 12)
            pe.wait_ge(s_sel, 1)
            pe.wait_ge(s_c, 1)
            for g in range(GROUPS):
                last = mm(bank[4 + g // 16][:, 0:CHUNK], Sel[:, g, :], Ctab[:, g, 0:CHUNK], start=(g % 16 == 0),
                          stop=(g % 16 == 15))
            last.then_inc(s_kp, 1)
            for k in range(4):
                project(3, k)

            def mix(r, k):
                g = r * T_SLOTS + k
                s, yt = bank[6 + k % 2], bank[k % 2]
                xg = XG[:, k % 2, :, :]
                out_s = s[:, 0:GH * SCOLS].rearrange("p (h c) -> p h c", h=GH)
                pe.wait_ge(s_xg, g + 1)
                pe.wait_ge(s_bc, g + 1)
                wait_past(pe, s_v, g - 1)
                for lag in range(LAGS):
                    cols = SCOLS - lag * BATCH
                    last = mm(out_s[:, :, lag * BATCH:], BC[:, k % 2, lag, :], xg[:, :, 0:cols], start=(lag == 0),
                              stop=(lag == LAGS - 1))
                last.then_inc(s_s, 1)
                pe.wait_ge(s_t[k], (r + 1) * 16)
                wait_past(pe, s_yt, g - 1)
                for h in range(GH):
                    at, part = h // 4 * P, h % 4 * TILES
                    last = mm(yt[part:part + TILES, at:at + P], xg[:, h, :], Tring[:, k, h, :], start=True, stop=True)
                last.then_inc(s_tm, 1)

            def finish(r, k):
                g, slot = r * T_SLOTS + k, k % 2
                y = bank[4 + slot]
                pe.wait_ge(s_yt, g + 1)
                wait_past(pe, s_yc, g - 1)
                for j in range(2):
                    nc.tensor.transpose(y[:, j * P:(j + 1) * P], YT[:, slot, j * P:(j + 1) * P], ident[:, :])
                pe.wait_ge(s_v, g + 1)
                pe.wait_ge(s_cc, g + 1)
                mm(y[:, GH * TILES:GH * (TILES + SCOLS)], BC[:, slot, LAGS, :],
                   V[:, slot, :, :].rearrange("p h c -> p (h c)"), start=True, stop=True).then_inc(s_y, 1)

            pe.wait_ge(s_z, PAIRS)
            pe.wait_ge(s_kx, 2)
            pe.wait_ge(s_const, 3)
            mix(0, 0)
            for k in range(1, T_SLOTS):
                mix(0, k)
                finish(0, k - 1)
            with pe.Fori(1, GROUPS // T_SLOTS) as r:
                for k in range(T_SLOTS):
                    mix(r, k)
                    finish(r, k - 1)
            finish(GROUPS // T_SLOTS - 1, T_SLOTS - 1)

            pe.wait_ge(s_late, 64)

            def transpose_gated(s):
                at = quad_of(s, 0)
                if at:
                    n, slot, ring, turn = at
                    for k in range(4):
                        pe.wait_ge(s_g if k < 2 else s_g2, n * 2 + (k % 2 + 1))
                        wait_past(pe, s_gt, n * 2 + (k // 2 - 1))
                        for j in range(2):
                            at = (k % 2) * 256 + j * P
                            last = nc.tensor.transpose(bank[k // 2][:, at:at + P], G[:, k, j * P:j * P + P], ident[:, :])
                        last.then_inc(s_tp, 1)

            def output_projection(s):
                at = quad_of(s, 1)
                if at:
                    n, slot, ring, turn = at
                    wait_past(pe, s_r, n)
                    if isinstance(n, int) and n == 0:
                        pe.wait_ge(s_wo, 16)
                    for k in range(4):
                        pe.wait_ge(s_gt, n * 2 + (k // 2 + 1))
                        for j in range(2):
                            last = mm(bank[2][:, k * DM:k * DM + DM], GT[:, k, j * P:j * P + P], WoT[:, j, :],
                                      start=(j == 0), stop=(j == 1))
                        last.then_inc(s_o, 1)

            def transpose_x1(s):
                at = quad_of(s, 2)
                if at:
                    n, slot, ring, turn = at
                    pe.wait_ge(s_x1, n + 1)
                    wait_past(pe, s_x1t, n)
                    for k in range(4):
                        last = nc.tensor.transpose(bank[3][:, k * P:k * P + P], X1[:, ring, k, 0:DM], ident[:, :])
                    last.then_inc(s_xp, 1)

            def logits(s):
                at = quad_of(s, 2)
                if at:
                    n, slot, ring, turn = at
                    pe.wait_ge(s_x1t, n + 1)
                    wait_past(pe, s_lg, n * 2)
                    for k in range(4):
                        last = mm(bank[4][:, k * EXPERTS:(k + 1) * EXPERTS], X1T[:, k, :], gwT[:, :], start=True, stop=True)
                    last.then_inc(s_lp, 1)

            def count(s):
                at = quad_of(s, 3)
                if at:
                    n, slot, ring, turn = at
                    pe.wait_ge(s_oh, n + 1)
                    if isinstance(n, int) and n == 0:
                        pe.wait_ge(s_rconst, 4)
                    flat = lambda a: a.rearrange("p k e -> p (k e)")
                    mm(bank[5][:, 0:32], before[:, :], flat(OH), start=True, stop=False)
                    for m in range(1, 4):
                        mm(bank[5][:, m * EXPERTS:32], ones[:, :], flat(OH[:, 0:4 - m, :]), start=False, stop=(m == 3))
                    mm(bank[6][:, 0:32], ones[:, :], flat(OH), start=True, stop=True).then_inc(s_cp, 1)

            for s in range(-1, QUADS + 3):
                output_projection(s)
                count(s)
                transpose_gated(s)
                transpose_x1(s)
                logits(s)

            pe.wait_ge(s_ew, 48 * EXPERTS)
            pe.wait_ge(s_be2, 1)

            def transpose_slots(r, k):
                at = block_of(r, k, 0)
                if at:
                    n, slot, turn = at
                    pe.wait_ge(s_xs[slot], (turn + 1) * 16)
                    wait_past(pe, s_ext, n)
                    nc.tensor.transpose(bank[6][:, 0:P], XS[:, slot, 0:DM], ident[:, :]).then_inc(s_ep, 1)

            def up(r, k):
                at = block_of(r, k, 1)
                if at:
                    n, slot, turn = at
                    pe.wait_ge(s_ws, n + 1)
                    pe.wait_ge(s_ext, n + 1)
                    wait_past(pe, s_ht, n - 2)
                    for c in range(FCH):
                        last = mm(bank[slot][:, c * P:c * P + P], WS[:, slot, c * P:c * P + P], XsT[:, slot, :], start=True,
                                  stop=True)
                    last.then_inc(s_up, 1)

            def down(r, k, e):
                at = block_of(r, k, 2)
                if at:
                    n, slot, turn = at
                    pe.wait_ge(s_ht, n + 1)
                    wait_past(pe, s_f1, n)
                    for c in range(FCH):
                        last = mm(bank[7][:, 0:P], HT[:, slot, c * P:c * P + P],
                                  W2[:, bass.ds(e, 1), c * DM:(c + 1) * DM].rearrange("p e d -> p (e d)"),
                                  start=(c == 0), stop=(c == FCH - 1))
                    last.then_inc(s_dn, 1)

            def step(r, k):
                at = block_of(r, k, 2)
                e = at and pe.value_load(bexp[0:1, bass.ds(at[0], 1)], min_val=0, max_val=EXPERTS - 1)
                transpose_slots(r, k)
                up(r, k)
                down(r, k, e)

            for r in range(2):
                for k in range(3):
                    step(r, k)
            with pe.Fori(2, BLOCKS // 3) as r:
                for k in range(3):
                    step(r, k)
            for k in range(3):
                step(BLOCKS // 3, k)


_ORDER = ("hidden", "hidden_t", "hidden_r", "w_in_t", "conv_w", "conv_b", "states", "d_skip",
          "w_out_t", "gate_w_t", "gate_b", "expert_bias", "w1", "b1", "w2", "b2")


def kernel(**inputs):
    import numpy as _np
    import concourse.bacc as _bacc
    from concourse import mybir as _mybir
    from concourse.bass_utils import run_bass_kernel_spmd as _run

    a = {name: _np.asarray(value) for name, value in inputs.items()}

    def by_group(x):
        return x.reshape((GH, GROUPS) + x.shape[1:]).swapaxes(0, 1).reshape(x.shape)

    def by_state(x):
        x = x.reshape(GH, GROUPS, STATES).transpose(0, 2, 1).reshape(GH * STATES, GROUPS)
        return _np.concatenate([x, x])

    hidden = a["L0_attn_hidden_states"]
    w_in = a["L0_attn_W_in"]
    laid = {
        "hidden": hidden,
        "hidden_t": hidden.transpose(2, 0, 1),
        "hidden_r": hidden[:, ::-1].transpose(2, 0, 1),
        "w_in_t": _np.concatenate([by_group(w_in[:CHAN]), by_group(w_in[CHAN:])]).T,
        "conv_w": by_group(a["L0_attn_conv_w"]).T,
        "conv_b": by_group(a["L0_attn_conv_b"])[None],
        "states": _np.stack([by_state(x) for x in (
            _np.broadcast_to(a["L0_attn_log_dt"][:, None], (CHAN, STATES)), a["L0_attn_log_A_real"],
            a["L0_attn_A_imag"], a["L0_attn_C_re"], a["L0_attn_C_im"])], axis=1),
        "d_skip": by_group(a["L0_attn_D"]).reshape(2, P).T,
        "w_out_t": by_group(a["L0_attn_W_out"].T),
        "gate_w_t": a["L0_ffn_gate_w"].T,
        "gate_b": a["L0_ffn_gate_b"][None],
        "expert_bias": a["L0_ffn_expert_bias"][None],
        "w1": a["L0_ffn_w1"],
        "b1": a["L0_ffn_b1"].reshape(EXPERTS, FCH, P).transpose(2, 0, 1).reshape(P, EXPERTS * FCH),
        "w2": a["L0_ffn_w2"],
        "b2": a["L0_ffn_b2"],
    }
    nc = _bacc.Bacc("TRN2", target_bir_lowering=False, num_devices=1)
    arrays, args = {}, []
    for name in _ORDER:
        x = _np.ascontiguousarray(laid[name])
        arrays[name] = x
        args.append(nc.dram_tensor(name, x.shape, _mybir.dt.from_np(x.dtype), kind="ExternalInput").ap())
    args.append(nc.dram_tensor("out", (BATCH, SEQ, DM), F32, kind="ExternalOutput").ap())
    build(nc, *args)
    result = _run(nc, [arrays], core_ids=[0])
    return result.results[0]["out"]
```
